# Optimizing a Trainium2 kernel written in Bass

```python
import numpy as np
import jax
import jax.numpy as jnp

def _softmax(x, axis=-1):
    return jax.nn.softmax(x, axis=axis)

def _gelu(x):
    return jax.nn.gelu(x, approximate=True)

def _silu(x):
    return jax.nn.silu(x)

def _sigmoid(x):
    return jax.nn.sigmoid(x)

def _layernorm(x, axis=-1, eps=1e-05):
    m = jnp.mean(x, axis=axis, keepdims=True)
    v = jnp.var(x, axis=axis, keepdims=True)
    return (x - m) / jnp.sqrt(v + eps)

def _scatter_add(tgt, idx, src, axis=0):
    return tgt.at[idx].add(src)

def _segment_sum(src, seg, n):
    return jax.ops.segment_sum(src, seg, n)
kernel_name = 'mk_seq_postln_d2_jaxref_r4_dfe70d'

def setup_inputs(seed: int=0):
    np.random.seed(seed)
    _w = jnp.asarray

    def _L0_attn_setup():
        import jax, jax.numpy as jnp
        import numpy as np
        B, L, D = (2, 512, 256)
        H, HD = (16, 64)
        LD = 64
        key = jax.random.key(seed)
        ks = jax.random.split(key, 6)
        s = lambda fan_in: 1.0 / np.sqrt(fan_in)
        x_bld = jax.random.normal(ks[0], (B, L, D), dtype=jnp.float32)
        Wq = jax.random.normal(ks[1], (D, H, HD), dtype=jnp.float32) * s(D)
        Wkv_down = jax.random.normal(ks[2], (D, LD), dtype=jnp.float32) * s(D)
        Wk_up = jax.random.normal(ks[3], (LD, H, HD), dtype=jnp.float32) * s(LD)
        Wv_up = jax.random.normal(ks[4], (LD, H, HD), dtype=jnp.float32) * s(LD)
        Wout = jax.random.normal(ks[5], (H, HD, D), dtype=jnp.float32) * s(H * HD)
        return {'x_bld': x_bld, 'Wq': Wq, 'Wkv_down': Wkv_down, 'Wk_up': Wk_up, 'Wv_up': Wv_up, 'Wout': Wout}
    _L0_attn_in = _L0_attn_setup()

    def _L0_ffn_setup():
        import jax, jax.numpy as jnp
        import numpy as np
        B, S, D = (2, 512, 256)
        I = 128
        E = 16
        TOP_K = 2

        def _mlp(x, wg, wu, wd):
            return jnp.einsum('bsi,id->bsd', jax.nn.silu(x @ wg) * (x @ wu), wd)
        key = jax.random.key(seed)
        ks = jax.random.split(key, 10)
        sc_d = 1.0 / np.sqrt(D)
        sc_i = 1.0 / np.sqrt(I)
        return {'x': jax.random.normal(ks[0], (B, S, D), dtype=jnp.float32), 'gate_w': jax.random.normal(ks[1], (D, E), dtype=jnp.float32) * sc_d, 'gate_b': jnp.zeros((E,), dtype=jnp.float32), 'shared_wg': jax.random.normal(ks[2], (D, I), dtype=jnp.float32) * sc_d, 'shared_wu': jax.random.normal(ks[3], (D, I), dtype=jnp.float32) * sc_d, 'shared_wd': jax.random.normal(ks[4], (I, D), dtype=jnp.float32) * sc_i, 'experts_wg': jax.random.normal(ks[5], (E, D, I), dtype=jnp.float32) * sc_d, 'experts_wu': jax.random.normal(ks[6], (E, D, I), dtype=jnp.float32) * sc_d, 'experts_wd': jax.random.normal(ks[7], (E, I, D), dtype=jnp.float32) * sc_i}
    _L0_ffn_in = _L0_ffn_setup()

    def _L1_attn_setup():
        import jax, jax.numpy as jnp
        import numpy as np
        B, T, D = (2, 512, 256)
        H = 16
        HD = D // H
        DL = 128
        NR = 64
        EPS = 1.1920929e-07

        def _rms_norm(x, w):
            ms = jnp.mean(jnp.square(x), axis=-1, keepdims=True)
            return x * jax.lax.rsqrt(ms + EPS) * w
        key = jax.random.key(seed)
        ks = jax.random.split(key, 10)
        s = 0.02
        return {'x': jax.random.normal(ks[0], (B, T, D), dtype=jnp.float32), 'W_DQ': jax.random.normal(ks[1], (DL, HD), dtype=jnp.float32) * s, 'W_UQ': jax.random.normal(ks[2], (HD, DL), dtype=jnp.float32) * s, 'W_DKV': jax.random.normal(ks[3], (2 * DL, HD), dtype=jnp.float32) * s, 'W_UKV': jax.random.normal(ks[4], (2 * HD, 2 * DL), dtype=jnp.float32) * s, 'W_QR': jax.random.normal(ks[5], (NR, HD), dtype=jnp.float32) * s, 'W_KR': jax.random.normal(ks[6], (NR, HD), dtype=jnp.float32) * s, 'W_O': jax.random.normal(ks[7], (HD, HD), dtype=jnp.float32) * s, 'q_norm_w': jnp.ones((HD,), dtype=jnp.float32), 'k_norm_w': jnp.ones((HD,), dtype=jnp.float32)}
    _L1_attn_in = _L1_attn_setup()

    def _L1_ffn_setup():
        import jax, jax.numpy as jnp
        import numpy as np
        import math
        BETA = 0.9
        THRESHOLD = 1.0
        NUM_STEPS = 5
        ALPHA = 2.0

        @jax.custom_vjp
        def spike_fn(u):
            return (u > 0).astype(u.dtype)

        def _spike_fwd(u):
            return (spike_fn(u), u)

        def _spike_bwd(u, g):
            s = jnp.pi / 2.0 * ALPHA * u
            return (g * (ALPHA / 2.0) / (1.0 + s * s),)
        spike_fn.defvjp(_spike_fwd, _spike_bwd)
        key = jax.random.key(seed)
        k1, k2, k3 = jax.random.split(key, 3)
        n_embd = 256
        x = jax.random.normal(k1, (4, 512, n_embd), dtype=jnp.float32)
        W_fc = jax.random.normal(k2, (4 * n_embd, n_embd), dtype=jnp.float32) / math.sqrt(n_embd)
        W_proj = jax.random.normal(k3, (n_embd, 4 * n_embd), dtype=jnp.float32) / math.sqrt(4 * n_embd)
        return {'x': x, 'W_fc': W_fc, 'W_proj': W_proj}
    _L1_ffn_in = _L1_ffn_setup()
    _d = {'L0_attn_x_bld': _L0_attn_in['x_bld'], 'L0_attn_Wq': _L0_attn_in['Wq'], 'L0_attn_Wkv_down': _L0_attn_in['Wkv_down'], 'L0_attn_Wk_up': _L0_attn_in['Wk_up'], 'L0_attn_Wv_up': _L0_attn_in['Wv_up'], 'L0_attn_Wout': _L0_attn_in['Wout'], 'L0_ffn_gate_w': _L0_ffn_in['gate_w'], 'L0_ffn_gate_b': _L0_ffn_in['gate_b'], 'L0_ffn_shared_wg': _L0_ffn_in['shared_wg'], 'L0_ffn_shared_wu': _L0_ffn_in['shared_wu'], 'L0_ffn_shared_wd': _L0_ffn_in['shared_wd'], 'L0_ffn_experts_wg': _L0_ffn_in['experts_wg'], 'L0_ffn_experts_wu': _L0_ffn_in['experts_wu'], 'L0_ffn_experts_wd': _L0_ffn_in['experts_wd'], 'L1_attn_W_DQ': _L1_attn_in['W_DQ'], 'L1_attn_W_UQ': _L1_attn_in['W_UQ'], 'L1_attn_W_DKV': _L1_attn_in['W_DKV'], 'L1_attn_W_UKV': _L1_attn_in['W_UKV'], 'L1_attn_W_QR': _L1_attn_in['W_QR'], 'L1_attn_W_KR': _L1_attn_in['W_KR'], 'L1_attn_W_O': _L1_attn_in['W_O'], 'L1_attn_q_norm_w': _L1_attn_in['q_norm_w'], 'L1_attn_k_norm_w': _L1_attn_in['k_norm_w'], 'L1_ffn_W_fc': _L1_ffn_in['W_fc'], 'L1_ffn_W_proj': _L1_ffn_in['W_proj']}
    _x0 = _d['L0_attn_x_bld']
    _d['L0_attn_x_bld'] = jax.random.normal(jax.random.fold_in(jax.random.key(seed), 1), (8, 512, 256), dtype=_x0.dtype)
    del _x0
    return _d

def reference(L0_attn_x_bld, L0_attn_Wq, L0_attn_Wkv_down, L0_attn_Wk_up, L0_attn_Wv_up, L0_attn_Wout, L0_ffn_gate_w, L0_ffn_gate_b, L0_ffn_shared_wg, L0_ffn_shared_wu, L0_ffn_shared_wd, L0_ffn_experts_wg, L0_ffn_experts_wu, L0_ffn_experts_wd, L1_attn_W_DQ, L1_attn_W_UQ, L1_attn_W_DKV, L1_attn_W_UKV, L1_attn_W_QR, L1_attn_W_KR, L1_attn_W_O, L1_attn_q_norm_w, L1_attn_k_norm_w, L1_ffn_W_fc, L1_ffn_W_proj):

    def _L0_attn_ref(x_bld, Wq, Wkv_down, Wk_up, Wv_up, Wout):
        import jax, jax.numpy as jnp
        import numpy as np
        B, L, D = (2, 512, 256)
        H, HD = (16, 64)
        LD = 64
        q_blhd = jnp.einsum('bld,dhk->blhk', x_bld, Wq)
        latent_bll = jnp.einsum('bld,dc->blc', x_bld, Wkv_down)
        k_blhd = jnp.einsum('blc,chk->blhk', latent_bll, Wk_up)
        v_blhd = jnp.einsum('blc,chk->blhk', latent_bll, Wv_up)
        attn = jnp.einsum('bqhd,bkhd->bhqk', q_blhd, k_blhd) / jnp.sqrt(jnp.asarray(HD, dtype=x_bld.dtype))
        l = x_bld.shape[1]
        mask = (jnp.arange(l)[None, :] <= jnp.arange(l)[:, None])[None, None]
        neg_inf = jnp.finfo(attn.dtype).min
        attn = jax.nn.softmax(jnp.where(mask, attn, neg_inf), axis=-1)
        y_blhd = jnp.einsum('bhqk,bkhd->bqhd', attn, v_blhd)
        return jnp.einsum('bqhd,hdo->bqo', y_blhd, Wout)

    def _L0_ffn_ref(x, gate_w, gate_b, shared_wg, shared_wu, shared_wd, experts_wg, experts_wu, experts_wd):
        import jax, jax.numpy as jnp
        import numpy as np
        B, S, D = (2, 512, 256)
        I = 128
        E = 16
        TOP_K = 2

        def _mlp(x, wg, wu, wd):
            return jnp.einsum('bsi,id->bsd', jax.nn.silu(x @ wg) * (x @ wu), wd)
        router_logits = jax.nn.sigmoid(x @ gate_w + gate_b)
        expert_values, expert_indices = jax.lax.top_k(router_logits, k=TOP_K)
        expert_values = expert_values / jnp.sum(expert_values, axis=-1, keepdims=True)
        hg = jnp.einsum('bsd,edi->bsei', x, experts_wg)
        hu = jnp.einsum('bsd,edi->bsei', x, experts_wu)
        all_outputs = jnp.einsum('bsei,eid->bsed', jax.nn.silu(hg) * hu, experts_wd)
        selected = jnp.take_along_axis(all_outputs, expert_indices[..., None], axis=2)
        expert_weighted = jnp.sum(expert_values[..., None] * selected, axis=2)
        return x + _mlp(x, shared_wg, shared_wu, shared_wd) + expert_weighted

    def _L1_attn_ref(x, W_DQ, W_UQ, W_DKV, W_UKV, W_QR, W_KR, W_O, q_norm_w, k_norm_w):
        import jax, jax.numpy as jnp
        import numpy as np
        B, T, D = (2, 512, 256)
        H = 16
        HD = D // H
        DL = 128
        NR = 64
        EPS = 1.1920929e-07

        def _rms_norm(x, w):
            ms = jnp.mean(jnp.square(x), axis=-1, keepdims=True)
            return x * jax.lax.rsqrt(ms + EPS) * w
        b, t, d = x.shape
        scale = HD ** (-0.5)
        xh = x.reshape(b, t, H, HD).transpose(0, 2, 1, 3)
        c_q = jnp.einsum('bhtd,ld->bhtl', xh, W_DQ)
        q_c = jnp.einsum('bhtl,dl->bhtd', c_q, W_UQ)
        q_c_norm = _rms_norm(q_c, q_norm_w)
        q_r = jnp.einsum('bhtd,rd->bhtr', q_c_norm, W_QR)
        q = jnp.concatenate([q_c_norm, q_r], axis=-1)
        c_kv = jnp.einsum('bhtd,ld->bhtl', xh, W_DKV)
        kv = jnp.einsum('bhtl,dl->bhtd', c_kv, W_UKV)
        k_c, v_c = (kv[..., :HD], kv[..., HD:])
        k_c_norm = _rms_norm(k_c, k_norm_w)
        k_r = jnp.einsum('bhtd,rd->bhtr', xh, W_KR)
        k = jnp.concatenate([k_c_norm, k_r], axis=-1)
        scores = jnp.einsum('bhqd,bhkd->bhqk', q, k) * scale
        causal = jnp.triu(jnp.full((t, t), -jnp.inf, dtype=scores.dtype), k=1)
        attn = jax.nn.softmax(scores + causal, axis=-1)
        ctx = jnp.einsum('bhqk,bhkd->bhqd', attn, v_c)
        out = jnp.einsum('bhtd,od->bhto', ctx, W_O)
        return out.transpose(0, 2, 1, 3).reshape(b, t, d)

    def _L1_ffn_ref(x, W_fc, W_proj):
        import jax, jax.numpy as jnp
        import numpy as np
        import math
        BETA = 0.9
        THRESHOLD = 1.0
        NUM_STEPS = 5
        ALPHA = 2.0

        @jax.custom_vjp
        def spike_fn(u):
            return (u > 0).astype(u.dtype)

        def _spike_fwd(u):
            return (spike_fn(u), u)

        def _spike_bwd(u, g):
            s = jnp.pi / 2.0 * ALPHA * u
            return (g * (ALPHA / 2.0) / (1.0 + s * s),)
        spike_fn.defvjp(_spike_fwd, _spike_bwd)
        h = jnp.square(jax.nn.relu(jnp.einsum('bsd,fd->bsf', x, W_fc)))
        y = jnp.einsum('bsf,df->bsd', h, W_proj)

        def step(mem, _):
            reset = jax.lax.stop_gradient(spike_fn(mem - THRESHOLD))
            mem_new = BETA * mem + y - reset * THRESHOLD
            spk = spike_fn(mem_new - THRESHOLD)
            return (mem_new, spk)
        mem0 = jnp.zeros_like(y)
        _, spks = jax.lax.scan(step, mem0, None, length=NUM_STEPS)
        return jnp.sum(spks, axis=0) / NUM_STEPS
    x = L0_attn_x_bld
    x = _layernorm(x + _L0_attn_ref(x, L0_attn_Wq, L0_attn_Wkv_down, L0_attn_Wk_up, L0_attn_Wv_up, L0_attn_Wout), axis=-1)
    x = _layernorm(x + _L0_ffn_ref(x, L0_ffn_gate_w, L0_ffn_gate_b, L0_ffn_shared_wg, L0_ffn_shared_wu, L0_ffn_shared_wd, L0_ffn_experts_wg, L0_ffn_experts_wu, L0_ffn_experts_wd), axis=-1)
    x = _layernorm(x + _L1_attn_ref(x, L1_attn_W_DQ, L1_attn_W_UQ, L1_attn_W_DKV, L1_attn_W_UKV, L1_attn_W_QR, L1_attn_W_KR, L1_attn_W_O, L1_attn_q_norm_w, L1_attn_k_norm_w), axis=-1)
    x = _layernorm(x + _L1_ffn_ref(x, L1_ffn_W_fc, L1_ffn_W_proj), axis=-1)
    return x

_drawn_inputs = setup_inputs


def setup_inputs(seed=0):
    import zlib

    import numpy as np

    out = dict(_drawn_inputs(seed))
    spreads = {'L0_ffn_gate_b': (0.0, 0.1),
     'L1_attn_q_norm_w': (1.0, 0.6),
     'L1_attn_k_norm_w': (1.0, 0.6)}
    factors = {'L1_attn_W_DQ': 8.0,
     'L1_attn_W_UQ': 8.0,
     'L1_attn_W_DKV': 8.0,
     'L1_attn_W_UKV': 8.0,
     'L1_attn_W_QR': 8.0,
     'L1_attn_W_KR': 8.0,
     'L1_attn_W_O': 8.0}
    for name, (base, spread) in spreads.items():
        noise = np.random.default_rng([zlib.crc32(name.encode()), seed]).standard_normal(out[name].shape)
        drawn = base * np.exp(spread * noise) if base else spread * noise
        out[name] = jnp.asarray(drawn.astype(out[name].dtype))
    for name, factor in factors.items():
        out[name] = (out[name] * factor).astype(out[name].dtype)
    return out
```

```python
from contextlib import ExitStack

import numpy as np
import concourse.bass as bass
from concourse import mybir
from concourse.alu_op_type import AluOpType as ALU

F32 = mybir.dt.float32
R32 = mybir.dt.float32r
U32 = mybir.dt.uint32
I32 = mybir.dt.int32
ACT = mybir.ActivationFunctionType
AX = mybir.AxisListType

P = 128
B, L, D = 8, 512, 256
KT = D // P
TT = L // P
NT = B * TT
H = 16
LD = 64
NPAIR = H // 2
E, I = 16, 128
NW = E + 1
HD = D // H
FF = 1024
NF = FF // P
LN_EPS = 1e-5
RMS_EPS = 1.1920929e-07
MASKED = -1.0e30

QOFF = [P * i * (i + 1) // 2 for i in range(TT + 1)]
TRI = QOFF[TT]
SGROUP = [[0, 1], [2], [3]]
SCOL = [0, P, 0, 0]
TGROUPS = [[0], [1, 3], [2]]
TCOL = {0: 0, 1: L, 3: L + 3 * P, 2: 2 * L}
TGCOL = [0, L, 2 * L]
TGLEN = [L, L, 2 * P]


class Held:

    def __init__(self, nc, ctx, stage):
        self.nc, self.ctx, self.stage, self.sems = nc, ctx, stage, []
        ctx.callback(self.clear)

    def clear(self):
        self.nc.clear_and_free_semaphores(self.sems)
        self.nc.all_engine_barrier()

    def sb(self, name, shape, dt=F32):
        return self.ctx.enter_context(self.nc.sbuf_tensor(f"{self.stage}_{name}", shape, dt))

    def ps(self, name):
        return self.ctx.enter_context(self.nc.psum_tensor(f"{self.stage}_{name}", [P, 512], F32))

    def sem(self, name, from1=False):
        self.sems.append(self.nc.alloc_semaphore(f"{self.stage}_{name}" + ("_from1" if from1 else "")))
        return self.sems[-1]


def start_at_one(eng, *sems):
    for s in sems:
        eng.sem_inc(s, 1)


def need(eng, sem, value):
    if not isinstance(value, int) or value > 0:
        eng.wait_ge(sem, value + 1 if sem.name.endswith("_from1") else value)


def hold(eng, sem, value, passed):
    need(eng, sem, value)
    eng.sem_inc(passed, 1)


class Softmax:

    def __init__(self, S, C, ring):
        self.S, self.C, self.ring = S, C, ring
        self.prob = S.sb("prob", [P, 4, TRI])
        self.probT = S.sb("probT", [P, ring, TRI])
        self.negmax, self.rowsum, self.recip = (
            S.sb(n, [P, 4, TT]) for n in ("negmax", "rowsum", "recip"))
        self.ps_score = [S.ps(f"ps_score{g}") for g in range(3)]
        self.ps_trans = [S.ps(f"ps_trans{g}") for g in range(2)]
        self.s_score, self.s_max, self.s_exp, self.s_recip, self.s_norm, self.s_trans, self.passed = (
            S.sem(n) for n in ("score", "max", "exp", "recip", "norm", "trans", "passed"))
        self.s_pt_act, self.s_pt_dve = S.sem("pt_act", True), S.sem("pt_dve", True)

    def scores(self, pe, n, h, product):
        for g, tiles in enumerate(SGROUP):
            need(pe, self.s_max, n * TT - TT + tiles[-1] + 1)
            for i in tiles:
                keys = P * (i + 1)
                at = SCOL[i]
                last = product(self.ps_score[g][:, at:at + keys], i, keys)
            last.then_inc(self.s_score, 1)

    def mask_max(self, dve, n, h):
        for g, tiles in enumerate(SGROUP):
            hold(dve, self.s_score, n * 3 + g + 1, self.passed)
            for i in tiles:
                keys = P * (i + 1)
                at = SCOL[i]
                dve.tensor_tensor_reduce(
                    out=self.prob[:, h % 4, QOFF[i]:QOFF[i] + keys],
                    in0=self.ps_score[g][:, at:at + keys], in1=self.C.mask[:, L - keys:L], scale=-1.0,
                    scalar=3.0e38, op0=ALU.add, op1=ALU.min,
                    accum_out=self.negmax[:, h % 4, i:i + 1]).then_inc(self.s_max, 1)

    def exps(self, act, n, h):
        for i in range(TT):
            need(act, self.s_max, n * TT + i + 1)
            at = self.prob[:, h % 4, QOFF[i]:QOFF[i + 1]]
            act.activation(at, at, ACT.Exp, scale=-1.0, bias=self.negmax[:, h % 4, i:i + 1],
                           accum_out=self.rowsum[:, h % 4, i:i + 1]).then_inc(self.s_exp, 1)

    def normalise(self, dve, n, h):
        need(dve, self.s_exp, n * TT + TT)
        dve.reciprocal(self.recip[:, h % 4, :], self.rowsum[:, h % 4, :]).then_inc(self.s_recip, 1)
        need(dve, self.s_recip, n + 1)
        for i in range(TT):
            at = self.prob[:, h % 4, QOFF[i]:QOFF[i + 1]]
            dve.tensor_scalar(at, at, self.recip[:, h % 4, i:i + 1], None,
                              ALU.mult).then_inc(self.s_norm, 1)

    def transposes(self, pe, n, h):
        need(pe, self.s_norm, n * TT + TT)
        for g, tiles in enumerate(TGROUPS):
            if g == 0:
                need(pe, self.s_pt_dve, n)
            elif g == 1:
                need(pe, self.s_pt_act, n * 2)
            else:
                need(pe, self.s_pt_act, n * 2 + 1)
            for k, i in [(k, i) for k in tiles for i in range(k, TT)]:
                col = TCOL[k] - TGCOL[g] + P * (i - k)
                last = pe.transpose(self.ps_trans[(3 * h + g) % 2][:, col:col + P],
                                    self.prob[:, h % 4, QOFF[i] + P * k:QOFF[i] + P * (k + 1)],
                                    self.C.ident[:])
            last.then_inc(self.s_trans, 1)

    def copy_group(self, eng, n, h, g):
        need(eng, self.s_trans, n * 3 + g + 1)
        out = self.probT[:, h % self.ring, TGCOL[g]:TGCOL[g] + TGLEN[g]]
        src = self.ps_trans[(3 * h + g) % 2][:, 0:TGLEN[g]]
        if g == 1:
            eng.tensor_copy(out, src).then_inc(self.s_pt_dve, 1)
        else:
            eng.activation(out, src, ACT.Copy).then_inc(self.s_pt_act, 1)

    def need_probT(self, pe, n):
        need(pe, self.s_pt_act, n * 2 + 2)
        need(pe, self.s_pt_dve, n + 1)


def over_batches(eng, start, slot, finish):
    start(0)
    slot(0, 0)
    slot(0, 1)
    with eng.Fori(0, B - 1) as b:
        for h in range(2, H):
            slot(b, h)
        start(b + 1)
        for h in range(2):
            slot(b + 1, h)
            slot(b, H + h)
        finish(b)
    for h in range(2, H + 2):
        slot(B - 1, h)
    finish(B - 1)


def layer0_attention(nc, X, C, A):
    with ExitStack() as ctx:
        S = Held(nc, ctx, "a0")
        wqk = S.sb("wqk", [P, KT, H * LD])
        wvo = S.sb("wvo", [P, NPAIR, D])
        wdn2 = S.sb("wdn2", [P, KT, 2, LD])

        with ExitStack() as pctx:
            W = Held(nc, pctx, "a0w")
            wqT = W.sb("wqT", [LD, H, D])
            wkT = W.sb("wkT", [LD, H, LD])
            wvT = W.sb("wvT", [LD, H, LD])
            wo = W.sb("wo", [LD, H, D])
            s_load, s_qk, s_vo, s_cp = W.sem("load"), W.sem("qk"), W.sem("vo"), W.sem("cp")
            s_cv = W.sem("cv")
            pqk = [W.ps("pqk0"), W.ps("pqk1")]
            pvo = [W.ps("pvo0"), W.ps("pvo1")]
            with nc.Block() as blk:
                @blk.sync
                def _(sp):
                    for dst, src in ((wqT, A["wqT"]), (wkT, A["wkT"]), (wvT, A["wvT"]), (wo, A["wo"])):
                        sp.dma_start(dst[:], src).then_inc(s_load, 16)
                    for c in range(2):
                        sp.dma_start(wdn2[:, :, c, :], A["wdn"].rearrange("(k p) c -> p k c", p=P)
                                     ).then_inc(s_load, 16)
                    need(sp, s_load, 16 * 6)

                @blk.tensor
                def _(pe):
                    need(pe, s_load, 16 * 6)
                    for k in range(KT):
                        for half in range(2):
                            n = 2 * k + half
                            if n >= 2:
                                need(pe, s_cp, n - 1)
                            for h in range(8):
                                hh = 8 * half + h
                                ins = pe.matmul(pqk[n % 2][:, h * LD:(h + 1) * LD],
                                                wqT[:, hh, k * P:(k + 1) * P], wkT[:, hh, :],
                                                start=True, stop=True)
                            ins.then_inc(s_qk, 1)
                    for p in range(NPAIR):
                        if p >= 2:
                            need(pe, s_cv, p - 1)
                        for c in range(2):
                            ins = pe.matmul(pvo[p % 2][LD * c:LD * (c + 1), 0:D], wvT[:, 2 * p + c, :],
                                            wo[:, 2 * p + c, :], start=True, stop=True)
                        ins.then_inc(s_vo, 1)

                @blk.scalar
                def _(act):
                    for n in range(4):
                        need(act, s_qk, n + 1)
                        act.activation(wqk[:, n // 2, 512 * (n % 2):512 * (n % 2 + 1)], pqk[n % 2][:],
                                       ACT.Copy, scale=LD ** -0.5).then_inc(s_cp, 1)

                @blk.vector
                def _(dve):
                    for p in range(NPAIR):
                        need(dve, s_vo, p + 1)
                        dve.tensor_copy(wvo[:, p, :], pvo[p % 2][:, 0:D]).then_inc(s_cv, 1)

        sm = Softmax(S, C, 4)
        xT = S.sb("xT", [P, KT, L])
        xtok = S.sb("xtok", [P, TT, D])
        kh = S.sb("kh", [P, L], R32)
        kl = S.sb("kl", [P, L], R32)
        latv = S.sb("latv", [P, TT, LD])
        qs = S.sb("qs", [P, 2, 2, L], R32)
        qlow = S.sb("qlow", [P, 2, L], R32)
        yT = S.sb("yT", [P, NPAIR, L])
        ln = LayerNorm(S, C, X, TT)
        ps_q, ps_y, ps_kv = S.ps("ps_q"), S.ps("ps_y"), S.ps("ps_kv")
        ps_out = [ps_y, ps_kv]
        s_xT, s_xtok, s_qdma = S.sem("xT"), S.sem("xtok"), [S.sem("qdma0"), S.sem("qdma1")]
        s_lat, s_v, s_q, s_y, s_out = S.sem("lat"), S.sem("v"), S.sem("q"), S.sem("y"), S.sem("out", True)
        s_kh, s_latv, s_qhi, s_yc = S.sem("kh"), S.sem("latv"), S.sem("qhi"), S.sem("yc", True)
        s_kl, s_qlo = S.sem("kl"), S.sem("qlo")
        s_pass_sp = S.sem("pass_sp")

        with nc.Block() as blk:
            @blk.sync
            def _(sp):
                def load_x(b):
                    if not isinstance(b, int):
                        hold(sp, s_q, b * NPAIR, s_pass_sp)
                        hold(sp, s_v, b, s_pass_sp)
                    sp.dma_start(xT[:], A["xT"][bass.ds(b, 1), :, :].rearrange(
                        "o (k p) t -> p (o k) t", p=P)).then_inc(s_xT, 16)

                def load_tokens(b):
                    hold(sp, ln.s_sum, b * TT, s_pass_sp)
                    sp.dma_start(xtok[:], A["x"][bass.ds(b, 1), :, :].rearrange(
                        "o (t p) d -> p (o t) d", p=P)).then_inc(s_xtok, 16)

                def low_words(b, p):
                    hold(sp, s_qlo, b * (2 * NPAIR) + 2 * p + 2, s_pass_sp)
                    for c in range(2):
                        rows, to = slice(LD * c, LD * (c + 1)), slice(LD * (1 - c), LD * (2 - c))
                        sp.dma_start(qs[to, p % 2, c, :].bitcast(F32),
                                     qlow[rows, p % 2, :].bitcast(F32)).then_inc(s_qdma[p % 2], 16)

                def low_words_and_tokens(b):
                    for p in range(1, NPAIR):
                        low_words(b, p)
                        if p == 1:
                            load_tokens(b)

                load_x(0)
                low_words(0, 0)
                with sp.Fori(0, B - 1) as b:
                    low_words_and_tokens(b)
                    load_x(b + 1)
                    low_words(b + 1, 0)
                low_words_and_tokens(B - 1)

            @blk.tensor
            def _(pe):
                def project(b, p):
                    need(pe, s_qlo, b * (2 * NPAIR) + 2 * p)
                    for k in range(KT):
                        last = pe.matmul(ps_q[:], wqk[:, k, P * p:P * (p + 1)], xT[:, k, :],
                                         start=k == 0, stop=k == KT - 1)
                    last.then_inc(s_q, 1)

                def scores(b, h):
                    p = h // 2
                    need(pe, s_qhi, b * (2 * NPAIR) + 2 * p + 2)
                    need(pe, s_qdma[p % 2], b * (16 * NPAIR) + 32 * (p // 2 + 1))
                    if h == 0:
                        need(pe, s_kl, b + 1)

                    def product(out, i, keys):
                        q = qs[:, p % 2, h % 2, P * i:P * (i + 1)]
                        pe.matmul(out, q, kh[:, 0:keys], start=True, stop=False)
                        return pe.matmul(out, q, kl[:, 0:keys], start=False, stop=True)

                    sm.scores(pe, b * H + h, h, product)

                def attend(b, p):
                    sm.need_probT(pe, b * H + 2 * p + 1)
                    need(pe, s_yc, b * NPAIR + p)
                    if p == 0:
                        need(pe, s_latv, b + 1)
                        need(pe, ln.s_sum, b * TT)
                    for k in range(TT):
                        for c in range(2):
                            n = TCOL[k]
                            last = pe.matmul(ps_y[LD * c:LD * (c + 1), P * k:L], latv[:, k, :],
                                             sm.probT[:, (2 * p + c) % 4, n:n + L - P * k],
                                             start=k == 0, stop=k == TT - 1)
                    last.then_inc(s_y, 1)

                def values(b):
                    for t in range(TT):
                        for k in range(KT):
                            last = pe.matmul(ps_kv[:, LD * t:LD * (t + 1)], xT[:, k, P * t:P * (t + 1)],
                                             wdn2[:, k, 0, :], start=k == 0, stop=k == KT - 1)
                    last.then_inc(s_v, 1)

                def start(b):
                    need(pe, s_xT, b * 16 + 16)
                    need(pe, ln.s_sum, (b - 1) * TT)
                    for k in range(KT):
                        last = pe.matmul(ps_kv[:], wdn2[:, k, :, :], xT[:, k, :],
                                         start=k == 0, stop=k == KT - 1)
                    last.then_inc(s_lat, 1)
                    project(b, 0)
                    if isinstance(b, int):
                        need(pe, s_kl, b + 1)
                        values(b)

                def slot(b, h):
                    if h < H:
                        scores(b, h)
                    if h % 2 == 0 and h + 2 < H:
                        project(b, h // 2 + 1)
                    if h >= 5 and h % 2:
                        attend(b, (h - 5) // 2)
                    if h >= 2:
                        sm.transposes(pe, b * H + h - 2, (h - 2) % H)

                def finish(b):
                    attend(b, NPAIR - 1)
                    if not isinstance(b, int):
                        values(b + 1)
                        need(pe, s_latv, b + 2)
                    need(pe, s_yc, b * NPAIR + NPAIR)
                    for t in range(TT):
                        if t >= 2:
                            need(pe, ln.s_sum, b * TT + t - 1)
                        for p in range(NPAIR):
                            last = pe.matmul(ps_out[t % 2][:, 0:D], yT[:, p, P * t:P * (t + 1)],
                                             wvo[:, p, :], start=p == 0, stop=p == NPAIR - 1)
                        last.then_inc(s_out, 1)

                start_at_one(pe, s_out)
                over_batches(pe, start, slot, finish)

            @blk.scalar
            def _(act):
                def q_high(b, p):
                    need(act, s_q, b * NPAIR + p + 1)
                    act.activation(qs[0:LD, p % 2, 0, :], ps_q[0:LD, :], ACT.Copy).then_inc(s_qhi, 1)
                    act.activation(qs[LD:P, p % 2, 1, :], ps_q[LD:P, :], ACT.Copy).then_inc(s_qhi, 1)

                def values(b):
                    need(act, s_v, b + 1)
                    act.activation(latv[:], ps_kv[:, 0:TT * LD].rearrange("p (t c) -> p t c", t=TT),
                                   ACT.Copy).then_inc(s_latv, 1)

                def start(b):
                    need(act, s_lat, b + 1)
                    act.activation(kh[:], ps_kv[:], ACT.Copy).then_inc(s_kh, 1)
                    q_high(b, 0)
                    if isinstance(b, int):
                        values(b)

                def slot(b, h):
                    if h % 2 == 0 and h + 2 < H:
                        q_high(b, h // 2 + 1)
                    if h < H:
                        sm.exps(act, b * H + h, h)
                    if h >= 2:
                        sm.copy_group(act, b * H + h - 2, (h - 2) % H, 0)
                        sm.copy_group(act, b * H + h - 2, (h - 2) % H, 2)
                    if h >= 5 and h % 2:
                        outputs(b, (h - 5) // 2)

                def outputs(b, p):
                    if p == 0:
                        need(act, s_out, b * TT)
                    need(act, s_y, b * NPAIR + p + 1)
                    act.activation(yT[:, p, :], ps_y[:], ACT.Copy).then_inc(s_yc, 1)

                def finish(b):
                    outputs(b, NPAIR - 1)
                    if not isinstance(b, int):
                        values(b + 1)

                start_at_one(act, sm.s_pt_act, s_yc)
                over_batches(act, start, slot, finish)

            @blk.vector
            def _(dve):
                def q_low(b, p):
                    for c in range(2):
                        rows = slice(LD * c, LD * (c + 1))
                        need(dve, s_qhi, b * (2 * NPAIR) + 2 * p + c + 1)
                        dve.tensor_tensor(qlow[rows, p % 2, :], ps_q[rows, :],
                                          qs[rows, p % 2, c, :].bitcast(F32),
                                          ALU.subtract).then_inc(s_qlo, 1)

                def start(b):
                    need(dve, s_kh, b + 1)
                    dve.tensor_tensor(kl[:], ps_kv[:], kh[:].bitcast(F32), ALU.subtract
                                      ).then_inc(s_kl, 1)
                    q_low(b, 0)

                def slot(b, h):
                    if h < H:
                        sm.mask_max(dve, b * H + h, h)
                    if h >= 2:
                        sm.copy_group(dve, b * H + h - 2, (h - 2) % H, 1)
                    if 1 <= h <= H:
                        sm.normalise(dve, b * H + h - 1, h - 1)
                    if h % 2 == 0 and h + 2 < H:
                        q_low(b, h // 2 + 1)

                def finish(b):
                    need(dve, s_xtok, b * 16 + 16)
                    for t in range(TT):
                        need(dve, s_out, b * TT + t + 1)
                        ln.add(dve, b, t, ps_out[t % 2][:, 0:D], xtok[:, t, :])
                    ln.write(dve, b)

                start_at_one(dve, ln.s_sum, ln.s_x, sm.s_pt_dve)
                over_batches(dve, start, slot, finish)

            @blk.gpsimd
            def _(pool):
                with pool.Fori(0, B) as b:
                    ln.root(pool, b)


class LayerNorm:

    def __init__(self, S, C, X, n):
        self.C, self.X, self.n = C, X, n
        self.res = S.sb("res", [P, n, D])
        self.stats, self.mv, self.rstd = S.sb("stats", [P, n, 6]), S.sb("mv", [P, n, 2]), S.sb("rstd", [P, n])
        self.s_sum, self.s_x = S.sem("ln_sum", True), S.sem("ln_x", True)
        self.s_stat, self.s_mv, self.s_var, self.s_rstd, self.passed = (
            S.sem("ln_" + k) for k in ("stat", "mv", "var", "rstd", "pass"))
        self.passed_pool = S.sem("ln_pass_pool")

    def add(self, dve, b, t, u, v):
        if t == 0:
            need(dve, self.s_x, b * self.n)
        dve.tensor_tensor(self.res[:, t, :], u, v, ALU.add).then_inc(self.s_sum, 1)
        need(dve, self.s_sum, b * self.n + t + 1)
        self.statistics(dve, b, t)

    def statistics(self, dve, b, t):
        dve.bn_stats(self.stats[:, t, :], self.res[:, t, :]).then_inc(self.s_stat, 1)
        hold(dve, self.s_stat, b * self.n + t + 1, self.passed)
        dve.bn_aggr(self.mv[:, t, :], self.stats[:, t, :]).then_inc(self.s_mv, 1)

    def root(self, pool, b):
        hold(pool, self.s_mv, b * self.n + self.n, self.passed_pool)
        pool.tensor_scalar(self.rstd[:], self.mv[:, :, 1], LN_EPS, None, ALU.add).then_inc(self.s_var, 1)
        hold(pool, self.s_var, b + 1, self.passed_pool)
        pool.tensor_tensor(self.rstd[:], self.rstd[:], self.C.minus_half[:, 0:self.n],
                           ALU.pow).then_inc(self.s_rstd, 1)

    def write(self, dve, b):
        need(dve, self.s_rstd, b + 1)
        for t in range(self.n):
            dve.tensor_scalar(self.X[:, bass.ds(b * self.n + t, 1), :].rearrange("p o d -> p (o d)"),
                              self.res[:, t, :], self.mv[:, t, 0:1], self.rstd[:, t:t + 1],
                              ALU.subtract, ALU.mult).then_inc(self.s_x, 1)


NS = 80
SLOTS = NS * P
GT = 4
GL = GT * P
NG = NT // GT


class Features:

    def __init__(self, S, C, X):
        self.C, self.X = C, X
        self.tok = [S.sb(f"tok{j}", [P, GT, D]) for j in range(2)]
        self.xs = [S.sb(f"xs{j}", [P, KT, GL]) for j in range(2)]
        self.ps = [S.ps(f"ps_turn{k}") for k in range(KT)]
        self.s_tok, self.s_turn, self.s_xs = S.sem("tok"), S.sem("turn"), S.sem("xs")
        self.passed = S.sem("tok_pass")

    def fetch(self, pool, g, j):
        if not isinstance(g, int) or g >= 2:
            hold(pool, self.s_turn, g * KT - KT, self.passed)
        pool.tensor_copy(self.tok[j][:], self.X[:, bass.ds(g * GT, GT), :]).then_inc(self.s_tok, 1)

    def turn(self, pe, g, j):
        need(pe, self.s_tok, g + 1)
        for k in range(KT):
            need(pe, self.s_xs, g * KT - KT + k + 1)
            for t in range(GT):
                last = pe.transpose(self.ps[k][:, P * t:P * (t + 1)],
                                    self.tok[j][:, t, P * k:P * (k + 1)], self.C.ident[:])
            last.then_inc(self.s_turn, 1)

    def keep(self, act, g, j):
        for k in range(KT):
            need(act, self.s_turn, g * KT + k + 1)
            act.activation(self.xs[j][:, k, :], self.ps[k][:], ACT.Copy).then_inc(self.s_xs, 1)


def in_twos(eng, n, step):
    step(0, 0)
    step(1, 1)
    with eng.Fori(1, n // 2) as r:
        for j in range(2):
            step(r * 2 + j, j)


def shared_expert(nc, X, base, logits, C, A, Z):
    with ExitStack() as ctx:
        S = Held(nc, ctx, "m1")
        F = Features(S, C, X)
        gate = S.sb("gate", [P, KT, E])
        wgu = S.sb("wgu", [P, KT, 2, I])
        wd = S.sb("wd", [I, D])
        zero = S.sb("zero", [P, 5 * D])
        act_g = [S.sb(f"act{j}", [I, GL]) for j in range(2)]
        hid = [S.sb(f"hid{j}", [I, GL]) for j in range(2)]
        ps_gate, ps_g, ps_u = S.ps("ps_gate"), S.ps("ps_g"), S.ps("ps_u")
        ps_d = [S.ps("ps_d0"), S.ps("ps_d1")]
        s_w, s_z, s_zero = S.sem("w"), S.sem("z"), S.sem("zero")
        s_gate, s_gu, s_down = S.sem("gate"), S.sem("gu"), S.sem("down")
        s_log, s_silu, s_hid, s_base = S.sem("log"), S.sem("silu"), S.sem("hid"), S.sem("base")
        with nc.Block() as blk:
            @blk.sync
            def _(sp):
                sp.dma_start(gate[:], A["gate_w"].rearrange("(k p) e -> p k e", p=P)).then_inc(s_w, 16)
                sp.dma_start(wgu[:, :, 0, :], A["swg"].rearrange("(k p) i -> p k i", p=P)).then_inc(s_w, 16)
                sp.dma_start(wgu[:, :, 1, :], A["swu"].rearrange("(k p) i -> p k i", p=P)).then_inc(s_w, 16)
                sp.dma_start(wd[:], A["swd"]).then_inc(s_w, 16)
                need(sp, s_zero, 1)
                for n in range(16):
                    sp.dma_start(Z[bass.ts(n, SLOTS // 16), :].rearrange("(p a) d -> p (a d)", p=P),
                                 zero[:]).then_inc(s_z, 16)
                need(sp, s_z, 16 * 16)

            @blk.gpsimd
            def _(pool):
                pool.memset(zero[:], 0.0).then_inc(s_zero, 1)
                F.fetch(pool, 0, 0)
                F.fetch(pool, 1, 1)
                with pool.Fori(1, NG // 2) as r:
                    for j in range(2):
                        F.fetch(pool, r * 2 + j, j)

            @blk.tensor
            def _(pe):
                need(pe, s_w, 64)

                def step(g, j):
                    F.turn(pe, g, j)
                    need(pe, F.s_xs, g * KT + KT)
                    need(pe, s_log, g)
                    for t in range(GT):
                        for k in range(KT):
                            last = pe.matmul(ps_gate[:, E * t:E * (t + 1)],
                                             F.xs[j][:, k, P * t:P * (t + 1)], gate[:, k, :],
                                             start=k == 0, stop=k == KT - 1)
                    last.then_inc(s_gate, 1)
                    need(pe, s_hid, g)
                    for c, ps in enumerate((ps_g, ps_u)):
                        for k in range(KT):
                            last = pe.matmul(ps[:], wgu[:, k, c, :], F.xs[j][:, k, :],
                                             start=k == 0, stop=k == KT - 1)
                        last.then_inc(s_gu, 1)
                    need(pe, s_hid, g + 1)
                    need(pe, s_base, g * 2)
                    for t in range(GT):
                        last = pe.matmul(ps_d[t // 2][:, D * (t % 2):D * (t % 2 + 1)],
                                         hid[j][:, P * t:P * (t + 1)], wd[:], start=True, stop=True)
                        if t % 2:
                            last.then_inc(s_down, 1)

                in_twos(pe, NG, step)

            @blk.scalar
            def _(act):
                def step(g, j):
                    need(act, s_down, g * 2 - 2)
                    F.keep(act, g, j)
                    need(act, s_gate, g + 1)
                    act.activation(logits[:, bass.ds(g * GT, GT), :],
                                   ps_gate[:, 0:GT * E].rearrange("p (t e) -> p t e", e=E),
                                   ACT.Copy).then_inc(s_log, 1)
                    need(act, s_gu, g * 2 + 1)
                    act.activation(act_g[j][:], ps_g[:], ACT.Silu).then_inc(s_silu, 1)

                in_twos(act, NG, step)

            @blk.vector
            def _(dve):
                def step(g, j):
                    need(dve, s_silu, g + 1)
                    need(dve, s_gu, g * 2 + 2)
                    dve.tensor_tensor(hid[j][:], act_g[j][:], ps_u[:], ALU.mult).then_inc(s_hid, 1)
                    for c in range(2):
                        need(dve, s_down, g * 2 + c + 1)
                        tiles = bass.ds(g * GT + 2 * c, 2)
                        dve.scalar_tensor_tensor(
                            base[:, tiles, :], X[:, tiles, :], 2.0,
                            ps_d[c][:].rearrange("p (t d) -> p t d", d=D), ALU.mult, ALU.add
                        ).then_inc(s_base, 1)

                in_twos(dve, NG, step)


def route(nc, logits, slot, weight, tile_expert, C, A):
    with ExitStack() as ctx:
        S = Held(nc, ctx, "m2")
        bias = S.sb("bias", [P, E])
        iota = S.sb("iota", [P, E])
        tiota = S.sb("tiota", [P, NS])
        before = S.sb("before", [P, P])
        ones = S.sb("ones", [P, P])
        sig = S.sb("sig", [P, NT, E])
        top = S.sb("top", [P, NT, 8])
        tidx = S.sb("tidx", [P, NT, 8], U32)
        idx = S.sb("idx", [P, NT, 2])
        total = S.sb("total", [P, NT])
        hot = [S.sb(f"hot{c}", [P, NT, E]) for c in range(2)]
        count = S.sb("count", [P, NT, E])
        scan = [S.sb("scan0", [P, NT, E]), S.sb("scan1", [P, NT, E])]
        pos = S.sb("pos", [P, NT, E])
        big = S.sb("big", [P, E, 32])
        thr = S.sb("thr", [P, 32])
        lower = S.sb("lower", [P, E, E])
        prod = S.sb("prod", [P, E, E])
        tiles, first, after = S.sb("tiles", [P, E]), S.sb("first", [P, E]), S.sb("after", [P, E])
        cmp = S.sb("cmp", [P, NS, E])
        te = S.sb("te", [P, NS])
        slotf = S.sb("slotf", [P, NT, 2])
        ps_rank, ps_tot = S.ps("ps_rank"), S.ps("ps_tot")
        s_w, s_sig, s_ps, s_v, s_bias, s_c, s_pass = (S.sem(n) for n in (
            "w", "sig", "ps", "v", "bias", "c", "pass"))
        with nc.Block() as blk:
            @blk.sync
            def _(sp):
                for dst, src in ((bias, "gate_b"), (iota, "iota"), (tiota, "tiota"), (before, "before"),
                                 (thr, "thr"), (lower, "lower")):
                    sp.dma_start(dst[:], A[src]).then_inc(s_w, 16)

            @blk.scalar
            def _(act):
                need(act, s_bias, 1)
                act.activation(sig[:], sig[:], ACT.Sigmoid).then_inc(s_sig, 1)

            @blk.tensor
            def _(pe):
                need(pe, s_c, 1)
                c = count[:].rearrange("p t e -> p (t e)")
                pe.matmul(ps_rank[:], before[:], c, start=True, stop=True)
                pe.matmul(ps_tot[:], ones[:], c, start=True, stop=True).then_inc(s_ps, 1)

            @blk.vector
            def _(dve):
                done = [0]

                def do(ins):
                    done[0] += 1
                    ins.then_inc(s_v, 1)
                    need(dve, s_v, done[0])

                def over_e(ap):
                    return ap.unsqueeze(2).to_broadcast([P, NT, E])

                need(dve, s_w, 16 * 6)
                do(dve.memset(ones[:], 1.0))
                dve.tensor_tensor(sig[:], logits[:], bias[:].unsqueeze(1).to_broadcast([P, NT, E]),
                                  ALU.add).then_inc(s_bias, 1)
                need(dve, s_sig, 1)
                for t in range(NT):
                    dve.max(top[:, t, :], sig[:, t, :]).then_inc(s_v, 1)
                done[0] += NT
                need(dve, s_v, done[0])
                for t in range(NT):
                    dve.max_index(tidx[:, t, :], top[:, t, :], sig[:, t, :]).then_inc(s_v, 1)
                done[0] += NT
                need(dve, s_v, done[0])
                do(dve.tensor_tensor(total[:], top[:, :, 0], top[:, :, 1], ALU.add))
                do(dve.reciprocal(total[:], total[:]))
                do(dve.tensor_tensor(weight[:], top[:, :, 0:2],
                                     total[:].unsqueeze(2).to_broadcast([P, NT, 2]), ALU.mult))
                do(dve.tensor_copy(idx[:], tidx[:, :, 0:2]))
                for c in range(2):
                    do(dve.tensor_tensor(hot[c][:], iota[:].unsqueeze(1).to_broadcast([P, NT, E]),
                                         over_e(idx[:, :, c]), ALU.is_equal))
                dve.tensor_tensor(count[:], hot[0][:], hot[1][:], ALU.add).then_inc(s_c, 1)
                need(dve, s_ps, 1)
                tot = ps_tot[:].rearrange("p (t e) -> p t e", e=E)
                do(dve.tensor_copy(scan[0][:], tot))
                n, d = 0, 1
                while d < NT:
                    do(dve.tensor_copy(scan[1 - n][:, 0:d, :], scan[n][:, 0:d, :]))
                    do(dve.tensor_tensor(scan[1 - n][:, d:NT, :], scan[n][:, d:NT, :],
                                         scan[n][:, 0:NT - d, :], ALU.add))
                    n, d = 1 - n, 2 * d
                run = scan[n]
                do(dve.tensor_tensor(big[:], run[:, NT - 1, :].unsqueeze(2).to_broadcast([P, E, 32]),
                                     thr[:].unsqueeze(1).to_broadcast([P, E, 32]), ALU.is_gt))
                do(dve.tensor_reduce(tiles[:], big[:], AX.X, ALU.add))
                do(dve.tensor_tensor(prod[:], tiles[:].unsqueeze(1).to_broadcast([P, E, E]), lower[:],
                                     ALU.mult))
                do(dve.tensor_reduce(first[:], prod[:], AX.X, ALU.add))
                do(dve.tensor_tensor(after[:], first[:], tiles[:], ALU.add))
                do(dve.tensor_tensor(cmp[:], tiota[:].unsqueeze(2).to_broadcast([P, NS, E]),
                                     after[:].unsqueeze(1).to_broadcast([P, NS, E]), ALU.is_ge))
                do(dve.tensor_reduce(te[:], cmp[:], AX.X, ALU.add))
                do(dve.tensor_scalar(te[:], te[:], float(E - 1), None, ALU.min))
                do(dve.tensor_copy(tile_expert[:], te[0:1, :]))
                do(dve.tensor_tensor(pos[:], run[:], tot, ALU.subtract))
                do(dve.tensor_tensor(pos[:], pos[:], ps_rank[:].rearrange("p (t e) -> p t e", e=E),
                                     ALU.add))
                do(dve.tensor_scalar(first[:], first[:], float(P), None, ALU.mult))
                do(dve.tensor_tensor(pos[:], pos[:], first[:].unsqueeze(1).to_broadcast([P, NT, E]),
                                     ALU.add))
                for c in range(2):
                    do(dve.tensor_tensor(hot[c][:], hot[c][:], pos[:], ALU.mult))
                    do(dve.tensor_reduce(slotf[:, :, c], hot[c][:], AX.X, ALU.add))
                do(dve.tensor_copy(slot[:], slotf[:]))


def experts(nc, X, slot, tile_expert, C, A, Z, Y):
    with ExitStack() as ctx:
        S = Held(nc, ctx, "m3")
        wgu = S.sb("wgu", [P, E, KT * 2 * I])
        wd = S.sb("wd", [I, E, D])
        R = 4
        z = [S.sb(f"z{r}", [P, D]) for r in range(R)]
        zT = [S.sb(f"zT{r}", [P, KT, P]) for r in range(2)]
        gact = [S.sb(f"gact{r}", [P, I]) for r in range(2)]
        hid = [S.sb(f"hid{r}", [P, I]) for r in range(2)]
        hidT = [S.sb(f"hidT{r}", [I, P]) for r in range(2)]
        y = [S.sb(f"y{r}", [P, D]) for r in range(R)]
        ps_zT = [S.ps(f"ps_zT{r}") for r in range(2)]
        ps_gu = [S.ps(f"ps_gu{r}") for r in range(2)]
        ps_hT = [S.ps(f"ps_hT{r}") for r in range(2)]
        ps_y = [S.ps(f"ps_y{r}") for r in range(2)]
        s_w, s_scatter = S.sem("w"), S.sem("scatter")
        s_z, s_out = [S.sem(f"z{r}") for r in range(R)], [S.sem(f"out{r}", True) for r in range(R)]
        s_zT, s_yc = S.sem("zT", True), S.sem("yc", True)
        s_zTc, s_gu, s_silu, s_hid, s_hT, s_hTc, s_y, s_pass, s_pass_act = (
            S.sem(n) for n in ("zTc", "gu", "silu", "hid", "hT", "hTc", "y", "pass", "pass_act"))
        with nc.Block() as blk:
            @blk.gpsimd
            def _(pool):
                for t in range(NT):
                    for c in range(2):
                        pool.indirect_dma_start(
                            Z, bass.IndirectOffsetOnAxis(slot[:, t, c:c + 1], 0), X[:, t, :], None
                        ).then_inc(s_scatter, 16)
                need(pool, s_scatter, 16 * 2 * NT)

            @blk.sync
            def _(sp):
                wgu_v = wgu[:].rearrange("p e (k c i) -> p e k c i", k=KT, c=2)
                for e in range(E):
                    sp.dma_start(wgu_v[:, e, :, 0, :], A["ewg"][e].rearrange("(k p) i -> p k i", p=P)
                                 ).then_inc(s_w, 16)
                    sp.dma_start(wgu_v[:, e, :, 1, :], A["ewu"][e].rearrange("(k p) i -> p k i", p=P)
                                 ).then_inc(s_w, 16)
                sp.dma_start(wd[:], A["ewd"].rearrange("e i d -> i e d")).then_inc(s_w, 16)
                need(sp, s_scatter, 16 * 2 * NT)
                with sp.Fori(0, NS // R) as q:
                    for r in range(R):
                        hold(sp, s_zT, q * R, s_pass)
                        sp.dma_start(z[r][:], Z[bass.ds(q * (R * P) + r * P, P), :]).then_inc(s_z[r], 16)

            @blk.tensor
            def _(pe):
                def up(n, r):
                    j = r % 2
                    expert = pe.value_load(tile_expert[0:1, bass.ds(n, 1)], min_val=0, max_val=E - 1)
                    need(pe, s_zTc, n + 1)
                    for k in range(KT):
                        last = pe.matmul(ps_gu[j][:, 0:2 * I], zT[j][:, k, :],
                                         wgu[:, bass.ds(expert, 1), 2 * I * k:2 * I * (k + 1)],
                                         start=k == 0, stop=k == KT - 1)
                    last.then_inc(s_gu, 1)
                    return expert

                start_at_one(pe, s_zT)
                need(pe, s_w, 16 * (2 * E + 1))
                with pe.Fori(0, NS // R) as q:
                    for r in range(R):
                        n, j = q * R + r, r % 2
                        need(pe, s_z[r], q * 16 + 16)
                        for k in range(KT):
                            last = pe.transpose(ps_zT[j][:, P * k:P * (k + 1)],
                                                z[r][:, P * k:P * (k + 1)], C.ident[:])
                        last.then_inc(s_zT, 1)
                        expert = up(n, r)
                        need(pe, s_hid, n + 1)
                        pe.transpose(ps_hT[j][:, 0:P], hid[j][:], C.ident[:]).then_inc(s_hT, 1)
                        need(pe, s_hTc, n + 1)
                        need(pe, s_yc, q * R + (r - 1) if r else q * R)
                        pe.matmul(ps_y[j][:, 0:D], hidT[j][:], wd[:, bass.ds(expert, 1), :],
                                  start=True, stop=True).then_inc(s_y, 1)

            @blk.scalar
            def _(act):
                start_at_one(act, s_yc, *s_out)
                with act.Fori(0, NS // R) as q:
                    for r in range(R):
                        n, j = q * R + r, r % 2
                        need(act, s_zT, n + 1)
                        act.activation(zT[j][:], ps_zT[j][:, 0:D].rearrange("p (k t) -> p k t", k=KT),
                                       ACT.Copy).then_inc(s_zTc, 1)
                        need(act, s_gu, n + 1)
                        act.activation(gact[j][:], ps_gu[j][:, 0:I], ACT.Silu).then_inc(s_silu, 1)
                        need(act, s_y, n + 1)
                        hold(act, s_out[r], q * 16, s_pass_act)
                        act.activation(y[r][:], ps_y[j][:, 0:D], ACT.Copy).then_inc(s_yc, 1)
                        need(act, s_yc, n + 1)
                        act.dma_start(Y[bass.ds(q * (R * P) + r * P, P), :], y[r][:]
                                      ).then_inc(s_out[r], 16)
                for r in range(R):
                    need(act, s_out[r], NS // R * 16)

            @blk.vector
            def _(dve):
                with dve.Fori(0, NS // R) as q:
                    for r in range(R):
                        n, j = q * R + r, r % 2
                        need(dve, s_silu, n + 1)
                        dve.tensor_tensor(hid[j][:], gact[j][:], ps_gu[j][:, I:2 * I], ALU.mult
                                          ).then_inc(s_hid, 1)
                        need(dve, s_hT, n + 1)
                        dve.tensor_copy(hidT[j][:], ps_hT[j][:, 0:P]).then_inc(s_hTc, 1)


def combine(nc, X, base, slot, weight, C, Y):
    with ExitStack() as ctx:
        S = Held(nc, ctx, "m4")
        R = 3
        g = [S.sb(f"g{r}", [P, 2, GT, D]) for r in range(R)]
        ln = LayerNorm(S, C, X, NT)
        s_g = [S.sem(f"g{r}") for r in range(R)]
        s_mix = S.sem("mix")
        with nc.Block() as blk:
            @blk.gpsimd
            def _(pool):
                for q in range(NG):
                    if q >= R:
                        need(pool, s_mix, 2 * GT * (q - R + 1))
                    for t in range(GT):
                        for c in range(2):
                            pool.indirect_dma_start(
                                g[q % R][:, c, t, :], None, Y,
                                bass.IndirectOffsetOnAxis(slot[:, q * GT + t, c:c + 1], 0)
                            ).then_inc(s_g[q % R], 16)
                ln.root(pool, 0)

            @blk.vector
            def _(dve):
                start_at_one(dve, ln.s_x)
                for q in range(NG):
                    need(dve, s_g[q % R], 16 * 2 * GT * (q // R + 1))
                    for t in range(GT):
                        n = q * GT + t
                        for c in range(2):
                            dve.scalar_tensor_tensor(base[:, n, :], g[q % R][:, c, t, :],
                                                     weight[:, n, c:c + 1], base[:, n, :], ALU.mult,
                                                     ALU.add).then_inc(s_mix, 1)
                            need(dve, s_mix, 2 * n + c + 1)
                        dve.bn_stats(ln.stats[:, n, :], base[:, n, :]).then_inc(ln.s_stat, 1)
                        need(dve, ln.s_stat, n + 1)
                        dve.bn_aggr(ln.mv[:, n, :], ln.stats[:, n, :]).then_inc(ln.s_mv, 1)
                need(dve, ln.s_rstd, 1)
                for n in range(NT):
                    dve.tensor_scalar(X[:, n, :], base[:, n, :], ln.mv[:, n, 0:1], ln.rstd[:, n:n + 1],
                                      ALU.subtract, ALU.mult).then_inc(ln.s_x, 1)
                need(dve, ln.s_x, NT)


def layer0_experts(nc, X, C, A):
    Z, Y = nc.dram_tensor("slot_in", (SLOTS, D), F32).ap(), nc.dram_tensor("slot_out", (SLOTS, D), F32).ap()
    with ExitStack() as ctx:
        S = Held(nc, ctx, "m")
        base = S.sb("base", [P, NT, D])
        logits = S.sb("logits", [P, NT, E])
        slot = S.sb("slot", [P, NT, 2], U32)
        weight = S.sb("weight", [P, NT, 2])
        tile_expert = S.sb("tile_expert", [1, NS], U32)
        shared_expert(nc, X, base, logits, C, A, Z)
        route(nc, logits, slot, weight, tile_expert, C, A)
        experts(nc, X, slot, tile_expert, C, A, Z, Y)
        combine(nc, X, base, slot, weight, C, Y)


HH = 8
HV = 32
QUAD = 4


def layer1_attention(nc, X, C, A):
    SQ, SK, SV, SG = range(4)
    bounce = nc.dram_tensor("bounce", (2, 4, P, L), F32).ap()
    with ExitStack() as ctx:
        S = Held(nc, ctx, "a1")
        w = S.sb("w", [P, 4, P])
        qk_norm = S.sb("qk_norm", [P, 2])
        mean8 = S.sb("mean8", [P, HH])
        with ExitStack() as pctx:
            W = Held(nc, pctx, "a1w")
            wdq, wuqT = W.sb("wdq", [P, P]), W.sb("wuqT", [P, P])
            wdkv, wukT, wuvT = W.sb("wdkv", [P, 2, P]), W.sb("wukT", [P, 2, P]), W.sb("wuvT", [P, 2, HD])
            wkr, wqr = W.sb("wkr", [64, P]), W.sb("wqr", [64, P])
            woT, vc, block = W.sb("woT", [HD, P]), W.sb("vc", [HD, P]), W.sb("block", [P, P])
            ps = [W.ps(f"ps{i}") for i in range(5)]
            s_w, s_p, s_c, s_v = W.sem("w"), W.sem("p"), W.sem("c"), W.sem("v")
            with nc.Block() as blk:
                @blk.sync
                def _(sp):
                    loads = [(wdq[:], A["wdq"]), (wuqT[:], A["wuqT"]),
                             (wdkv[:], A["wdkv"].rearrange("(c p) d -> p c d", p=P)),
                             (wukT[:], A["wukT"].rearrange("(c p) d -> p c d", p=P)),
                             (wuvT[:], A["wuvT"].rearrange("(c p) d -> p c d", p=P)),
                             (wkr[:], A["wkr"]), (wqr[:], A["wqr"]), (woT[:], A["woT"]),
                             (block[:], A["block"]), (qk_norm[:], A["qk_norm"]), (mean8[:], A["mean8"])]
                    for dst, src in loads:
                        sp.dma_start(dst, src).then_inc(s_w, 16)
                    need(sp, s_w, 16 * len(loads))

                @blk.tensor
                def _(pe):
                    need(pe, s_w, 16 * 11)
                    pe.matmul(ps[0][:, 0:P], wdq[:], wuqT[:], start=True, stop=True).then_inc(s_p, 1)
                    for c in range(2):
                        last = pe.matmul(ps[1][:, 0:P], wdkv[:, c, :], wukT[:, c, :], start=c == 0, stop=c == 1)
                    last.then_inc(s_p, 1)
                    pe.matmul(ps[2][:, 0:P], wkr[:], wqr[:], start=True, stop=True).then_inc(s_p, 1)
                    for c in range(2):
                        last = pe.matmul(ps[3][0:HD, 0:P], wuvT[:, c, :], wdkv[:, c, :], start=c == 0, stop=c == 1)
                    last.then_inc(s_p, 1)
                    need(pe, s_v, 1)
                    pe.matmul(ps[4][:, 0:P], vc[:], woT[:], start=True, stop=True).then_inc(s_p, 1)

                @blk.vector
                def _(dve):
                    need(dve, s_w, 16 * 11)
                    dve.tensor_scalar(qk_norm[:, 0:1], qk_norm[:, 0:1], HD ** -0.5, None, ALU.mult
                                      ).then_inc(s_c, 1)
                    for n, (bank, to) in enumerate(((0, SQ), (1, SK), (2, SG))):
                        need(dve, s_p, n + 1)
                        dve.tensor_tensor(w[:, to, :], ps[bank][:, 0:P], block[:], ALU.mult).then_inc(s_c, 1)
                    need(dve, s_p, 4)
                    dve.tensor_copy(vc[:], ps[3][0:HD, 0:P]).then_inc(s_v, 1)
                    need(dve, s_p, 5)
                    dve.tensor_tensor(w[:, SV, :], ps[4][:, 0:P], block[:], ALU.mult).then_inc(s_c, 1)

        sm = Softmax(S, C, 2 * QUAD)
        tok = S.sb("tok", [P, TT, D])
        xs = [S.sb(f"xs{k}", [P, L]) for k in range(KT)]
        raw = S.sb("raw", [P, 2, L])
        sq = S.sb("sq", [P, 2, L])
        ms = S.sb("ms", [P, 2, TT, HH])
        roots = S.sb("roots", [P, 2, TT, P])
        fin = sq
        words = [S.sb(f"words{m}", [P, L], R32) for m in range(4)]
        QS = [S.sb(f"qs{k}", [P, HH, L], R32) for k in range(KT)]
        KS = [S.sb(f"ks{k}", [P, HH, L], R32) for k in range(KT)]
        V = [S.sb(f"v{k}", [P, TT, HH, HV]) for k in range(KT)]
        yq = S.sb("yq", [P, L])
        ln = LayerNorm(S, C, X, TT)
        ps_a, ps_b, ps_y = S.ps("ps_a"), S.ps("ps_b"), S.ps("ps_y")
        s_tok, s_turn, s_xs, s_zero = S.sem("tok"), S.sem("turn"), S.sem("xs"), S.sem("zero")
        s_v, s_vc, s_raw, s_sq, s_rawc = S.sem("v"), S.sem("vc"), S.sem("raw"), S.sem("sq"), S.sem("rawc")
        s_ms, s_msc, s_root, s_g, s_bc, s_fin = (S.sem(n) for n in ("ms", "msc", "root", "g", "bc", "fin"))
        s_kn, s_hi, s_lo, s_wr, s_rd = (S.sem(n) for n in ("kn", "hi", "lo", "wr", "rd"))
        s_wrs = [S.sem("wr0"), S.sem("wr1")]
        s_rds = [S.sem("rd0"), S.sem("rd1")]
        s_y, s_yc, s_yt = S.sem("y", True), S.sem("yc"), S.sem("yt")
        s_pass_sp, s_pass_pool = S.sem("pass_sp"), S.sem("pass_pool")

        def walk(eng, front, values, slot, finish):
            for step in range(8):
                front(0, 0, step)
            for step in range(4):
                front(0, 1, step)
                if step == 0:
                    values(0, 0, False)

            def both(b, h, more=True):
                slot(b, h)
                if h < 4:
                    front(b, 1, h + 4)
                elif h < 12 and more:
                    front(b + 1, 0, h - 4)
                elif h < H and more:
                    front(b + 1, 1, h - 12)
                if h == 4:
                    values(b, 1, not more)
                elif h == 12 and more:
                    values(b + 1, 0, False)

            both(0, 0)
            both(0, 1)
            with eng.Fori(0, B - 1) as b:
                for h in range(2, H):
                    both(b, h)
                for h in range(2):
                    both(b + 1, h)
                    slot(b, H + h)
                finish(b)
            for h in range(2, H):
                both(B - 1, h, False)
            slot(B - 1, H)
            slot(B - 1, H + 1)
            finish(B - 1)

        def nothing(*_):
            pass

        with nc.Block() as blk:
            @blk.sync
            def _(sp):
                def front(b, k, step):
                    if step != 7:
                        return
                    f = b * 2 + k
                    for m, when in ((0, s_hi), (1, s_lo), (2, s_hi), (3, s_lo)):
                        hold(sp, when, f * 2 + m // 2 + 1, s_pass_sp)
                        sp.dma_start(bounce[k, m], words[m][:].bitcast(F32)).then_inc(s_wrs[k], 16)
                    hold(sp, s_wrs[k], b * 64 + 64, s_pass_sp)
                    for c in range(4):
                        rows = slice(HD * c, HD * (c + 1))
                        for buf, m in ((QS[k], c % 2), (KS[k], 2 + c // 2)):
                            sp.dma_start(buf[rows, :, :].bitcast(F32),
                                         bounce[k, m].rearrange("(h d) t -> d h t", d=HD)
                                         ).then_inc(s_rds[k], 16)

                walk(sp, front, nothing, nothing, nothing)

            @blk.gpsimd
            def _(pool):
                cleared = [buf[4 * HD:P, :, :].bitcast(F32) for buf in QS + KS] + [v[:] for v in V]
                for n, at in enumerate(cleared):
                    pool.memset(at, 0.0).then_inc(s_zero, 1)
                    need(pool, s_zero, n + 1)

                def front(b, k, step):
                    f = b * 2 + k
                    if step == 0 and k == 0:
                        if not isinstance(b, int):
                            hold(pool, s_turn, f, s_pass_pool)
                        pool.tensor_copy(tok[:], X[:, bass.ds(b * TT, TT), :]).then_inc(s_tok, 1)
                    if step == 3:
                        hold(pool, s_msc, f + 1, s_pass_pool)
                        at = ms[:].rearrange("p a t h -> p (a t h)")
                        pool.tensor_tensor(at, at, C.minus_half[:, 0:2 * TT * HH], ALU.pow
                                           ).then_inc(s_root, 1)
                        hold(pool, s_root, f * 2 + 1, s_pass_pool)
                        if not (isinstance(b, int) and b == 0 and k == 0):
                            hold(pool, s_bc, f * 2, s_pass_pool)
                        pool.tensor_copy(roots[:].rearrange("p a t (h d) -> p (a t) h d", d=HD),
                                         ms[:].rearrange("p a t h -> p (a t) h").unsqueeze(3)
                                         .to_broadcast([P, 2 * TT, HH, HD])).then_inc(s_root, 1)

                def finish(b):
                    ln.root(pool, b)

                walk(pool, front, nothing, nothing, finish)

            @blk.tensor
            def _(pe):
                def front(b, k, step):
                    f = b * 2 + k
                    if step == 0:
                        need(pe, s_tok, b + 1)
                        need(pe, s_fin, f * 2)
                        for t in range(TT):
                            last = pe.transpose(ps_a[:, P * t:P * (t + 1)], tok[:, t, P * k:P * (k + 1)],
                                                C.ident[:])
                        last.then_inc(s_turn, 1)
                    elif step == 1:
                        need(pe, s_xs, f + 1)
                        need(pe, s_kn, f * 2)
                        pe.matmul(ps_b[:], w[:, SQ, :], xs[k][:], start=True, stop=True).then_inc(s_raw, 1)
                    elif step == 2:
                        need(pe, s_sq, f * 2 + 1)
                        need(pe, s_rawc, f * 2 + 1)
                        pe.matmul(ps_b[:], w[:, SK, :], xs[k][:], start=True, stop=True).then_inc(s_raw, 1)
                        if isinstance(b, int) and f == 0:
                            need(pe, s_xs, 1)
                        else:
                            need(pe, s_vc, f)
                        need(pe, s_sq, f * 2 + 2)
                        for a in range(2):
                            for t in range(TT):
                                col = (a * TT + t) * HH
                                last = pe.matmul(ps_a[:, col:col + HH], sq[:, a, P * t:P * (t + 1)],
                                                 mean8[:], start=True, stop=True)
                        last.then_inc(s_ms, 1)
                    elif step == 3:
                        need(pe, s_rawc, f * 2 + 2)
                        pe.matmul(ps_b[:], w[:, SG, :], xs[k][:], start=True, stop=True).then_inc(s_g, 1)
                    elif step in (6, 7):
                        a = step - 6
                        need(pe, s_root, f * 2 + 2)
                        if a:
                            need(pe, s_fin, f * 2 + 1)
                        for t in range(TT):
                            last = pe.matmul(ps_a[:, P * t:P * (t + 1)],
                                             roots[:, a, t, :],
                                             C.ident[:], start=True, stop=True)
                        last.then_inc(s_bc, 1)

                def values(b, k, last_one):
                    f = b * 2 + k
                    if last_one:
                        need(pe, s_fin, f * 2 + 2)
                    else:
                        need(pe, s_xs, f + 2)
                    for t in range(TT):
                        last = pe.matmul(ps_a[:, P * t:P * (t + 1)], xs[k][:, P * t:P * (t + 1)],
                                         w[:, SV, :], start=True, stop=True)
                    last.then_inc(s_v, 1)

                def slot(b, h):
                    if h < H:
                        k, j = h // HH, h % HH
                        if j == 0:
                            need(pe, s_rds[k], b * 128 + 128)
                            if isinstance(b, int) and b == 0:
                                need(pe, s_zero, 6)

                        def product(out, i, keys):
                            return pe.matmul(out, QS[k][:, j, P * i:P * (i + 1)], KS[k][:, j, 0:keys],
                                             start=True, stop=True)

                        sm.scores(pe, b * H + h, h, product)
                    if h >= 6 and h % QUAD == 2:
                        attend(b, (h - 6) // QUAD)
                    if h >= 2:
                        sm.transposes(pe, b * H + h - 2, (h - 2) % H)
                    if h >= 7 and h % QUAD == 3:
                        turn_back(b, (h - 7) // QUAD)

                def attend(b, u):
                    sm.need_probT(pe, b * H + QUAD * (u + 1) - 1)
                    need(pe, ln.s_sum, b * TT + u)
                    k = u // 2
                    for t in range(TT):
                        for j in range(QUAD):
                            h = QUAD * u + j
                            n = TCOL[t]
                            last = pe.matmul(ps_y[HV * j:HV * (j + 1), P * t:L], V[k][:, t, h % HH, :],
                                             sm.probT[:, h % (2 * QUAD), n:n + L - P * t],
                                             start=t == 0, stop=t == TT - 1)
                    last.then_inc(s_y, 1)

                def turn_back(b, u):
                    need(pe, s_yc, b * (H // QUAD) + u + 1)
                    for t in range(TT):
                        last = pe.transpose(ps_y[:, P * t:P * (t + 1)], yq[:, P * t:P * (t + 1)],
                                            C.ident[:])
                    last.then_inc(s_yt, 1)

                def finish(b):
                    attend(b, 3)
                    turn_back(b, 3)

                start_at_one(pe, s_y)
                walk(pe, front, values, slot, finish)

            @blk.scalar
            def _(act):
                def front(b, k, step):
                    f = b * 2 + k
                    if step == 0:
                        need(act, s_turn, f + 1)
                        need(act, s_g, f - 1)
                        need(act, s_v, f - 1)
                        act.activation(xs[k][:], ps_a[:], ACT.Copy).then_inc(s_xs, 1)
                    elif step in (1, 2):
                        a = step - 1
                        need(act, s_raw, f * 2 + a + 1)
                        need(act, s_lo, f * 2)
                        act.activation(sq[:, a, :], ps_b[:], ACT.Square).then_inc(s_sq, 1)
                    elif step in (6, 7):
                        a = step - 6
                        need(act, s_fin, f * 2 + 1 if a == 0 else f * 2 + 2)
                        if a:
                            need(act, s_kn, f * 2 + 2)
                        if not (isinstance(b, int) and b == 0 and k == 0):
                            need(act, s_wrs[1 - k], b * 64 if k == 0 else b * 64 + 64)
                        act.activation(words[2 * a][:], fin[:, a, :], ACT.Copy).then_inc(s_hi, 1)

                def values(b, k, _):
                    need(act, s_v, b * 2 + k + 1)
                    need(act, s_y, b * (H // QUAD) - 4 + 2 * k + 2)
                    if isinstance(b, int):
                        need(act, s_zero, 6)
                    act.activation(V[k][:, :, :, 0:HD],
                                   ps_a[:].rearrange("p (t h d) -> p t h d", t=TT, h=HH),
                                   ACT.Copy).then_inc(s_vc, 1)

                def slot(b, h):
                    if h < H:
                        sm.exps(act, b * H + h, h)
                    if h >= 2:
                        sm.copy_group(act, b * H + h - 2, (h - 2) % H, 0)
                        sm.copy_group(act, b * H + h - 2, (h - 2) % H, 2)
                    if h >= 6 and h % QUAD == 2:
                        outputs(b, (h - 6) // QUAD)

                def outputs(b, u):
                    need(act, s_y, b * (H // QUAD) + u + 1)
                    act.activation(yq[:], ps_y[:], ACT.Copy).then_inc(s_yc, 1)

                def finish(b):
                    outputs(b, 3)

                start_at_one(act, sm.s_pt_act)
                walk(act, front, values, slot, finish)

            @blk.vector
            def _(dve):
                def front(b, k, step):
                    f = b * 2 + k
                    if step in (1, 2):
                        a = step - 1
                        need(dve, s_raw, f * 2 + a + 1)
                        need(dve, s_sq, f * 2 + a + 1)
                        dve.tensor_copy(raw[:, a, :], ps_b[:]).then_inc(s_rawc, 1)
                        if a:
                            need(dve, s_ms, f + 1)
                            dve.tensor_scalar(ms[:].rearrange("p a t h -> p (a t h)"),
                                              ps_a[:, 0:2 * TT * HH], RMS_EPS, None, ALU.add
                                              ).then_inc(s_msc, 1)
                    elif step in (6, 7):
                        a = step - 6
                        need(dve, s_bc, f * 2 + a + 1)
                        dve.scalar_tensor_tensor(fin[:, a, :], raw[:, a, :], qk_norm[:, a:a + 1],
                                                 ps_a[:], ALU.mult, ALU.mult).then_inc(s_fin, 1)
                        if a:
                            need(dve, s_fin, f * 2 + 2)
                            need(dve, s_g, f + 1)
                            dve.tensor_tensor(fin[:, 1, :], fin[:, 1, :], ps_b[:], ALU.add
                                              ).then_inc(s_kn, 2)
                        need(dve, s_hi, f * 2 + a + 1)
                        dve.tensor_tensor(words[2 * a + 1][:], fin[:, a, :],
                                          words[2 * a][:].bitcast(F32), ALU.subtract).then_inc(s_lo, 1)

                def slot(b, h):
                    if h < H:
                        sm.mask_max(dve, b * H + h, h)
                    if h >= 2:
                        sm.copy_group(dve, b * H + h - 2, (h - 2) % H, 1)
                    if 1 <= h <= H:
                        sm.normalise(dve, b * H + h - 1, h - 1)
                    if h >= 7 and h % QUAD == 3:
                        residual(b, (h - 7) // QUAD)

                def residual(b, u):
                    if u == 0:
                        need(dve, ln.s_x, b * TT)
                    need(dve, s_yt, b * (H // QUAD) + u + 1)
                    cols = slice(QUAD * HD * u, QUAD * HD * (u + 1))
                    dve.tensor_tensor(
                        ln.res[:, :, cols].rearrange("p t (j d) -> p t j d", d=HD),
                        X[:, bass.ds(b * TT, TT), cols].rearrange("p t (j d) -> p t j d", d=HD),
                        ps_y[:].rearrange("p (t j d) -> p t j d", t=TT, j=QUAD)[:, :, :, 0:HD],
                        ALU.add).then_inc(ln.s_sum, 1)

                def finish(b):
                    residual(b, 3)
                    need(dve, ln.s_sum, b * TT + TT)
                    for t in range(TT):
                        ln.statistics(dve, b, t)
                    ln.write(dve, b)

                start_at_one(dve, ln.s_sum, ln.s_x, sm.s_pt_dve)
                walk(dve, front, nothing, slot, finish)


def layer1_ffn(nc, X, C, A):
    STEPS, BETA, THRESHOLD = 5, 0.9, 1.0
    with ExitStack() as ctx:
        S = Held(nc, ctx, "f1")
        F = Features(S, C, X)
        wfc = S.sb("wfc", [P, KT, FF])
        wpj = S.sb("wpj", [P, NF, D])
        hid = [S.sb(f"hid{j}", [P, NF, GL]) for j in range(2)]
        pos = [S.sb(f"pos{j}", [P, GL]) for j in range(2)]
        cur = S.sb("cur", [P, GL])
        acc = S.sb("acc", [P, GL])
        mem, nxt = S.sb("mem", [P, GL]), S.sb("nxt", [P, GL])
        ln = LayerNorm(S, C, X, GT)
        ps_h = [S.ps(f"ps_h{j}") for j in range(2)]
        ps_y = [S.ps(f"ps_y{c}") for c in range(2)]
        s_w, s_h, s_pos, s_hid, s_y, s_cur = (S.sem(n) for n in ("w", "h", "pos", "hid", "y", "cur"))
        s_v, s_store = S.sem("v"), S.sem("store")
        V_STEPS = 3 * (STEPS - 1) + 1
        with nc.Block() as blk:
            @blk.sync
            def _(sp):
                sp.dma_start(wfc[:], A["wfcT"].rearrange("(k p) f -> p k f", p=P)).then_inc(s_w, 16)
                sp.dma_start(wpj[:], A["wpjT"].rearrange("(k p) d -> p k d", p=P)).then_inc(s_w, 16)
                out = A["out"].rearrange("b (t p) d -> p (b t) d", p=P)
                with sp.Fori(0, NG) as g:
                    hold(sp, ln.s_x, g * GT + GT, F.passed)
                    sp.dma_start(out[:, bass.ds(g * GT, GT), :], X[:, bass.ds(g * GT, GT), :]
                                 ).then_inc(s_store, 16)
                need(sp, s_store, 16 * NG)

            @blk.gpsimd
            def _(pool):
                F.fetch(pool, 0, 0)
                F.fetch(pool, 1, 1)
                with pool.Fori(1, NG // 2) as r:
                    for j in range(2):
                        ln.root(pool, r * 2 + j - 2)
                        F.fetch(pool, r * 2 + j, j)
                for g in range(NG - 2, NG):
                    ln.root(pool, g)

            @blk.tensor
            def _(pe):
                need(pe, s_w, 32)

                def up(g, j):
                    F.turn(pe, g, j)
                    need(pe, F.s_xs, g * KT + KT)
                    for f in range(NF):
                        need(pe, s_pos, g * NF + f - 1)
                        for k in range(KT):
                            last = pe.matmul(ps_h[f % 2][:], wfc[:, k, P * f:P * (f + 1)], F.xs[j][:, k, :],
                                             start=k == 0, stop=k == KT - 1)
                        last.then_inc(s_h, 1)

                def down(g, j):
                    need(pe, s_hid, g * NF + NF)
                    for t in range(GT):
                        if t % 2 == 0:
                            need(pe, s_cur, g * 2 + t // 2 - 1)
                        for f in range(NF):
                            last = pe.matmul(ps_y[t // 2][:, D * (t % 2):D * (t % 2 + 1)],
                                             hid[j][:, f, P * t:P * (t + 1)], wpj[:, f, :],
                                             start=f == 0, stop=f == NF - 1)
                        if t % 2:
                            last.then_inc(s_y, 1)

                up(0, 0)
                up(1, 1)
                down(0, 0)
                with pe.Fori(1, NG // 2) as r:
                    for j in range(2):
                        up(r * 2 + j, j)
                        down(r * 2 + j - 1, 1 - j)
                down(NG - 1, 1)

            @blk.scalar
            def _(act):
                def step(g, j):
                    if not isinstance(g, int) or g >= 2:
                        need(act, s_y, g * 2 - 2)
                    F.keep(act, g, j)
                    for f in range(NF):
                        need(act, s_h, g * NF + f + 1)
                        need(act, s_hid, g * NF + f - 1)
                        act.activation(pos[f % 2][:], ps_h[f % 2][:], ACT.Relu).then_inc(s_pos, 1)
                        need(act, s_pos, g * NF + f + 1)
                        act.activation(hid[j][:, f, :], pos[f % 2][:], ACT.Square).then_inc(s_hid, 1)

                step(0, 0)
                step(1, 1)
                with act.Fori(1, NG // 2) as r:
                    for j in range(2):
                        step(r * 2 + j, j)

            @blk.vector
            def _(dve):
                start_at_one(dve, ln.s_sum, ln.s_x)
                with dve.Fori(0, NG) as g:
                    for c in range(2):
                        n = g * 2 + c
                        need(dve, s_y, n + 1)
                        dve.tensor_copy(cur[:], ps_y[c][:]).then_inc(s_cur, 1)
                        need(dve, s_cur, n + 1)
                        base = n * V_STEPS
                        m = cur
                        dve.tensor_scalar(acc[:], cur[:], THRESHOLD, None, ALU.is_gt).then_inc(s_v, 1)
                        for i in range(STEPS - 1):
                            at = base + 3 * i + 1
                            dve.scalar_tensor_tensor(nxt[:], m[:], BETA, cur[:], ALU.mult, ALU.add
                                                     ).then_inc(s_v, 1)
                            need(dve, s_v, at + 1)
                            dve.scalar_tensor_tensor(mem[:], m[:], THRESHOLD, nxt[:], ALU.is_gt,
                                                     ALU.subtract, reverse1=True).then_inc(s_v, 1)
                            need(dve, s_v, at + 2)
                            dve.scalar_tensor_tensor(acc[:], mem[:], THRESHOLD, acc[:], ALU.is_gt,
                                                     ALU.add).then_inc(s_v, 1)
                            need(dve, s_v, at + 3)
                            m = mem
                        tiles = bass.ds(g * GT + 2 * c, 2)
                        if c == 0:
                            need(dve, ln.s_x, g * GT)
                        dve.scalar_tensor_tensor(ln.res[:, 2 * c:2 * c + 2, :].rearrange("p t d -> p (t d)"),
                                                 acc[:], 1.0 / STEPS,
                                                 X[:, tiles, :].rearrange("p t d -> p (t d)"), ALU.mult,
                                                 ALU.add).then_inc(ln.s_sum, 1)
                        need(dve, ln.s_sum, n + 1)
                        for t in range(2):
                            ln.statistics(dve, g, 2 * c + t)
                    ln.write(dve, g)


def build(nc, A):
    with ExitStack() as ctx:
        C = Held(nc, ctx, "c")
        X = C.sb("X", [P, NT, D])
        C.ident, C.mask = C.sb("ident", [P, P]), C.sb("mask", [P, L])
        C.minus_half = C.sb("minus_half", [P, 2 * TT * HH])
        s_const = C.sem("const")
        with nc.Block() as blk:
            @blk.sync
            def _(sp):
                sp.dma_start(C.ident[:], A["ident"]).then_inc(s_const, 16)
                sp.dma_start(C.mask[:], A["mask"]).then_inc(s_const, 16)
                sp.wait_ge(s_const, 32)

            @blk.gpsimd
            def _(pool):
                pool.memset(C.minus_half[:], -0.5)
        layer0_attention(nc, X, C, A)
        layer0_experts(nc, X, C, A)
        layer1_attention(nc, X, C, A)
        layer1_ffn(nc, X, C, A)


def shape_constants():
    f32 = np.float32
    after = np.arange(P)[None, :] > np.arange(P)[:, None]
    mask = np.zeros((P, L), f32)
    mask[:, L - P:] = np.where(after, f32(MASKED), f32(0))
    heads = np.kron(np.eye(HH), np.ones((HD, HD))).astype(f32)
    rows = lambda a: np.ascontiguousarray(np.broadcast_to(np.asarray(a, f32), (P,) + np.shape(a)))
    return {
        "ident": np.eye(P, dtype=f32), "mask": mask, "before": after.astype(f32),
        "iota": rows(np.arange(E)), "tiota": rows(np.arange(NS)), "thr": rows(P * np.arange(NT)),
        "lower": rows(np.tril(np.ones((E, E)), -1)), "block": heads,
        "mean8": np.ascontiguousarray(heads[:, ::HD] / f32(HD)),
    }


def laid_out(i):
    a0, f0, a1, f1 = "L0_attn_", "L0_ffn_", "L1_attn_", "L1_ffn_"
    eight = lambda a: np.tile(a, (1, HH))
    out = {
        "x": i[a0 + "x_bld"], "xT": i[a0 + "x_bld"].transpose(0, 2, 1),
        "wqT": i[a0 + "Wq"].transpose(2, 1, 0), "wkT": i[a0 + "Wk_up"].transpose(2, 1, 0),
        "wvT": i[a0 + "Wv_up"].transpose(2, 1, 0), "wo": i[a0 + "Wout"].transpose(1, 0, 2),
        "wdn": i[a0 + "Wkv_down"],
        "gate_w": i[f0 + "gate_w"], "gate_b": np.broadcast_to(i[f0 + "gate_b"], (P, E)),
        "swg": i[f0 + "shared_wg"], "swu": i[f0 + "shared_wu"], "swd": i[f0 + "shared_wd"],
        "ewg": i[f0 + "experts_wg"], "ewu": i[f0 + "experts_wu"], "ewd": i[f0 + "experts_wd"],
        "wdq": eight(i[a1 + "W_DQ"]), "wuqT": eight(i[a1 + "W_UQ"].T),
        "wdkv": eight(i[a1 + "W_DKV"]), "wukT": eight(i[a1 + "W_UKV"][:HD].T),
        "wuvT": i[a1 + "W_UKV"][HD:].T, "wkr": eight(i[a1 + "W_KR"]), "wqr": eight(i[a1 + "W_QR"]),
        "woT": eight(i[a1 + "W_O"].T),
        "qk_norm": np.stack([np.tile(i[a1 + "q_norm_w"], HH), np.tile(i[a1 + "k_norm_w"], HH)], 1),
        "wfcT": i[f1 + "W_fc"].T, "wpjT": i[f1 + "W_proj"].T,
    }
    return {k: np.ascontiguousarray(v) for k, v in out.items()}


def kernel(**inputs):
    from concourse import bacc
    from concourse.bass_utils import run_bass_kernel_spmd

    arrays = {**laid_out({k: np.asarray(v) for k, v in inputs.items()}), **shape_constants()}
    nc = bacc.Bacc("TRN2", target_bir_lowering=False, num_devices=1)
    A = {k: nc.dram_tensor(f"in_{k}", v.shape, mybir.dt.from_np(v.dtype), kind="ExternalInput").ap()
         for k, v in arrays.items()}
    A["out"] = nc.dram_tensor("out", (B, L, D), F32, kind="ExternalOutput").ap()
    build(nc, A)
    r = run_bass_kernel_spmd(nc, [{f"in_{k}": v for k, v in arrays.items()}], core_ids=[0])
    return r.results[0]["out"]
```

```python
from contextlib import ExitStack

import numpy as np
import concourse.bass as bass
from concourse import mybir
from concourse.alu_op_type import AluOpType as ALU

F32 = mybir.dt.float32
R32 = mybir.dt.float32r
U32 = mybir.dt.uint32
I32 = mybir.dt.int32
ACT = mybir.ActivationFunctionType
AX = mybir.AxisListType

P = 128
B, L, D = 8, 512, 256
KT = D // P
TT = L // P
NT = B * TT
H = 16
LD = 64
NPAIR = H // 2
E, I = 16, 128
NW = E + 1
HD = D // H
FF = 1024
NF = FF // P
LN_EPS = 1e-5
RMS_EPS = 1.1920929e-07
MASKED = -1.0e30

QOFF = [P * i * (i + 1) // 2 for i in range(TT + 1)]
TRI = QOFF[TT]
SGROUP = [[0, 1], [2], [3]]
SCOL = [0, P, 0, 0]
TGROUPS = [[0], [1, 3], [2]]
TCOL = {0: 0, 1: L, 3: L + 3 * P, 2: 2 * L}
TGCOL = [0, L, 2 * L]
TGLEN = [L, L, 2 * P]


class Held:

    def __init__(self, nc, ctx, stage):
        self.nc, self.ctx, self.stage, self.sems = nc, ctx, stage, []
        ctx.callback(self.clear)

    def clear(self):
        self.nc.clear_and_free_semaphores(self.sems)
        self.nc.all_engine_barrier()

    def sb(self, name, shape, dt=F32):
        return self.ctx.enter_context(self.nc.sbuf_tensor(f"{self.stage}_{name}", shape, dt))

    def ps(self, name):
        return self.ctx.enter_context(self.nc.psum_tensor(f"{self.stage}_{name}", [P, 512], F32))

    def sem(self, name, from1=False):
        self.sems.append(self.nc.alloc_semaphore(f"{self.stage}_{name}" + ("_from1" if from1 else "")))
        return self.sems[-1]


def start_at_one(eng, *sems):
    for s in sems:
        eng.sem_inc(s, 1)


def need(eng, sem, value):
    if not isinstance(value, int) or value > 0:
        eng.wait_ge(sem, value + 1 if sem.name.endswith("_from1") else value)


def hold(eng, sem, value, passed):
    need(eng, sem, value)
    eng.sem_inc(passed, 1)


class Softmax:

    def __init__(self, S, C, ring, normed):
        self.C, self.ring, self.normed = C, ring, normed
        self.prob = S.sb("prob", [P, 4, TRI])
        self.probT = S.sb("probT", [P, ring, TRI])
        self.negmax = S.sb("negmax", [P, 4, TT])
        self.rowsum, self.recip = (S.sb(n, [P, ring, TT]) for n in ("rowsum", "recip"))
        self.ps_score = [S.ps(f"ps_score{g}") for g in range(3)]
        self.ps_trans = [S.ps(f"ps_trans{g}") for g in range(2)]
        self.s_score, self.s_max, self.s_exp, self.s_recip, self.s_norm, self.s_trans, self.passed = (
            S.sem(n) for n in ("score", "max", "exp", "recip", "norm", "trans", "passed"))
        self.s_pt_act, self.s_pt_dve = S.sem("pt_act", True), S.sem("pt_dve", True)

    def scores(self, pe, n, h, product):
        for g, tiles in enumerate(SGROUP):
            need(pe, self.s_max, n * TT - TT + tiles[-1] + 1)
            for i in tiles:
                keys = P * (i + 1)
                at = SCOL[i]
                last = product(self.ps_score[g][:, at:at + keys], i, keys)
            last.then_inc(self.s_score, 1)

    def mask_max(self, dve, n, h):
        for g, tiles in enumerate(SGROUP):
            hold(dve, self.s_score, n * 3 + g + 1, self.passed)
            for i in tiles:
                keys = P * (i + 1)
                at = SCOL[i]
                dve.tensor_tensor_reduce(
                    out=self.prob[:, h % 4, QOFF[i]:QOFF[i] + keys],
                    in0=self.ps_score[g][:, at:at + keys], in1=self.C.mask[:, L - keys:L], scale=-1.0,
                    scalar=3.0e38, op0=ALU.add, op1=ALU.min,
                    accum_out=self.negmax[:, h % 4, i:i + 1]).then_inc(self.s_max, 1)

    def exps(self, act, n, h):
        for i in range(TT):
            need(act, self.s_max, n * TT + i + 1)
            at = self.prob[:, h % 4, QOFF[i]:QOFF[i + 1]]
            act.activation(at, at, ACT.Exp, scale=-1.0, bias=self.negmax[:, h % 4, i:i + 1],
                           accum_out=self.rowsum[:, h % self.ring, i:i + 1]).then_inc(self.s_exp, 1)

    def normalise(self, dve, n, h):
        need(dve, self.s_exp, n * TT + TT)
        r = h % self.ring
        dve.reciprocal(self.recip[:, r, :], self.rowsum[:, r, :]).then_inc(self.s_recip, 1)
        need(dve, self.s_recip, n + 1)
        for i in range(TT):
            at = self.prob[:, h % 4, QOFF[i]:QOFF[i + 1]]
            dve.tensor_scalar(at, at, self.recip[:, r, i:i + 1], None, ALU.mult
                              ).then_inc(self.s_norm, 1)

    def transposes(self, pe, n, h, groups):
        for g in groups:
            if g == 0:
                need(pe, self.s_norm if self.normed else self.s_exp, n * TT + TT)
            if g == 0:
                need(pe, self.s_pt_dve, n)
            elif g == 1:
                need(pe, self.s_pt_act, n * 2)
            else:
                need(pe, self.s_pt_act, n * 2 + 1)
            for k, i in [(k, i) for k in TGROUPS[g] for i in range(k, TT)]:
                col = TCOL[k] - TGCOL[g] + P * (i - k)
                last = pe.transpose(self.ps_trans[(3 * h + g) % 2][:, col:col + P],
                                    self.prob[:, h % 4, QOFF[i] + P * k:QOFF[i] + P * (k + 1)],
                                    self.C.ident[:])
            last.then_inc(self.s_trans, 1)

    def copy_group(self, eng, n, h, g):
        need(eng, self.s_trans, n * 3 + g + 1)
        out = self.probT[:, h % self.ring, TGCOL[g]:TGCOL[g] + TGLEN[g]]
        src = self.ps_trans[(3 * h + g) % 2][:, 0:TGLEN[g]]
        if g == 1:
            eng.tensor_copy(out, src).then_inc(self.s_pt_dve, 1)
        else:
            eng.activation(out, src, ACT.Copy).then_inc(self.s_pt_act, 1)

    def need_probT(self, pe, n):
        need(pe, self.s_pt_act, n * 2 + 2)
        need(pe, self.s_pt_dve, n + 1)


    def tensor_slot(self, pe, b, h, product, between):
        if 2 <= h < H + 2:
            self.transposes(pe, b * H + h - 2, h - 2, (0, 1))
        if h < H:
            self.scores(pe, b * H + h, h, product)
        between()
        if 2 <= h < H + 2:
            self.transposes(pe, b * H + h - 2, h - 2, (2,))

    def scalar_slot(self, act, b, h):
        if 2 <= h < H + 2:
            self.copy_group(act, b * H + h - 2, h - 2, 0)
        if 1 <= h <= H:
            self.exps(act, b * H + h - 1, h - 1)
        if 2 <= h < H + 2:
            self.copy_group(act, b * H + h - 2, h - 2, 2)

    def vector_slot(self, dve, b, h):
        if 2 <= h < H + 2:
            self.copy_group(dve, b * H + h - 2, h - 2, 1)
        if h < H:
            self.mask_max(dve, b * H + h, h)
        if self.normed and 1 <= h <= H:
            self.normalise(dve, b * H + h - 1, h - 1)


def over_batches(slot, eng, lag, ahead=1):

    def batch(b):
        for h in range(lag, H):
            slot(b, h)
        for h in range(lag):
            slot(b, H + h)
            slot(b + 1, h)

    for h in range(lag):
        slot(0, h)
    with eng.Fori(0, B - ahead) as b:
        batch(b)
    for b in range(B - ahead, B - 1):
        batch(b)
    for h in range(lag, H + lag):
        slot(B - 1, h)


def layer0_attention(nc, X, C, A, meanwhile=None):
    with ExitStack() as ctx:
        S = Held(nc, ctx, "a0")
        wqk = S.sb("wqk", [P, KT, H * LD])
        wvo = S.sb("wvo", [P, NPAIR, D])
        wdn2 = S.sb("wdn2", [P, KT, 2, LD])

        with ExitStack() as pctx:
            W = Held(nc, pctx, "a0w")
            wqT = W.sb("wqT", [LD, H, D])
            wkT = W.sb("wkT", [LD, H, LD])
            wvT = W.sb("wvT", [LD, H, LD])
            wo = W.sb("wo", [LD, H, D])
            s_load, s_qk, s_vo, s_cp = W.sem("load"), W.sem("qk"), W.sem("vo"), W.sem("cp")
            s_cv = W.sem("cv")
            pqk = [W.ps("pqk0"), W.ps("pqk1")]
            pvo = [W.ps("pvo0"), W.ps("pvo1")]
            with nc.Block() as blk:
                @blk.sync
                def _(sp):
                    for dst, src in ((wqT, A["wqT"]), (wkT, A["wkT"]), (wvT, A["wvT"]), (wo, A["wo"])):
                        sp.dma_start(dst[:], src).then_inc(s_load, 16)
                    for c in range(2):
                        sp.dma_start(wdn2[:, :, c, :], A["wdn"].rearrange("(k p) c -> p k c", p=P)
                                     ).then_inc(s_load, 16)
                    need(sp, s_load, 16 * 6)

                @blk.tensor
                def _(pe):
                    need(pe, s_load, 16 * 6)
                    for k in range(KT):
                        for half in range(2):
                            n = 2 * k + half
                            if n >= 2:
                                need(pe, s_cp, n - 1)
                            for h in range(8):
                                hh = 8 * half + h
                                ins = pe.matmul(pqk[n % 2][:, h * LD:(h + 1) * LD],
                                                wqT[:, hh, k * P:(k + 1) * P], wkT[:, hh, :],
                                                start=True, stop=True)
                            ins.then_inc(s_qk, 1)
                    for p in range(NPAIR):
                        if p >= 2:
                            need(pe, s_cv, p - 1)
                        for c in range(2):
                            ins = pe.matmul(pvo[p % 2][LD * c:LD * (c + 1), 0:D], wvT[:, 2 * p + c, :],
                                            wo[:, 2 * p + c, :], start=True, stop=True)
                        ins.then_inc(s_vo, 1)

                @blk.scalar
                def _(act):
                    for n in range(4):
                        need(act, s_qk, n + 1)
                        act.activation(wqk[:, n // 2, 512 * (n % 2):512 * (n % 2 + 1)], pqk[n % 2][:],
                                       ACT.Copy, scale=LD ** -0.5).then_inc(s_cp, 1)

                @blk.vector
                def _(dve):
                    for p in range(NPAIR):
                        need(dve, s_vo, p + 1)
                        dve.tensor_copy(wvo[:, p, :], pvo[p % 2][:, 0:D]).then_inc(s_cv, 1)

        sm = Softmax(S, C, 4, True)
        xT = S.sb("xT", [P, KT, L])
        xtok = S.sb("xtok", [P, TT, D])
        kh = S.sb("kh", [P, L], R32)
        kl = S.sb("kl", [P, L], R32)
        latv = S.sb("latv", [P, TT, LD])
        qs = S.sb("qs", [P, 2, 2, L], R32)
        qlow = S.sb("qlow", [P, 2, L], R32)
        yT = S.sb("yT", [P, NPAIR, L])
        ln = LayerNorm(S, C, X, TT)
        ps_q, ps_y, ps_kv = S.ps("ps_q"), S.ps("ps_y"), S.ps("ps_kv")
        ps_out = [ps_y, ps_kv]
        s_xT, s_xtok, s_qdma = S.sem("xT"), S.sem("xtok"), [S.sem("qdma0"), S.sem("qdma1")]
        s_lat, s_v, s_q, s_y, s_out = S.sem("lat"), S.sem("v"), S.sem("q"), S.sem("y"), S.sem("out", True)
        s_kh, s_latv, s_qhi, s_yc = S.sem("kh"), S.sem("latv"), S.sem("qhi"), S.sem("yc", True)
        s_kl, s_qlo = S.sem("kl"), S.sem("qlo")
        s_pass_sp = S.sem("pass_sp")
        LAG = 3

        with nc.Block() as blk:
            @blk.sync
            def _(sp):
                def load_x(b):
                    if not isinstance(b, int):
                        hold(sp, s_q, b * NPAIR, s_pass_sp)
                        hold(sp, s_v, b, s_pass_sp)
                    sp.dma_start(xT[:], A["xT"][bass.ds(b, 1), :, :].rearrange(
                        "o (k p) t -> p (o k) t", p=P)).then_inc(s_xT, 16)

                def load_tokens(b):
                    hold(sp, ln.s_sum, b * TT, s_pass_sp)
                    sp.dma_start(xtok[:], A["x"][bass.ds(b, 1), :, :].rearrange(
                        "o (t p) d -> p (o t) d", p=P)).then_inc(s_xtok, 16)

                def low_words(b, p):
                    hold(sp, s_qlo, b * (2 * NPAIR) + 2 * p + 2, s_pass_sp)
                    for c in range(2):
                        rows, to = slice(LD * c, LD * (c + 1)), slice(LD * (1 - c), LD * (2 - c))
                        sp.dma_start(qs[to, p % 2, c, :].bitcast(F32),
                                     qlow[rows, p % 2, :].bitcast(F32)).then_inc(s_qdma[p % 2], 16)

                def low_words_and_tokens(b):
                    for p in range(1, NPAIR):
                        low_words(b, p)
                        if p == 1:
                            load_tokens(b)

                load_x(0)
                low_words(0, 0)
                with sp.Fori(0, B - 1) as b:
                    low_words_and_tokens(b)
                    load_x(b + 1)
                    low_words(b + 1, 0)
                low_words_and_tokens(B - 1)

            @blk.tensor
            def _(pe):
                def project(b, p):
                    need(pe, s_qlo, b * (2 * NPAIR) + 2 * p)
                    for k in range(KT):
                        last = pe.matmul(ps_q[:], wqk[:, k, P * p:P * (p + 1)], xT[:, k, :],
                                         start=k == 0, stop=k == KT - 1)
                    last.then_inc(s_q, 1)

                def product(b, h, out, i, keys):
                    p = h // 2
                    if i == 0:
                        need(pe, s_qhi, b * (2 * NPAIR) + 2 * p + 2)
                        need(pe, s_qdma[p % 2], b * (16 * NPAIR) + 32 * (p // 2 + 1))
                        if h == 0:
                            need(pe, s_kl, b + 1)
                    q = qs[:, p % 2, h % 2, P * i:P * (i + 1)]
                    pe.matmul(out, q, kh[:, 0:keys], start=True, stop=False)
                    return pe.matmul(out, q, kl[:, 0:keys], start=False, stop=True)

                def attend(b, p):
                    sm.need_probT(pe, b * H + 2 * p + 1)
                    need(pe, s_yc, b * NPAIR + p)
                    if p == 0:
                        need(pe, s_latv, b + 1)
                        need(pe, ln.s_sum, b * TT)
                    for k in range(TT):
                        for c in range(2):
                            n = TCOL[k]
                            last = pe.matmul(ps_y[LD * c:LD * (c + 1), P * k:L], latv[:, k, :],
                                             sm.probT[:, (2 * p + c) % 4, n:n + L - P * k],
                                             start=k == 0, stop=k == TT - 1)
                    last.then_inc(s_y, 1)

                def values(b):
                    for t in range(TT):
                        for k in range(KT):
                            last = pe.matmul(ps_kv[:, LD * t:LD * (t + 1)], xT[:, k, P * t:P * (t + 1)],
                                             wdn2[:, k, 0, :], start=k == 0, stop=k == KT - 1)
                    last.then_inc(s_v, 1)

                def start(b):
                    need(pe, s_xT, b * 16 + 16)
                    need(pe, ln.s_sum, (b - 1) * TT)
                    for k in range(KT):
                        last = pe.matmul(ps_kv[:], wdn2[:, k, :, :], xT[:, k, :],
                                         start=k == 0, stop=k == KT - 1)
                    last.then_inc(s_lat, 1)
                    project(b, 0)
                    if isinstance(b, int):
                        need(pe, s_kl, b + 1)
                        values(b)

                def slot(b, h):
                    if h == 0:
                        start(b)
                    if h == H + 2:
                        finish(b)
                        return

                    def between():
                        if h % 2 == 0 and h + 2 < H:
                            project(b, h // 2 + 1)
                        if h >= 5 and h % 2:
                            attend(b, (h - 5) // 2)

                    sm.tensor_slot(pe, b, h, lambda *to: product(b, h, *to), between)

                def finish(b):
                    attend(b, NPAIR - 1)
                    if not isinstance(b, int):
                        values(b + 1)
                        need(pe, s_latv, b + 2)
                    need(pe, s_yc, b * NPAIR + NPAIR)
                    for t in range(TT):
                        if t >= 2:
                            need(pe, ln.s_sum, b * TT + t - 1)
                        for p in range(NPAIR):
                            last = pe.matmul(ps_out[t % 2][:, 0:D], yT[:, p, P * t:P * (t + 1)],
                                             wvo[:, p, :], start=p == 0, stop=p == NPAIR - 1)
                        last.then_inc(s_out, 1)

                start_at_one(pe, s_out)
                over_batches(slot, pe, LAG)

            @blk.scalar
            def _(act):
                def q_high(b, p):
                    need(act, s_q, b * NPAIR + p + 1)
                    act.activation(qs[0:LD, p % 2, 0, :], ps_q[0:LD, :], ACT.Copy).then_inc(s_qhi, 1)
                    act.activation(qs[LD:P, p % 2, 1, :], ps_q[LD:P, :], ACT.Copy).then_inc(s_qhi, 1)

                def values(b):
                    need(act, s_v, b + 1)
                    act.activation(latv[:], ps_kv[:, 0:TT * LD].rearrange("p (t c) -> p t c", t=TT),
                                   ACT.Copy).then_inc(s_latv, 1)

                def start(b):
                    need(act, s_lat, b + 1)
                    act.activation(kh[:], ps_kv[:], ACT.Copy).then_inc(s_kh, 1)
                    q_high(b, 0)
                    if isinstance(b, int):
                        values(b)

                def slot(b, h):
                    if h == 0:
                        start(b)
                    sm.scalar_slot(act, b, h)
                    if h % 2 == 0 and h + 2 < H:
                        q_high(b, h // 2 + 1)
                    if h >= 5 and h % 2:
                        outputs(b, (h - 5) // 2)
                    if h == H + 2:
                        finish(b)

                def outputs(b, p):
                    if p == 0:
                        need(act, s_out, b * TT)
                    need(act, s_y, b * NPAIR + p + 1)
                    act.activation(yT[:, p, :], ps_y[:], ACT.Copy).then_inc(s_yc, 1)

                def finish(b):
                    outputs(b, NPAIR - 1)
                    if not isinstance(b, int):
                        values(b + 1)

                start_at_one(act, sm.s_pt_act, s_yc)
                over_batches(slot, act, LAG)

            @blk.vector
            def _(dve):
                def q_low(b, p):
                    for c in range(2):
                        rows = slice(LD * c, LD * (c + 1))
                        need(dve, s_qhi, b * (2 * NPAIR) + 2 * p + c + 1)
                        dve.tensor_tensor(qlow[rows, p % 2, :], ps_q[rows, :],
                                          qs[rows, p % 2, c, :].bitcast(F32),
                                          ALU.subtract).then_inc(s_qlo, 1)

                def start(b):
                    need(dve, s_kh, b + 1)
                    dve.tensor_tensor(kl[:], ps_kv[:], kh[:].bitcast(F32), ALU.subtract
                                      ).then_inc(s_kl, 1)
                    q_low(b, 0)

                def slot(b, h):
                    if h == 0:
                        start(b)
                    sm.vector_slot(dve, b, h)
                    if h % 2 == 0 and h + 2 < H:
                        q_low(b, h // 2 + 1)
                    if h == H + 2:
                        finish(b)

                def finish(b):
                    need(dve, s_xtok, b * 16 + 16)
                    for t in range(TT):
                        need(dve, s_out, b * TT + t + 1)
                        ln.add(dve, b, t, ps_out[t % 2][:, 0:D], xtok[:, t, :])
                    ln.write(dve, b)

                start_at_one(dve, ln.s_sum, ln.s_x, sm.s_pt_dve)
                over_batches(slot, dve, LAG)

            @blk.gpsimd
            def _(pool):
                if meanwhile:
                    meanwhile(pool)
                with pool.Fori(0, B) as b:
                    ln.root(pool, b)


class LayerNorm:

    def __init__(self, S, C, X, n):
        self.C, self.X, self.n = C, X, n
        self.res = S.sb("res", [P, n, D])
        self.stats, self.mv, self.rstd = S.sb("stats", [P, n, 6]), S.sb("mv", [P, n, 2]), S.sb("rstd", [P, n])
        self.s_sum, self.s_x = S.sem("ln_sum", True), S.sem("ln_x", True)
        self.s_stat, self.s_mv, self.s_var, self.s_rstd, self.passed = (
            S.sem("ln_" + k) for k in ("stat", "mv", "var", "rstd", "pass"))
        self.passed_pool = S.sem("ln_pass_pool")

    def add(self, dve, b, t, u, v):
        if t == 0:
            need(dve, self.s_x, b * self.n)
        dve.tensor_tensor(self.res[:, t, :], u, v, ALU.add).then_inc(self.s_sum, 1)
        need(dve, self.s_sum, b * self.n + t + 1)
        self.statistics(dve, b, t)

    def statistics(self, dve, b, t):
        dve.bn_stats(self.stats[:, t, :], self.res[:, t, :]).then_inc(self.s_stat, 1)
        hold(dve, self.s_stat, b * self.n + t + 1, self.passed)
        dve.bn_aggr(self.mv[:, t, :], self.stats[:, t, :]).then_inc(self.s_mv, 1)

    def root(self, pool, b):
        hold(pool, self.s_mv, b * self.n + self.n, self.passed_pool)
        pool.tensor_scalar(self.rstd[:], self.mv[:, :, 1], LN_EPS, None, ALU.add).then_inc(self.s_var, 1)
        hold(pool, self.s_var, b + 1, self.passed_pool)
        pool.tensor_tensor(self.rstd[:], self.rstd[:], self.C.minus_half[:, 0:self.n],
                           ALU.pow).then_inc(self.s_rstd, 1)

    def write(self, dve, b):
        need(dve, self.s_rstd, b + 1)
        for t in range(self.n):
            dve.tensor_scalar(self.X[:, bass.ds(b * self.n + t, 1), :].rearrange("p o d -> p (o d)"),
                              self.res[:, t, :], self.mv[:, t, 0:1], self.rstd[:, t:t + 1],
                              ALU.subtract, ALU.mult).then_inc(self.s_x, 1)


NS = 80
SLOTS = NS * P
GT = 4
GL = GT * P
NG = NT // GT
NZ = 16


class Features:

    def __init__(self, S, C, X):
        self.C, self.X = C, X
        self.tok = [S.sb(f"tok{j}", [P, GT, D]) for j in range(2)]
        self.xs = [S.sb(f"xs{j}", [P, KT, GL]) for j in range(2)]
        self.ps = [S.ps(f"ps_turn{k}") for k in range(KT)]
        self.s_tok, self.s_turn, self.s_xs = S.sem("tok"), S.sem("turn"), S.sem("xs")
        self.passed = S.sem("tok_pass")

    def fetch(self, pool, g, j):
        if not isinstance(g, int) or g >= 2:
            hold(pool, self.s_turn, g * KT - KT, self.passed)
        pool.tensor_copy(self.tok[j][:], self.X[:, bass.ds(g * GT, GT), :]).then_inc(self.s_tok, 1)

    def turn(self, pe, g, j):
        need(pe, self.s_tok, g + 1)
        for k in range(KT):
            need(pe, self.s_xs, g * KT - KT + k + 1)
            for t in range(GT):
                last = pe.transpose(self.ps[k][:, P * t:P * (t + 1)],
                                    self.tok[j][:, t, P * k:P * (k + 1)], self.C.ident[:])
            last.then_inc(self.s_turn, 1)

    def keep(self, act, g, j):
        for k in range(KT):
            need(act, self.s_turn, g * KT + k + 1)
            act.activation(self.xs[j][:, k, :], self.ps[k][:], ACT.Copy).then_inc(self.s_xs, 1)


def in_twos(eng, n, step):
    step(0, 0)
    step(1, 1)
    with eng.Fori(1, n // 2) as r:
        for j in range(2):
            step(r * 2 + j, j)


class ExpertStore:

    def __init__(self, nc, ctx):
        S = Held(nc, ctx, "es")
        self.wgu = S.sb("wgu", [P, E, KT * 2 * I])
        self.wd = S.sb("wd", [I, E, D])
        self.zero = S.sb("zero", [P, D])
        self.s_w, self.s_z, self.s_zero = S.sem("w"), S.sem("z"), S.sem("zero")
        self.Z = nc.dram_tensor("slot_in", (SLOTS, D), F32).ap()
        self.Y = nc.dram_tensor("slot_out", (SLOTS, D), F32).ap()

    def start(self, pool, A):
        pool.memset(self.zero[:], 0.0).then_inc(self.s_zero, 1)
        wgu = self.wgu[:].rearrange("p e (k c i) -> p e k c i", k=KT, c=2)
        for c, src in enumerate(("ewg", "ewu")):
            for e in range(E):
                pool.dma_start(wgu[:, e, :, c, :], A[src][e].rearrange("(k p) i -> p k i", p=P)
                             ).then_inc(self.s_w, 16)
        pool.dma_start(self.wd[:], A["ewd"].rearrange("e i d -> i e d")).then_inc(self.s_w, 16)
        need(pool, self.s_zero, 1)
        for n in range(NZ):
            rows = self.Z[bass.ts(n, SLOTS // NZ), :].rearrange("(a p) d -> p a d", p=P)
            pool.dma_start(rows, self.zero[:].unsqueeze(1).to_broadcast([P, NS // NZ, D])
                         ).then_inc(self.s_z, 16)

    def ready(self, eng):
        need(eng, self.s_w, 16 * (2 * E + 1))
        need(eng, self.s_z, 16 * NZ)


def logits_of(nc, X, xs_all, logits, C, A):
    with ExitStack() as ctx:
        S = Held(nc, ctx, "m1")
        F = Features(S, C, X)
        gate = S.sb("gate", [P, KT, E])
        ps_gate = S.ps("ps_gate")
        s_w, s_gate, s_log, s_all = S.sem("w"), S.sem("gate"), S.sem("log"), S.sem("all")
        with nc.Block() as blk:
            @blk.sync
            def _(sp):
                sp.dma_start(gate[:], A["gate_w"].rearrange("(k p) e -> p k e", p=P)).then_inc(s_w, 16)

            @blk.tensor
            def _(pe):
                need(pe, s_w, 16)

                def step(g, j):
                    F.turn(pe, g, j)
                    need(pe, F.s_xs, g * KT + KT)
                    need(pe, s_log, g)
                    for t in range(GT):
                        for k in range(KT):
                            last = pe.matmul(ps_gate[:, E * t:E * (t + 1)],
                                             F.xs[j][:, k, P * t:P * (t + 1)], gate[:, k, :],
                                             start=k == 0, stop=k == KT - 1)
                    last.then_inc(s_gate, 1)

                in_twos(pe, NG, step)

            @blk.scalar
            def _(act):
                def step(g, j):
                    if not isinstance(g, int) or g >= 2:
                        need(act, s_gate, g - 1)
                        need(act, s_all, g - 1)
                    F.keep(act, g, j)
                    need(act, s_gate, g + 1)
                    act.activation(logits[:, bass.ds(g * GT, GT), :],
                                   ps_gate[:, 0:GT * E].rearrange("p (t e) -> p t e", e=E),
                                   ACT.Copy).then_inc(s_log, 1)

                in_twos(act, NG, step)

            @blk.vector
            def _(dve):
                F.fetch(dve, 0, 0)

                def step(g, j):
                    if not isinstance(g, int) or g < NG - 1:
                        F.fetch(dve, g + 1, 1 - j)
                    need(dve, F.s_xs, g * KT + KT)
                    dve.tensor_copy(xs_all[:, :, bass.ds(g * GL, GL)], F.xs[j][:]).then_inc(s_all, 1)

                step(0, 0)
                step(1, 1)
                with dve.Fori(1, NG // 2 - 1) as r:
                    for j in range(2):
                        step(r * 2 + j, j)
                step(NG - 2, 0)
                step(NG - 1, 1)


def shared_expert(nc, X, xs_all, base, slot, ES, A):
    with ExitStack() as ctx:
        S = Held(nc, ctx, "m2")
        wgu = S.sb("wgu", [P, KT, 2, I])
        wd = S.sb("wd", [I, D])
        act_g = [S.sb(f"act{j}", [I, GL]) for j in range(2)]
        hid = [S.sb(f"hid{j}", [I, GL]) for j in range(2)]
        ps_g, ps_u = ([S.ps(f"{n}{j}") for j in range(2)] for n in ("ps_g", "ps_u"))
        ps_d = [S.ps("ps_d0"), S.ps("ps_d1")]
        s_w, s_scatter, s_gu, s_down = S.sem("w"), S.sem("scatter"), S.sem("gu"), S.sem("down")
        s_silu, s_hid, s_base = S.sem("silu"), S.sem("hid"), S.sem("base")
        with nc.Block() as blk:
            @blk.sync
            def _(sp):
                sp.dma_start(wgu[:, :, 0, :], A["swg"].rearrange("(k p) i -> p k i", p=P)).then_inc(s_w, 16)
                sp.dma_start(wgu[:, :, 1, :], A["swu"].rearrange("(k p) i -> p k i", p=P)).then_inc(s_w, 16)
                sp.dma_start(wd[:], A["swd"]).then_inc(s_w, 16)

            @blk.gpsimd
            def _(pool):
                ES.ready(pool)
                for t in range(NT):
                    for c in range(2):
                        pool.indirect_dma_start(
                            ES.Z, bass.IndirectOffsetOnAxis(slot[:, t, c:c + 1], 0), X[:, t, :], None
                        ).then_inc(s_scatter, 16)
                need(pool, s_scatter, 16 * 2 * NT)

            @blk.tensor
            def _(pe):
                need(pe, s_w, 16 * 3)

                def up(g, j):
                    if not isinstance(g, int) or g >= 2:
                        need(pe, s_hid, g - 1)
                    for c, ps in enumerate((ps_g[j], ps_u[j])):
                        for k in range(KT):
                            last = pe.matmul(ps[:], wgu[:, k, c, :], xs_all[:, k, bass.ds(g * GL, GL)],
                                             start=k == 0, stop=k == KT - 1)
                        last.then_inc(s_gu, 1)

                def down(g, j):
                    need(pe, s_hid, g + 1)
                    for t in range(GT):
                        if t % 2 == 0:
                            need(pe, s_base, g * 2 + t // 2 - 1)
                        last = pe.matmul(ps_d[t // 2][:, D * (t % 2):D * (t % 2 + 1)],
                                         hid[j][:, P * t:P * (t + 1)], wd[:], start=True, stop=True)
                        if t % 2:
                            last.then_inc(s_down, 1)

                up(0, 0)
                up(1, 1)
                down(0, 0)
                with pe.Fori(1, NG // 2) as r:
                    for j in range(2):
                        up(r * 2 + j, j)
                        down(r * 2 + j - 1, 1 - j)
                down(NG - 1, 1)

            @blk.scalar
            def _(act):
                def step(g, j):
                    need(act, s_gu, g * 2 + 1)
                    if not isinstance(g, int) or g >= 2:
                        need(act, s_hid, g - 1)
                    act.activation(act_g[j][:], ps_g[j][:], ACT.Silu).then_inc(s_silu, 1)

                in_twos(act, NG, step)

            @blk.vector
            def _(dve):
                def hidden(g, j):
                    need(dve, s_silu, g + 1)
                    need(dve, s_gu, g * 2 + 2)
                    if not isinstance(g, int) or g >= 2:
                        need(dve, s_down, g * 2 - 2)
                    dve.tensor_tensor(hid[j][:], act_g[j][:], ps_u[j][:], ALU.mult).then_inc(s_hid, 1)

                def add(g):
                    for c in range(2):
                        need(dve, s_down, g * 2 + c + 1)
                        tiles = bass.ds(g * GT + 2 * c, 2)
                        dve.scalar_tensor_tensor(
                            base[:, tiles, :], X[:, tiles, :], 2.0,
                            ps_d[c][:].rearrange("p (t d) -> p t d", d=D), ALU.mult, ALU.add
                        ).then_inc(s_base, 1)

                hidden(0, 0)
                hidden(1, 1)
                add(0)
                with dve.Fori(1, NG // 2) as r:
                    for j in range(2):
                        hidden(r * 2 + j, j)
                        add(r * 2 + j - 1)
                add(NG - 1)


def route(nc, logits, slot, weight, tile_expert, C, A):
    with ExitStack() as ctx:
        S = Held(nc, ctx, "mr")
        bias = S.sb("bias", [P, E])
        iota = S.sb("iota", [P, E])
        tiota = S.sb("tiota", [P, NS])
        before = S.sb("before", [P, P])
        ones = S.sb("ones", [P, P])
        sig = S.sb("sig", [P, NT, E])
        top = S.sb("top", [P, NT, 8])
        tidx = S.sb("tidx", [P, NT, 8], U32)
        idx = S.sb("idx", [P, NT, 2])
        total = S.sb("total", [P, NT])
        hot = [S.sb(f"hot{c}", [P, NT, E]) for c in range(2)]
        count = S.sb("count", [P, NT, E])
        scan = [S.sb("scan0", [P, NT, E]), S.sb("scan1", [P, NT, E])]
        pos = S.sb("pos", [P, NT, E])
        big = S.sb("big", [P, E, 32])
        thr = S.sb("thr", [P, 32])
        lower = S.sb("lower", [P, E, E])
        prod = S.sb("prod", [P, E, E])
        tiles, first, after = S.sb("tiles", [P, E]), S.sb("first", [P, E]), S.sb("after", [P, E])
        cmp = S.sb("cmp", [P, NS, E])
        te = S.sb("te", [P, NS])
        slotf = S.sb("slotf", [P, NT, 2])
        ps_rank, ps_tot = S.ps("ps_rank"), S.ps("ps_tot")
        s_w, s_sig, s_ps, s_v, s_bias, s_c, s_pass = (S.sem(n) for n in (
            "w", "sig", "ps", "v", "bias", "c", "pass"))
        with nc.Block() as blk:
            @blk.sync
            def _(sp):
                for dst, src in ((bias, "gate_b"), (iota, "iota"), (tiota, "tiota"), (before, "before"),
                                 (thr, "thr"), (lower, "lower")):
                    sp.dma_start(dst[:], A[src]).then_inc(s_w, 16)

            @blk.scalar
            def _(act):
                need(act, s_bias, 1)
                act.activation(sig[:], sig[:], ACT.Sigmoid).then_inc(s_sig, 1)

            @blk.tensor
            def _(pe):
                need(pe, s_c, 1)
                c = count[:].rearrange("p t e -> p (t e)")
                pe.matmul(ps_rank[:], before[:], c, start=True, stop=True)
                pe.matmul(ps_tot[:], ones[:], c, start=True, stop=True).then_inc(s_ps, 1)

            @blk.vector
            def _(dve):
                done = [0]

                def do(ins):
                    done[0] += 1
                    ins.then_inc(s_v, 1)
                    need(dve, s_v, done[0])

                def over_e(ap):
                    return ap.unsqueeze(2).to_broadcast([P, NT, E])

                need(dve, s_w, 16 * 6)
                do(dve.memset(ones[:], 1.0))
                dve.tensor_tensor(sig[:], logits[:], bias[:].unsqueeze(1).to_broadcast([P, NT, E]),
                                  ALU.add).then_inc(s_bias, 1)
                need(dve, s_sig, 1)
                for t in range(NT):
                    dve.max(top[:, t, :], sig[:, t, :]).then_inc(s_v, 1)
                done[0] += NT
                need(dve, s_v, done[0])
                for t in range(NT):
                    dve.max_index(tidx[:, t, :], top[:, t, :], sig[:, t, :]).then_inc(s_v, 1)
                done[0] += NT
                need(dve, s_v, done[0])
                do(dve.tensor_tensor(total[:], top[:, :, 0], top[:, :, 1], ALU.add))
                do(dve.reciprocal(total[:], total[:]))
                do(dve.tensor_tensor(weight[:], top[:, :, 0:2],
                                     total[:].unsqueeze(2).to_broadcast([P, NT, 2]), ALU.mult))
                do(dve.tensor_copy(idx[:], tidx[:, :, 0:2]))
                for c in range(2):
                    do(dve.tensor_tensor(hot[c][:], iota[:].unsqueeze(1).to_broadcast([P, NT, E]),
                                         over_e(idx[:, :, c]), ALU.is_equal))
                dve.tensor_tensor(count[:], hot[0][:], hot[1][:], ALU.add).then_inc(s_c, 1)
                need(dve, s_ps, 1)
                tot = ps_tot[:].rearrange("p (t e) -> p t e", e=E)
                do(dve.tensor_copy(scan[0][:], tot))
                n, d = 0, 1
                while d < NT:
                    do(dve.tensor_copy(scan[1 - n][:, 0:d, :], scan[n][:, 0:d, :]))
                    do(dve.tensor_tensor(scan[1 - n][:, d:NT, :], scan[n][:, d:NT, :],
                                         scan[n][:, 0:NT - d, :], ALU.add))
                    n, d = 1 - n, 2 * d
                run = scan[n]
                do(dve.tensor_tensor(big[:], run[:, NT - 1, :].unsqueeze(2).to_broadcast([P, E, 32]),
                                     thr[:].unsqueeze(1).to_broadcast([P, E, 32]), ALU.is_gt))
                do(dve.tensor_reduce(tiles[:], big[:], AX.X, ALU.add))
                do(dve.tensor_tensor(prod[:], tiles[:].unsqueeze(1).to_broadcast([P, E, E]), lower[:],
                                     ALU.mult))
                do(dve.tensor_reduce(first[:], prod[:], AX.X, ALU.add))
                do(dve.tensor_tensor(after[:], first[:], tiles[:], ALU.add))
                do(dve.tensor_tensor(cmp[:], tiota[:].unsqueeze(2).to_broadcast([P, NS, E]),
                                     after[:].unsqueeze(1).to_broadcast([P, NS, E]), ALU.is_ge))
                do(dve.tensor_reduce(te[:], cmp[:], AX.X, ALU.add))
                do(dve.tensor_scalar(te[:], te[:], float(E - 1), None, ALU.min))
                do(dve.tensor_copy(tile_expert[:], te[0:1, :]))
                do(dve.tensor_tensor(pos[:], run[:], tot, ALU.subtract))
                do(dve.tensor_tensor(pos[:], pos[:], ps_rank[:].rearrange("p (t e) -> p t e", e=E),
                                     ALU.add))
                do(dve.tensor_scalar(first[:], first[:], float(P), None, ALU.mult))
                do(dve.tensor_tensor(pos[:], pos[:], first[:].unsqueeze(1).to_broadcast([P, NT, E]),
                                     ALU.add))
                for c in range(2):
                    do(dve.tensor_tensor(hot[c][:], hot[c][:], pos[:], ALU.mult))
                    do(dve.tensor_reduce(slotf[:, :, c], hot[c][:], AX.X, ALU.add))
                do(dve.tensor_copy(slot[:], slotf[:]))


def experts(nc, tile_expert, C, ES):
    Z, Y, wgu, wd = ES.Z, ES.Y, ES.wgu, ES.wd
    with ExitStack() as ctx:
        S = Held(nc, ctx, "m3")
        R, AHEAD = 8, 4
        z = [S.sb(f"z{r}", [P, D]) for r in range(R)]
        y = [S.sb(f"y{r}", [P, D]) for r in range(R)]
        zT = [S.sb(f"zT{r}", [P, KT, P]) for r in range(2)]
        gact = [S.sb(f"gact{r}", [P, I]) for r in range(2)]
        hid = [S.sb(f"hid{r}", [P, I]) for r in range(2)]
        hidT = [S.sb(f"hidT{r}", [I, P]) for r in range(2)]
        ps_zT, ps_gu, ps_hT, ps_y = ([S.ps(f"{n}{r}") for r in range(2)]
                                     for n in ("ps_zT", "ps_gu", "ps_hT", "ps_y"))
        s_z, s_out = [S.sem(f"z{r}") for r in range(R)], [S.sem(f"out{r}") for r in range(R)]
        s_zT, s_zTc, s_gu, s_silu, s_hid, s_hT, s_hTc, s_y, s_yc, s_pass = (
            S.sem(n) for n in ("zT", "zTc", "gu", "silu", "hid", "hT", "hTc", "y", "yc", "pass"))

        def walk(eng, slot, first=0, last=NS + 3):
            for n in range(first, R):
                slot(n, n // R, n % R)
            with eng.Fori(1, NS // R - 1) as q:
                for r in range(R):
                    slot(q * R + r, q, r)
            for n in range(NS - R, last):
                slot(n, n // R, n % R)

        def within(n, back=0):
            return not isinstance(n, int) or back <= n < NS + back

        with nc.Block() as blk:
            @blk.sync
            def _(sp):
                def load(n, q, r):
                    need(sp, s_zT, n - R + 1)
                    if not isinstance(n, int) or n >= R:
                        sp.sem_inc(s_pass, 1)
                    sp.dma_start(z[r][:], Z[bass.ds(n * P, P), :]).then_inc(s_z[r], 16)

                def slot(n, q, r):
                    if not isinstance(n, int) or n + AHEAD < NS:
                        load(n + AHEAD, q + (r + AHEAD) // R, (r + AHEAD) % R)
                    if within(n, AHEAD):
                        m = n - AHEAD
                        hold(sp, s_yc, m + 1, s_pass)
                        sp.dma_start(Y[bass.ds(m * P, P), :], y[(r - AHEAD) % R][:]
                                     ).then_inc(s_out[(r - AHEAD) % R], 16)

                for n in range(AHEAD):
                    load(n, 0, n)
                walk(sp, slot, last=NS + AHEAD)
                for r in range(R):
                    need(sp, s_out[r], NS // R * 16)

            @blk.tensor
            def _(pe):
                def expert_of(m):
                    return pe.value_load(tile_expert[0:1, bass.ds(m, 1)], min_val=0, max_val=E - 1)

                def slot(n, q, r):
                    if within(n):
                        j = r % 2
                        need(pe, s_z[r], q * 16 + 16)
                        need(pe, s_zTc, n - 1)
                        for k in range(KT):
                            last = pe.transpose(ps_zT[j][:, P * k:P * (k + 1)],
                                                z[r][:, P * k:P * (k + 1)], C.ident[:])
                        last.then_inc(s_zT, 1)
                    if within(n, 1):
                        m, j = n - 1, (r - 1) % 2
                        expert = expert_of(m)
                        need(pe, s_zTc, m + 1)
                        need(pe, s_hid, m - 1)
                        for k in range(KT):
                            last = pe.matmul(ps_gu[j][:, 0:2 * I], zT[j][:, k, :],
                                             wgu[:, bass.ds(expert, 1), 2 * I * k:2 * I * (k + 1)],
                                             start=k == 0, stop=k == KT - 1)
                        last.then_inc(s_gu, 1)
                    if within(n, 2):
                        m, j = n - 2, r % 2
                        need(pe, s_hid, m + 1)
                        need(pe, s_hTc, m - 1)
                        pe.transpose(ps_hT[j][:, 0:P], hid[j][:], C.ident[:]).then_inc(s_hT, 1)
                    if within(n, 3):
                        m, j = n - 3, (r - 3) % 2
                        expert = expert_of(m)
                        need(pe, s_hTc, m + 1)
                        need(pe, s_yc, m - 1)
                        pe.matmul(ps_y[j][:, 0:D], hidT[j][:], wd[:, bass.ds(expert, 1), :],
                                  start=True, stop=True).then_inc(s_y, 1)

                ES.ready(pe)
                walk(pe, slot)

            @blk.scalar
            def _(act):
                def slot(n, q, r):
                    if within(n):
                        j = r % 2
                        need(act, s_zT, n + 1)
                        need(act, s_gu, n - 1)
                        act.activation(zT[j][:], ps_zT[j][:, 0:D].rearrange("p (k t) -> p k t", k=KT),
                                       ACT.Copy).then_inc(s_zTc, 1)
                    if within(n, 1):
                        m, j = n - 1, (r - 1) % 2
                        need(act, s_gu, m + 1)
                        need(act, s_hid, m - 1)
                        act.activation(gact[j][:], ps_gu[j][:, 0:I], ACT.Silu).then_inc(s_silu, 1)

                walk(act, slot)

            @blk.vector
            def _(dve):
                def slot(n, q, r):
                    if within(n, 3):
                        m, j = n - 3, (r - 3) % 2
                        rm = (r - 3) % R
                        need(dve, s_y, m + 1)
                        if not isinstance(m, int):
                            need(dve, s_out[rm], q * 16 - 16 if r < 3 else q * 16)
                        elif m >= R:
                            need(dve, s_out[rm], m // R * 16)
                        dve.tensor_copy(y[rm][:], ps_y[j][:, 0:D]).then_inc(s_yc, 1)
                    if within(n, 1):
                        m, j = n - 1, (r - 1) % 2
                        need(dve, s_silu, m + 1)
                        need(dve, s_hT, m - 1)
                        dve.tensor_tensor(hid[j][:], gact[j][:], ps_gu[j][:, I:2 * I], ALU.mult
                                          ).then_inc(s_hid, 1)
                    if within(n, 2):
                        m, j = n - 2, r % 2
                        need(dve, s_hT, m + 1)
                        need(dve, s_y, m - 1)
                        dve.tensor_copy(hidT[j][:], ps_hT[j][:, 0:P]).then_inc(s_hTc, 1)

                walk(dve, slot)


def combine(nc, X, base, slot, weight, C, Y):
    with ExitStack() as ctx:
        S = Held(nc, ctx, "m4")
        R = 3
        g = [S.sb(f"g{r}", [P, 2, GT, D]) for r in range(R)]
        ln = LayerNorm(S, C, X, NT)
        s_g = [S.sem(f"g{r}") for r in range(R)]
        s_mix = S.sem("mix")
        with nc.Block() as blk:
            @blk.gpsimd
            def _(pool):
                for q in range(NG):
                    if q >= R:
                        need(pool, s_mix, 2 * GT * (q - R + 1))
                    for t in range(GT):
                        for c in range(2):
                            pool.indirect_dma_start(
                                g[q % R][:, c, t, :], None, Y,
                                bass.IndirectOffsetOnAxis(slot[:, q * GT + t, c:c + 1], 0)
                            ).then_inc(s_g[q % R], 16)
                ln.root(pool, 0)

            @blk.vector
            def _(dve):
                start_at_one(dve, ln.s_x)
                for q in range(NG):
                    need(dve, s_g[q % R], 16 * 2 * GT * (q // R + 1))
                    for t in range(GT):
                        n = q * GT + t
                        for c in range(2):
                            dve.scalar_tensor_tensor(base[:, n, :], g[q % R][:, c, t, :],
                                                     weight[:, n, c:c + 1], base[:, n, :], ALU.mult,
                                                     ALU.add).then_inc(s_mix, 1)
                            need(dve, s_mix, 2 * n + c + 1)
                        dve.bn_stats(ln.stats[:, n, :], base[:, n, :]).then_inc(ln.s_stat, 1)
                        need(dve, ln.s_stat, n + 1)
                        dve.bn_aggr(ln.mv[:, n, :], ln.stats[:, n, :]).then_inc(ln.s_mv, 1)
                need(dve, ln.s_rstd, 1)
                for n in range(NT):
                    dve.tensor_scalar(X[:, n, :], base[:, n, :], ln.mv[:, n, 0:1], ln.rstd[:, n:n + 1],
                                      ALU.subtract, ALU.mult).then_inc(ln.s_x, 1)
                need(dve, ln.s_x, NT)


def layer0_experts(nc, X, ES, C, A):
    with ExitStack() as ctx:
        S = Held(nc, ctx, "m")
        base = S.sb("base", [P, NT, D])
        logits = S.sb("logits", [P, NT, E])
        slot = S.sb("slot", [P, NT, 2], U32)
        weight = S.sb("weight", [P, NT, 2])
        tile_expert = S.sb("tile_expert", [1, NS], U32)
        with ExitStack() as xctx:
            xs_all = Held(nc, xctx, "mx").sb("xs", [P, KT, NT * P])
            logits_of(nc, X, xs_all, logits, C, A)
            route(nc, logits, slot, weight, tile_expert, C, A)
            shared_expert(nc, X, xs_all, base, slot, ES, A)
        experts(nc, tile_expert, C, ES)
        combine(nc, X, base, slot, weight, C, ES.Y)


HH = 8
HV = 32
QUAD = 4


def layer1_attention(nc, X, C, A):
    SQ, SK, SV, SG = range(4)
    bounce = nc.dram_tensor("bounce", (2, 4, P, L), F32).ap()
    with ExitStack() as ctx:
        S = Held(nc, ctx, "a1")
        w = S.sb("w", [P, 4, P])
        qk_norm = S.sb("qk_norm", [P, 2])
        mean8 = S.sb("mean8", [P, HH])
        with ExitStack() as pctx:
            W = Held(nc, pctx, "a1w")
            wdq, wuqT = W.sb("wdq", [P, P]), W.sb("wuqT", [P, P])
            wdkv, wukT, wuvT = W.sb("wdkv", [P, 2, P]), W.sb("wukT", [P, 2, P]), W.sb("wuvT", [P, 2, HD])
            wkr, wqr = W.sb("wkr", [64, P]), W.sb("wqr", [64, P])
            woT, vc, block = W.sb("woT", [HD, P]), W.sb("vc", [HD, P]), W.sb("block", [P, P])
            ps = [W.ps(f"ps{i}") for i in range(5)]
            s_w, s_p, s_c, s_v = W.sem("w"), W.sem("p"), W.sem("c"), W.sem("v")
            with nc.Block() as blk:
                @blk.sync
                def _(sp):
                    loads = [(wdq[:], A["wdq"]), (wuqT[:], A["wuqT"]),
                             (wdkv[:], A["wdkv"].rearrange("(c p) d -> p c d", p=P)),
                             (wukT[:], A["wukT"].rearrange("(c p) d -> p c d", p=P)),
                             (wuvT[:], A["wuvT"].rearrange("(c p) d -> p c d", p=P)),
                             (wkr[:], A["wkr"]), (wqr[:], A["wqr"]), (woT[:], A["woT"]),
                             (block[:], A["block"]), (qk_norm[:], A["qk_norm"]), (mean8[:], A["mean8"])]
                    for dst, src in loads:
                        sp.dma_start(dst, src).then_inc(s_w, 16)
                    need(sp, s_w, 16 * len(loads))

                @blk.tensor
                def _(pe):
                    need(pe, s_w, 16 * 11)
                    pe.matmul(ps[0][:, 0:P], wdq[:], wuqT[:], start=True, stop=True).then_inc(s_p, 1)
                    for c in range(2):
                        last = pe.matmul(ps[1][:, 0:P], wdkv[:, c, :], wukT[:, c, :], start=c == 0, stop=c == 1)
                    last.then_inc(s_p, 1)
                    pe.matmul(ps[2][:, 0:P], wkr[:], wqr[:], start=True, stop=True).then_inc(s_p, 1)
                    for c in range(2):
                        last = pe.matmul(ps[3][0:HD, 0:P], wuvT[:, c, :], wdkv[:, c, :], start=c == 0, stop=c == 1)
                    last.then_inc(s_p, 1)
                    need(pe, s_v, 1)
                    pe.matmul(ps[4][:, 0:P], vc[:], woT[:], start=True, stop=True).then_inc(s_p, 1)

                @blk.vector
                def _(dve):
                    need(dve, s_w, 16 * 11)
                    dve.tensor_scalar(qk_norm[:, 0:1], qk_norm[:, 0:1], HD ** -0.5, None, ALU.mult
                                      ).then_inc(s_c, 1)
                    for n, (bank, to) in enumerate(((0, SQ), (1, SK), (2, SG))):
                        need(dve, s_p, n + 1)
                        dve.tensor_tensor(w[:, to, :], ps[bank][:, 0:P], block[:], ALU.mult).then_inc(s_c, 1)
                    need(dve, s_p, 4)
                    dve.tensor_copy(vc[:], ps[3][0:HD, 0:P]).then_inc(s_v, 1)
                    need(dve, s_p, 5)
                    dve.tensor_tensor(w[:, SV, :], ps[4][:, 0:P], block[:], ALU.mult).then_inc(s_c, 1)

        sm = Softmax(S, C, 2 * QUAD, False)
        tok = S.sb("tok", [P, TT, D])
        xs = [S.sb(f"xs{k}", [P, L]) for k in range(KT)]
        raw = S.sb("raw", [P, 2, L])
        sq = S.sb("sq", [P, 2, L])
        ms = S.sb("ms", [P, 2, TT, HH])
        roots = S.sb("roots", [P, 2, TT, P])
        fin = sq
        words = [S.sb(f"words{m}", [P, L], R32) for m in range(4)]
        QS = [S.sb(f"qs{k}", [P, HH, L], R32) for k in range(KT)]
        KS = [S.sb(f"ks{k}", [P, HH, L], R32) for k in range(KT)]
        V = [S.sb(f"v{k}", [P, TT, HH, HV]) for k in range(KT)]
        yq = S.sb("yq", [P, L])
        part = S.sb("part", [P, TT, QUAD, HD])
        LAG = 7
        ln = LayerNorm(S, C, X, TT)
        ps_a, ps_b, ps_y = S.ps("ps_a"), S.ps("ps_b"), S.ps("ps_y")
        s_tok, s_turn, s_xs, s_zero = S.sem("tok"), S.sem("turn"), S.sem("xs"), S.sem("zero")
        s_v, s_vc, s_raw, s_sq, s_rawc = S.sem("v"), S.sem("vc"), S.sem("raw"), S.sem("sq"), S.sem("rawc")
        s_ms, s_msc, s_root, s_g, s_bc, s_fin = (S.sem(n) for n in ("ms", "msc", "root", "g", "bc", "fin"))
        s_wide, s_kn, s_hi, s_lo, s_wr, s_rd = (S.sem(n) for n in ("wide", "kn", "hi", "lo", "wr", "rd"))
        s_wrs = [S.sem("wr0"), S.sem("wr1")]
        s_rds = [S.sem("rd0"), S.sem("rd1")]
        s_y, s_yc, s_yt, s_part = S.sem("y", True), S.sem("yc"), S.sem("yt"), S.sem("part")
        s_pass_sp, s_pass_pool = S.sem("pass_sp"), S.sem("pass_pool")

        def walk(slot, eng):
            for step in range(8):
                slot(0, -16, (0, 0, step), (0, 0) if step == 2 else None)
            for step in range(4):
                slot(0, -16, (0, 1, step), None)

            def both(b, h):
                front, values = None, None
                more = not (isinstance(b, int) and b == B - 1)
                if h < 4:
                    front = (b, 1, h + 4)
                elif h < 12 and more:
                    front = (b + 1, 0, h - 4)
                elif h < H and more:
                    front = (b + 1, 1, h - 12)
                if h == 5:
                    values = (b, 1)
                elif h == 13 and more:
                    values = (b + 1, 0)
                slot(b, h, front, values)

            over_batches(both, eng, LAG, 2)

        with nc.Block() as blk:
            @blk.sync
            def _(sp):
                def front(b, k, step):
                    if step != 7:
                        return
                    f = b * 2 + k
                    for m, when in ((0, s_hi), (1, s_lo), (2, s_hi), (3, s_lo)):
                        hold(sp, when, f * 2 + m // 2 + 1, s_pass_sp)
                        sp.dma_start(bounce[k, m], words[m][:].bitcast(F32)).then_inc(s_wrs[k], 16)
                    hold(sp, s_wrs[k], b * 64 + 64, s_pass_sp)
                    for c in range(4):
                        rows = slice(HD * c, HD * (c + 1))
                        for buf, m in ((QS[k], c % 2), (KS[k], 2 + c // 2)):
                            sp.dma_start(buf[rows, :, :].bitcast(F32),
                                         bounce[k, m].rearrange("(h d) t -> d h t", d=HD)
                                         ).then_inc(s_rds[k], 16)

                walk(lambda b, h, f, v: f and front(*f), sp)

            @blk.gpsimd
            def _(pool):
                cleared = [buf[4 * HD:P, :, :].bitcast(F32) for buf in QS + KS] + [v[:] for v in V]
                for n, at in enumerate(cleared):
                    pool.memset(at, 0.0).then_inc(s_zero, 1)
                    need(pool, s_zero, n + 1)

                def fetch(b):
                    pool.tensor_copy(tok[:], X[:, bass.ds(b * TT, TT), :]).then_inc(s_tok, 1)

                def front(b, k, step):
                    f = b * 2 + k
                    if step in (2, 3):
                        a, n = step - 2, f * 2 + step - 2
                        hold(pool, s_msc, n + 1, s_pass_pool)
                        at = ms[:, a, :, :].rearrange("p t h -> p (t h)")
                        pool.tensor_tensor(at, at, C.minus_half[:, 0:TT * HH], ALU.pow
                                           ).then_inc(s_root, 1)
                        hold(pool, s_root, n + 1, s_pass_pool)
                        if a or not (isinstance(b, int) and b == 0 and k == 0):
                            hold(pool, s_bc, n - 1, s_pass_pool)
                        pool.tensor_copy(roots[:, a, :, :].rearrange("p t (h d) -> p t h d", d=HD),
                                         ms[:, a, :, :].unsqueeze(3).to_broadcast([P, TT, HH, HD])
                                         ).then_inc(s_wide, 1)

                def slot(b, h, f, v):
                    if h == 0 and not (isinstance(b, int) and b == B - 1):
                        hold(pool, s_turn, b * 2 + 2, s_pass_pool)
                        fetch(b + 1)
                    if f:
                        front(*f)
                    if h == H + 5:
                        ln.root(pool, b)

                fetch(0)
                walk(slot, pool)

            @blk.tensor
            def _(pe):
                def front(b, k, step):
                    f = b * 2 + k
                    if step == 0:
                        need(pe, s_tok, b + 1)
                        need(pe, s_fin, f * 2)
                        for t in range(TT):
                            last = pe.transpose(ps_a[:, P * t:P * (t + 1)], tok[:, t, P * k:P * (k + 1)],
                                                C.ident[:])
                        last.then_inc(s_turn, 1)
                    elif step == 1:
                        need(pe, s_xs, f + 1)
                        need(pe, s_kn, f * 2)
                        pe.matmul(ps_b[:], w[:, SQ, :], xs[k][:], start=True, stop=True).then_inc(s_raw, 1)
                    elif step in (2, 3):
                        a = step - 2
                        need(pe, s_rawc, f * 2 + a + 1)
                        pe.matmul(ps_b[:], w[:, SG if a else SK, :], xs[k][:], start=True, stop=True
                                  ).then_inc(s_g if a else s_raw, 1)
                        need(pe, s_vc, 1 if isinstance(b, int) and f == 0 else f)
                        need(pe, s_msc, f * 2 + a)
                        need(pe, s_sq, f * 2 + a + 1)
                        for t in range(TT):
                            last = pe.matmul(ps_a[:, t * HH:(t + 1) * HH], sq[:, a, P * t:P * (t + 1)],
                                             mean8[:], start=True, stop=True)
                        last.then_inc(s_ms, 1)
                    elif step in (6, 7):
                        a = step - 6
                        need(pe, s_wide, f * 2 + a + 1)
                        need(pe, s_msc, f * 2 + 2)
                        if a:
                            need(pe, s_fin, f * 2 + 1)
                        for t in range(TT):
                            last = pe.matmul(ps_a[:, P * t:P * (t + 1)],
                                             roots[:, a, t, :],
                                             C.ident[:], start=True, stop=True)
                        last.then_inc(s_bc, 1)

                def values(b, k):
                    f = b * 2 + k
                    if isinstance(b, int) and f in (0, 2 * B - 1):
                        need(pe, s_xs if f == 0 else s_fin, 1 if f == 0 else f * 2 + 2)
                    else:
                        need(pe, s_xs, f + 2)
                    for t in range(TT):
                        last = pe.matmul(ps_a[:, P * t:P * (t + 1)], xs[k][:, P * t:P * (t + 1)],
                                         w[:, SV, :], start=True, stop=True)
                    last.then_inc(s_v, 1)

                def product(b, h, out, i, keys):
                    k, j = h // HH, h % HH
                    if i == 0 and j == 0:
                        need(pe, s_rds[k], b * 128 + 128)
                        if isinstance(b, int) and b == 0:
                            need(pe, s_zero, 6)
                    return pe.matmul(out, QS[k][:, j, P * i:P * (i + 1)], KS[k][:, j, 0:keys],
                                     start=True, stop=True)

                def attend(b, u, tiles):
                    if tiles[0] == 0:
                        sm.need_probT(pe, b * H + QUAD * (u + 1) - 1)
                        need(pe, s_part, b * TT + u)
                        need(pe, s_vc, b * 2 + u // 2 + 1)
                    k = u // 2
                    for t in tiles:
                        for j in range(QUAD):
                            h = QUAD * u + j
                            n = TCOL[t]
                            last = pe.matmul(ps_y[HV * j:HV * (j + 1), P * t:L], V[k][:, t, h % HH, :],
                                             sm.probT[:, h % (2 * QUAD), n:n + L - P * t],
                                             start=t == 0, stop=t == TT - 1)
                    if t == TT - 1:
                        last.then_inc(s_y, 1)

                def turn_back(b, u):
                    need(pe, s_yc, b * (H // QUAD) + u + 1)
                    for t in range(TT):
                        last = pe.transpose(ps_y[:, P * t:P * (t + 1)], yq[:, P * t:P * (t + 1)],
                                            C.ident[:])
                    last.then_inc(s_yt, 1)

                def slot(b, h, f, v):
                    def between():
                        if v:
                            values(*v)
                        if f:
                            front(*f)
                        u = (h - 6) // QUAD
                        if u >= 0 and h < H + 6:
                            if h % QUAD == 2:
                                attend(b, u, (0,))
                            elif h % QUAD == 3:
                                attend(b, u, (1,))
                            elif h % QUAD == 0:
                                attend(b, u, (2, 3))

                    if h < 0 or h > H + 1:
                        between()
                    else:
                        sm.tensor_slot(pe, b, h, lambda *to: product(b, h, *to), between)
                    if h >= 9 and h % QUAD == 1:
                        turn_back(b, (h - 9) // QUAD)

                start_at_one(pe, s_y)
                walk(slot, pe)

            @blk.scalar
            def _(act):
                def front(b, k, step):
                    f = b * 2 + k
                    if step == 0:
                        need(act, s_turn, f + 1)
                        need(act, s_g, f - 1)
                        need(act, s_v, f - 1)
                        act.activation(xs[k][:], ps_a[:], ACT.Copy).then_inc(s_xs, 1)
                    elif step in (1, 2):
                        a = step - 1
                        need(act, s_rawc, f * 2 + a + 1)
                        need(act, s_lo, f * 2)
                        act.activation(sq[:, a, :], raw[:, a, :], ACT.Square).then_inc(s_sq, 1)
                    elif step in (6, 7):
                        a = step - 6
                        need(act, s_fin, f * 2 + 1 if a == 0 else f * 2 + 2)
                        if a:
                            need(act, s_kn, f * 2 + 2)
                        if not (isinstance(b, int) and b == 0 and k == 0):
                            need(act, s_wrs[1 - k], b * 64 if k == 0 else b * 64 + 64)
                        act.activation(words[2 * a][:], fin[:, a, :], ACT.Copy).then_inc(s_hi, 1)

                def values(b, k):
                    need(act, s_v, b * 2 + k + 1)
                    need(act, s_y, b * (H // QUAD) - 4 + 2 * k + 2)
                    if isinstance(b, int):
                        need(act, s_zero, 6)
                    act.activation(V[k][:, :, :, 0:HD],
                                   ps_a[:].rearrange("p (t h d) -> p t h d", t=TT, h=HH),
                                   ACT.Copy).then_inc(s_vc, 1)

                def slot(b, h, f, v):
                    if 0 <= h <= H + 1:
                        sm.scalar_slot(act, b, h)
                    if v:
                        values(*v)
                    if f:
                        front(*f)
                    if h >= 8 and h % QUAD == 0:
                        need(act, s_y, b * (H // QUAD) + (h - 8) // QUAD + 1)
                        act.activation(yq[:], ps_y[:], ACT.Copy).then_inc(s_yc, 1)

                start_at_one(act, sm.s_pt_act)
                walk(slot, act)

            @blk.vector
            def _(dve):
                def front(b, k, step):
                    f = b * 2 + k
                    if step in (1, 2):
                        need(dve, s_raw, f * 2 + step)
                        dve.tensor_copy(raw[:, step - 1, :], ps_b[:]).then_inc(s_rawc, 1)
                    if step in (2, 3):
                        a = step - 2
                        need(dve, s_ms, f * 2 + a + 1)
                        dve.tensor_scalar(ms[:, a, :, :].rearrange("p t h -> p (t h)"),
                                          ps_a[:, 0:TT * HH], RMS_EPS, None, ALU.add
                                          ).then_inc(s_msc, 1)
                    elif step in (6, 7):
                        a = step - 6
                        need(dve, s_bc, f * 2 + a + 1)
                        dve.scalar_tensor_tensor(fin[:, a, :], raw[:, a, :], qk_norm[:, a:a + 1],
                                                 ps_a[:], ALU.mult, ALU.mult).then_inc(s_fin, 1)
                        if a:
                            need(dve, s_fin, f * 2 + 2)
                            need(dve, s_g, f + 1)
                            dve.tensor_tensor(fin[:, 1, :], fin[:, 1, :], ps_b[:], ALU.add
                                              ).then_inc(s_kn, 2)

                def low_words(b, k, a):
                    f = b * 2 + k
                    need(dve, s_hi, f * 2 + a + 1)
                    dve.tensor_tensor(words[2 * a + 1][:], fin[:, a, :],
                                      words[2 * a][:].bitcast(F32), ALU.subtract).then_inc(s_lo, 1)

                def reciprocals(b, u):
                    j = slice(QUAD * (u % 2), QUAD * (u % 2) + QUAD)
                    need(dve, sm.s_exp, (b * H + QUAD * (u + 1)) * TT)
                    dve.reciprocal(sm.recip[:, j, :], sm.rowsum[:, j, :]).then_inc(sm.s_recip, 1)

                def outputs(b, u):
                    j = QUAD * (u % 2)
                    recip = sm.recip[:, j:j + QUAD, :]
                    n = b * (H // QUAD) + u + 1
                    need(dve, sm.s_recip, n)
                    need(dve, s_yt, n)
                    dve.tensor_tensor(
                        part[:], ps_y[:].rearrange("p (t j d) -> p t j d", t=TT, j=QUAD)[:, :, :, 0:HD],
                        recip.rearrange("p j t -> p t j").unsqueeze(3).to_broadcast([P, TT, QUAD, HD]),
                        ALU.mult).then_inc(s_part, 1)
                    need(dve, s_part, n)
                    if u == 0:
                        need(dve, ln.s_x, b * TT)
                    cols = slice(QUAD * HD * u, QUAD * HD * (u + 1))
                    dve.tensor_tensor(
                        ln.res[:, :, cols].rearrange("p t (j d) -> p t j d", d=HD),
                        X[:, bass.ds(b * TT, TT), cols].rearrange("p t (j d) -> p t j d", d=HD),
                        part[:], ALU.add).then_inc(ln.s_sum, 1)

                def slot(b, h, f, v):
                    if h >= 8 and h % QUAD == 0:
                        reciprocals(b, (h - 8) // QUAD)
                    if 0 <= h <= H + 1:
                        sm.vector_slot(dve, b, h)
                    if f and f[2] == 7:
                        low_words(f[0], f[1], 0)
                    if f:
                        front(*f)
                    if f and f[2] == 7 and h < 0:
                        low_words(f[0], f[1], 1)
                    if h == 4:
                        low_words(b, 1, 1)
                    if h == 12 and not (isinstance(b, int) and b == B - 1):
                        low_words(b + 1, 0, 1)
                    if h >= 9 and h % QUAD == 1:
                        outputs(b, (h - 9) // QUAD)
                    if h == H + 5:
                        need(dve, ln.s_sum, b * TT + TT)
                        for t in range(TT):
                            ln.statistics(dve, b, t)
                    if h == H + 6:
                        ln.write(dve, b)

                start_at_one(dve, ln.s_sum, ln.s_x, sm.s_pt_dve)
                walk(slot, dve)


def layer1_ffn(nc, X, C, A):
    STEPS, BETA, THRESHOLD = 5, 0.9, 1.0
    with ExitStack() as ctx:
        S = Held(nc, ctx, "f1")
        F = Features(S, C, X)
        wfc = S.sb("wfc", [P, KT, FF])
        wpj = S.sb("wpj", [P, NF, D])
        hid = [S.sb(f"hid{j}", [P, NF, GL]) for j in range(2)]
        pos = [S.sb(f"pos{j}", [P, GL]) for j in range(2)]
        cur = S.sb("cur", [P, GL])
        acc = S.sb("acc", [P, GL])
        mem, nxt = S.sb("mem", [P, GL]), S.sb("nxt", [P, GL])
        ln = LayerNorm(S, C, X, GT)
        ps_h = [S.ps(f"ps_h{j}") for j in range(2)]
        ps_y = [S.ps(f"ps_y{c}") for c in range(2)]
        s_w, s_h, s_pos, s_hid, s_y, s_cur = (S.sem(n) for n in ("w", "h", "pos", "hid", "y", "cur"))
        s_v, s_store = S.sem("v"), S.sem("store")
        V_STEPS = 3 * (STEPS - 1) + 1
        with nc.Block() as blk:
            @blk.sync
            def _(sp):
                sp.dma_start(wfc[:], A["wfcT"].rearrange("(k p) f -> p k f", p=P)).then_inc(s_w, 16)
                sp.dma_start(wpj[:], A["wpjT"].rearrange("(k p) d -> p k d", p=P)).then_inc(s_w, 16)
                out = A["out"].rearrange("b (t p) d -> p (b t) d", p=P)
                with sp.Fori(0, NG) as g:
                    hold(sp, ln.s_x, g * GT + GT, F.passed)
                    sp.dma_start(out[:, bass.ds(g * GT, GT), :], X[:, bass.ds(g * GT, GT), :]
                                 ).then_inc(s_store, 16)
                need(sp, s_store, 16 * NG)

            @blk.gpsimd
            def _(pool):
                F.fetch(pool, 0, 0)
                F.fetch(pool, 1, 1)
                with pool.Fori(1, NG // 2) as r:
                    for j in range(2):
                        ln.root(pool, r * 2 + j - 2)
                        F.fetch(pool, r * 2 + j, j)
                for g in range(NG - 2, NG):
                    ln.root(pool, g)

            @blk.tensor
            def _(pe):
                need(pe, s_w, 32)

                def up(g, j):
                    F.turn(pe, g, j)
                    need(pe, F.s_xs, g * KT + KT)
                    for f in range(NF):
                        need(pe, s_pos, g * NF + f - 1)
                        for k in range(KT):
                            last = pe.matmul(ps_h[f % 2][:], wfc[:, k, P * f:P * (f + 1)], F.xs[j][:, k, :],
                                             start=k == 0, stop=k == KT - 1)
                        last.then_inc(s_h, 1)

                def down(g, j):
                    need(pe, s_hid, g * NF + NF)
                    for t in range(GT):
                        if t % 2 == 0:
                            need(pe, s_cur, g * 2 + t // 2 - 1)
                        for f in range(NF):
                            last = pe.matmul(ps_y[t // 2][:, D * (t % 2):D * (t % 2 + 1)],
                                             hid[j][:, f, P * t:P * (t + 1)], wpj[:, f, :],
                                             start=f == 0, stop=f == NF - 1)
                        if t % 2:
                            last.then_inc(s_y, 1)

                up(0, 0)
                up(1, 1)
                down(0, 0)
                with pe.Fori(1, NG // 2) as r:
                    for j in range(2):
                        up(r * 2 + j, j)
                        down(r * 2 + j - 1, 1 - j)
                down(NG - 1, 1)

            @blk.scalar
            def _(act):
                def step(g, j):
                    if not isinstance(g, int) or g >= 2:
                        need(act, s_y, g * 2 - 2)
                    F.keep(act, g, j)
                    for f in range(NF):
                        need(act, s_h, g * NF + f + 1)
                        need(act, s_hid, g * NF + f - 1)
                        act.activation(pos[f % 2][:], ps_h[f % 2][:], ACT.Relu).then_inc(s_pos, 1)
                        need(act, s_pos, g * NF + f + 1)
                        act.activation(hid[j][:, f, :], pos[f % 2][:], ACT.Square).then_inc(s_hid, 1)

                step(0, 0)
                step(1, 1)
                with act.Fori(1, NG // 2) as r:
                    for j in range(2):
                        step(r * 2 + j, j)

            @blk.vector
            def _(dve):
                start_at_one(dve, ln.s_sum, ln.s_x)
                with dve.Fori(0, NG) as g:
                    for c in range(2):
                        n = g * 2 + c
                        need(dve, s_y, n + 1)
                        dve.tensor_copy(cur[:], ps_y[c][:]).then_inc(s_cur, 1)
                        need(dve, s_cur, n + 1)
                        base = n * V_STEPS
                        m = cur
                        dve.tensor_scalar(acc[:], cur[:], THRESHOLD, None, ALU.is_gt).then_inc(s_v, 1)
                        for i in range(STEPS - 1):
                            at = base + 3 * i + 1
                            dve.scalar_tensor_tensor(nxt[:], m[:], BETA, cur[:], ALU.mult, ALU.add
                                                     ).then_inc(s_v, 1)
                            need(dve, s_v, at + 1)
                            dve.scalar_tensor_tensor(mem[:], m[:], THRESHOLD, nxt[:], ALU.is_gt,
                                                     ALU.subtract, reverse1=True).then_inc(s_v, 1)
                            need(dve, s_v, at + 2)
                            dve.scalar_tensor_tensor(acc[:], mem[:], THRESHOLD, acc[:], ALU.is_gt,
                                                     ALU.add).then_inc(s_v, 1)
                            need(dve, s_v, at + 3)
                            m = mem
                        tiles = bass.ds(g * GT + 2 * c, 2)
                        if c == 0:
                            need(dve, ln.s_x, g * GT)
                        dve.scalar_tensor_tensor(ln.res[:, 2 * c:2 * c + 2, :].rearrange("p t d -> p (t d)"),
                                                 acc[:], 1.0 / STEPS,
                                                 X[:, tiles, :].rearrange("p t d -> p (t d)"), ALU.mult,
                                                 ALU.add).then_inc(ln.s_sum, 1)
                        need(dve, ln.s_sum, n + 1)
                        for t in range(2):
                            ln.statistics(dve, g, 2 * c + t)
                    ln.write(dve, g)


def build(nc, A):
    with ExitStack() as ctx:
        C = Held(nc, ctx, "c")
        X = C.sb("X", [P, NT, D])
        C.ident, C.mask = C.sb("ident", [P, P]), C.sb("mask", [P, L])
        C.minus_half = C.sb("minus_half", [P, 2 * TT * HH])
        s_const = C.sem("const")
        with nc.Block() as blk:
            @blk.sync
            def _(sp):
                sp.dma_start(C.ident[:], A["ident"]).then_inc(s_const, 16)
                sp.dma_start(C.mask[:], A["mask"]).then_inc(s_const, 16)
                sp.wait_ge(s_const, 32)

            @blk.gpsimd
            def _(pool):
                pool.memset(C.minus_half[:], -0.5)
        with ExitStack() as ectx:
            ES = ExpertStore(nc, ectx)
            layer0_attention(nc, X, C, A, lambda pool: ES.start(pool, A))
            layer0_experts(nc, X, ES, C, A)
        layer1_attention(nc, X, C, A)
        layer1_ffn(nc, X, C, A)


def shape_constants():
    f32 = np.float32
    after = np.arange(P)[None, :] > np.arange(P)[:, None]
    mask = np.zeros((P, L), f32)
    mask[:, L - P:] = np.where(after, f32(MASKED), f32(0))
    heads = np.kron(np.eye(HH), np.ones((HD, HD))).astype(f32)
    rows = lambda a: np.ascontiguousarray(np.broadcast_to(np.asarray(a, f32), (P,) + np.shape(a)))
    return {
        "ident": np.eye(P, dtype=f32), "mask": mask, "before": after.astype(f32),
        "iota": rows(np.arange(E)), "tiota": rows(np.arange(NS)), "thr": rows(P * np.arange(NT)),
        "lower": rows(np.tril(np.ones((E, E)), -1)), "block": heads,
        "mean8": np.ascontiguousarray(heads[:, ::HD] / f32(HD)),
    }


def laid_out(i):
    a0, f0, a1, f1 = "L0_attn_", "L0_ffn_", "L1_attn_", "L1_ffn_"
    eight = lambda a: np.tile(a, (1, HH))
    out = {
        "x": i[a0 + "x_bld"], "xT": i[a0 + "x_bld"].transpose(0, 2, 1),
        "wqT": i[a0 + "Wq"].transpose(2, 1, 0), "wkT": i[a0 + "Wk_up"].transpose(2, 1, 0),
        "wvT": i[a0 + "Wv_up"].transpose(2, 1, 0), "wo": i[a0 + "Wout"].transpose(1, 0, 2),
        "wdn": i[a0 + "Wkv_down"],
        "gate_w": i[f0 + "gate_w"], "gate_b": np.broadcast_to(i[f0 + "gate_b"], (P, E)),
        "swg": i[f0 + "shared_wg"], "swu": i[f0 + "shared_wu"], "swd": i[f0 + "shared_wd"],
        "ewg": i[f0 + "experts_wg"], "ewu": i[f0 + "experts_wu"], "ewd": i[f0 + "experts_wd"],
        "wdq": eight(i[a1 + "W_DQ"]), "wuqT": eight(i[a1 + "W_UQ"].T),
        "wdkv": eight(i[a1 + "W_DKV"]), "wukT": eight(i[a1 + "W_UKV"][:HD].T),
        "wuvT": i[a1 + "W_UKV"][HD:].T, "wkr": eight(i[a1 + "W_KR"]), "wqr": eight(i[a1 + "W_QR"]),
        "woT": eight(i[a1 + "W_O"].T),
        "qk_norm": np.stack([np.tile(i[a1 + "q_norm_w"], HH), np.tile(i[a1 + "k_norm_w"], HH)], 1),
        "wfcT": i[f1 + "W_fc"].T, "wpjT": i[f1 + "W_proj"].T,
    }
    return {k: np.ascontiguousarray(v) for k, v in out.items()}


def kernel(**inputs):
    from concourse import bacc
    from concourse.bass_utils import run_bass_kernel_spmd

    arrays = {**laid_out({k: np.asarray(v) for k, v in inputs.items()}), **shape_constants()}
    nc = bacc.Bacc("TRN2", target_bir_lowering=False, num_devices=1)
    A = {k: nc.dram_tensor(f"in_{k}", v.shape, mybir.dt.from_np(v.dtype), kind="ExternalInput").ap()
         for k, v in arrays.items()}
    A["out"] = nc.dram_tensor("out", (B, L, D), F32, kind="ExternalOutput").ap()
    build(nc, A)
    r = run_bass_kernel_spmd(nc, [{f"in_{k}": v for k, v in arrays.items()}], core_ids=[0])
    return r.results[0]["out"]
```

```python
from contextlib import ExitStack

import numpy as np
import concourse.bass as bass
from concourse import mybir
from concourse.alu_op_type import AluOpType as ALU

F32 = mybir.dt.float32
R32 = mybir.dt.float32r
U32 = mybir.dt.uint32
I32 = mybir.dt.int32
ACT = mybir.ActivationFunctionType
AX = mybir.AxisListType

P = 128
B, L, D = 8, 512, 256
KT = D // P
TT = L // P
NT = B * TT
H = 16
LD = 64
NPAIR = H // 2
E, I = 16, 128
NW = E + 1
HD = D // H
FF = 1024
NF = FF // P
LN_EPS = 1e-5
RMS_EPS = 1.1920929e-07
MASKED = -1.0e30

QOFF = [P * i * (i + 1) // 2 for i in range(TT + 1)]
TRI = QOFF[TT]
SGROUP = [[0, 1], [2], [3]]
SCOL = [0, P, 0, 0]
TGROUPS = [[0], [1, 3], [2]]
TCOL = {0: 0, 1: L, 3: L + 3 * P, 2: 2 * L}
TGCOL = [0, L, 2 * L]
TGLEN = [L, L, 2 * P]


class Held:

    def __init__(self, nc, ctx, stage):
        self.nc, self.ctx, self.stage, self.sems = nc, ctx, stage, []
        ctx.callback(self.clear)

    def clear(self):
        self.nc.clear_and_free_semaphores(self.sems)
        self.nc.all_engine_barrier()

    def sb(self, name, shape, dt=F32):
        return self.ctx.enter_context(self.nc.sbuf_tensor(f"{self.stage}_{name}", shape, dt))

    def ps(self, name):
        return self.ctx.enter_context(self.nc.psum_tensor(f"{self.stage}_{name}", [P, 512], F32))

    def sem(self, name, from1=False):
        self.sems.append(self.nc.alloc_semaphore(f"{self.stage}_{name}" + ("_from1" if from1 else "")))
        return self.sems[-1]


def start_at_one(eng, *sems):
    for s in sems:
        eng.sem_inc(s, 1)


def need(eng, sem, value):
    if not isinstance(value, int) or value > 0:
        eng.wait_ge(sem, value + 1 if sem.name.endswith("_from1") else value)


def hold(eng, sem, value, passed):
    need(eng, sem, value)
    eng.sem_inc(passed, 1)


class Softmax:

    def __init__(self, S, C, ring, normed):
        self.C, self.ring, self.normed = C, ring, normed
        self.back = 3 if normed else 2
        self.prob = S.sb("prob", [P, 4, TRI])
        self.probT = S.sb("probT", [P, ring, TRI])
        self.negmax = S.sb("negmax", [P, 4, TT])
        self.rowsum, self.recip = (S.sb(n, [P, ring, TT]) for n in ("rowsum", "recip"))
        self.ps_score = [S.ps(f"ps_score{g}") for g in range(3)]
        self.ps_trans = [S.ps(f"ps_trans{g}") for g in range(2)]
        self.s_score, self.s_max, self.s_exp, self.s_recip, self.s_norm, self.s_trans, self.passed = (
            S.sem(n) for n in ("score", "max", "exp", "recip", "norm", "trans", "passed"))
        self.s_pt_act, self.s_pt_dve = S.sem("pt_act", True), S.sem("pt_dve", True)

    def scores(self, pe, n, h, product):
        for g, tiles in enumerate(SGROUP):
            need(pe, self.s_max, n * TT - TT + tiles[-1] + 1)
            for i in tiles:
                keys = P * (i + 1)
                at = SCOL[i]
                last = product(self.ps_score[g][:, at:at + keys], i, keys)
            last.then_inc(self.s_score, 1)

    def mask_max(self, dve, n, h):
        for g, tiles in enumerate(SGROUP):
            hold(dve, self.s_score, n * 3 + g + 1, self.passed)
            for i in tiles:
                keys = P * (i + 1)
                at = SCOL[i]
                dve.tensor_tensor_reduce(
                    out=self.prob[:, h % 4, QOFF[i]:QOFF[i] + keys],
                    in0=self.ps_score[g][:, at:at + keys], in1=self.C.mask[:, L - keys:L], scale=-1.0,
                    scalar=3.0e38, op0=ALU.add, op1=ALU.min,
                    accum_out=self.negmax[:, h % 4, i:i + 1]).then_inc(self.s_max, 1)

    def exps(self, act, n, h):
        for i in range(TT):
            need(act, self.s_max, n * TT + i + 1)
            at = self.prob[:, h % 4, QOFF[i]:QOFF[i + 1]]
            act.activation(at, at, ACT.Exp, scale=-1.0, bias=self.negmax[:, h % 4, i:i + 1],
                           accum_out=self.rowsum[:, h % self.ring, i:i + 1]).then_inc(self.s_exp, 1)

    def normalise(self, dve, n, h):
        need(dve, self.s_exp, n * TT + TT)
        r = h % self.ring
        dve.reciprocal(self.recip[:, r, :], self.rowsum[:, r, :]).then_inc(self.s_recip, 1)
        need(dve, self.s_recip, n + 1)
        for i in range(TT):
            at = self.prob[:, h % 4, QOFF[i]:QOFF[i + 1]]
            dve.tensor_scalar(at, at, self.recip[:, r, i:i + 1], None, ALU.mult
                              ).then_inc(self.s_norm, 1)

    def transposes(self, pe, n, h, groups):
        for g in groups:
            if g == 0:
                need(pe, self.s_norm if self.normed else self.s_exp, n * TT + TT)
            if g == 0:
                need(pe, self.s_pt_dve, n)
            elif g == 1:
                need(pe, self.s_pt_act, n * 2)
            else:
                need(pe, self.s_pt_act, n * 2 + 1)
            for k, i in [(k, i) for k in TGROUPS[g] for i in range(k, TT)]:
                col = TCOL[k] - TGCOL[g] + P * (i - k)
                last = pe.transpose(self.ps_trans[(3 * h + g) % 2][:, col:col + P],
                                    self.prob[:, h % 4, QOFF[i] + P * k:QOFF[i] + P * (k + 1)],
                                    self.C.ident[:])
            last.then_inc(self.s_trans, 1)

    def copy_group(self, eng, n, h, g):
        need(eng, self.s_trans, n * 3 + g + 1)
        out = self.probT[:, h % self.ring, TGCOL[g]:TGCOL[g] + TGLEN[g]]
        src = self.ps_trans[(3 * h + g) % 2][:, 0:TGLEN[g]]
        if g == 1:
            eng.tensor_copy(out, src).then_inc(self.s_pt_dve, 1)
        else:
            eng.activation(out, src, ACT.Copy).then_inc(self.s_pt_act, 1)

    def need_probT(self, pe, n):
        need(pe, self.s_pt_act, n * 2 + 2)
        need(pe, self.s_pt_dve, n + 1)


    def tensor_slot(self, pe, b, h, product, between):
        turned, n, n_h = self.back <= h < H + self.back, b * H + h - self.back, h - self.back
        if h < H:
            self.scores(pe, b * H + h, h, product)
        if turned:
            self.transposes(pe, n, n_h, (0, 1))
        between()
        if turned:
            self.transposes(pe, n, n_h, (2,))

    def scalar_slot(self, act, b, h):
        turned, n, n_h = self.back <= h < H + self.back, b * H + h - self.back, h - self.back
        if turned:
            self.copy_group(act, n, n_h, 0)
        if 1 <= h <= H:
            self.exps(act, b * H + h - 1, h - 1)
        if turned:
            self.copy_group(act, n, n_h, 2)

    def vector_slot(self, dve, b, h):
        if h < H:
            self.mask_max(dve, b * H + h, h)
        if self.back <= h < H + self.back:
            self.copy_group(dve, b * H + h - self.back, h - self.back, 1)
        if self.normed and 2 <= h < H + 2:
            self.normalise(dve, b * H + h - 2, h - 2)


def over_batches(slot, eng, lag, ahead=1):

    def batch(b):
        for h in range(lag, H):
            slot(b, h)
        for h in range(lag):
            if h < 2:
                slot(b, H + h)
            slot(b + 1, h)
            if h >= 2:
                slot(b, H + h)

    for h in range(lag):
        slot(0, h)
    with eng.Fori(0, B - ahead) as b:
        batch(b)
    for b in range(B - ahead, B - 1):
        batch(b)
    for h in range(lag, H + lag):
        slot(B - 1, h)


def layer0_attention(nc, X, C, A, meanwhile):
    with ExitStack() as ctx:
        S = Held(nc, ctx, "a0")
        wqk = S.sb("wqk", [P, KT, H * LD])
        wvo = S.sb("wvo", [P, NPAIR, D])
        wdn2 = S.sb("wdn2", [P, KT, 2, LD])

        with ExitStack() as pctx:
            W = Held(nc, pctx, "a0w")
            wqT = W.sb("wqT", [LD, H, D])
            wkT = W.sb("wkT", [LD, H, LD])
            wvT = W.sb("wvT", [LD, H, LD])
            wo = W.sb("wo", [LD, H, D])
            s_load, s_qk, s_vo, s_cp = W.sem("load"), W.sem("qk"), W.sem("vo"), W.sem("cp")
            s_cv = W.sem("cv")
            pqk = [W.ps("pqk0"), W.ps("pqk1")]
            pvo = [W.ps("pvo0"), W.ps("pvo1")]
            with nc.Block() as blk:
                @blk.sync
                def _(sp):
                    for dst, src in ((wqT, A["wqT"]), (wkT, A["wkT"]), (wvT, A["wvT"]), (wo, A["wo"])):
                        sp.dma_start(dst[:], src).then_inc(s_load, 16)
                    for c in range(2):
                        sp.dma_start(wdn2[:, :, c, :], A["wdn"].rearrange("(k p) c -> p k c", p=P)
                                     ).then_inc(s_load, 16)
                    need(sp, s_load, 16 * 6)

                @blk.tensor
                def _(pe):
                    need(pe, s_load, 16 * 6)
                    for k in range(KT):
                        for half in range(2):
                            n = 2 * k + half
                            if n >= 2:
                                need(pe, s_cp, n - 1)
                            for h in range(8):
                                hh = 8 * half + h
                                ins = pe.matmul(pqk[n % 2][:, h * LD:(h + 1) * LD],
                                                wqT[:, hh, k * P:(k + 1) * P], wkT[:, hh, :],
                                                start=True, stop=True)
                            ins.then_inc(s_qk, 1)
                    for p in range(NPAIR):
                        if p >= 2:
                            need(pe, s_cv, p - 1)
                        for c in range(2):
                            ins = pe.matmul(pvo[p % 2][LD * c:LD * (c + 1), 0:D], wvT[:, 2 * p + c, :],
                                            wo[:, 2 * p + c, :], start=True, stop=True)
                        ins.then_inc(s_vo, 1)

                @blk.scalar
                def _(act):
                    for n in range(4):
                        need(act, s_qk, n + 1)
                        act.activation(wqk[:, n // 2, 512 * (n % 2):512 * (n % 2 + 1)], pqk[n % 2][:],
                                       ACT.Copy, scale=LD ** -0.5).then_inc(s_cp, 1)

                @blk.vector
                def _(dve):
                    for p in range(NPAIR):
                        need(dve, s_vo, p + 1)
                        dve.tensor_copy(wvo[:, p, :], pvo[p % 2][:, 0:D]).then_inc(s_cv, 1)

        sm = Softmax(S, C, 4, True)
        xT = S.sb("xT", [P, KT, L])
        xtok = S.sb("xtok", [P, TT, D])
        kh = S.sb("kh", [P, L], R32)
        kl = S.sb("kl", [P, L], R32)
        latv = S.sb("latv", [P, TT, LD])
        qs = S.sb("qs", [P, 2, 2, L], R32)
        qlow = S.sb("qlow", [P, 2, L], R32)
        yT = S.sb("yT", [P, NPAIR, L])
        ln = LayerNorm(S, C, X, TT)
        ps_q, ps_y, ps_kv = S.ps("ps_q"), S.ps("ps_y"), S.ps("ps_kv")
        s_xT, s_xtok, s_qdma = S.sem("xT"), S.sem("xtok"), [
            [S.sem(f"qdma{p}{c}") for c in range(2)] for p in range(2)]
        s_lat, s_v, s_q, s_y, s_out = S.sem("lat"), S.sem("v"), S.sem("q"), S.sem("y"), S.sem("out", True)
        s_kh, s_latv, s_qhi, s_yc = S.sem("kh"), S.sem("latv"), S.sem("qhi"), S.sem("yc", True)
        s_kl, s_qlo = S.sem("kl"), S.sem("qlo")
        s_pass_sp = S.sem("pass_sp")
        LAG = 7
        NEXT, VALUES, OUT = H - 2, 4, {H + 4: (0, 1), H + 5: (2, 3)}

        with nc.Block() as blk:
            @blk.sync
            def _(sp):
                def load_x(b):
                    if not isinstance(b, int):
                        hold(sp, s_q, b * NPAIR, s_pass_sp)
                        hold(sp, s_v, b, s_pass_sp)
                    sp.dma_start(xT[:], A["xT"][bass.ds(b, 1), :, :].rearrange(
                        "o (k p) t -> p (o k) t", p=P)).then_inc(s_xT, 16)

                def load_tokens(b):
                    hold(sp, ln.s_sum, b * TT, s_pass_sp)
                    sp.dma_start(xtok[:], A["x"][bass.ds(b, 1), :, :].rearrange(
                        "o (t p) d -> p (o t) d", p=P)).then_inc(s_xtok, 16)

                def low_words(b, p):
                    for c in range(2):
                        hold(sp, s_qlo, b * (2 * NPAIR) + 2 * p + c + 1, s_pass_sp)
                        rows, to = slice(LD * c, LD * (c + 1)), slice(LD * (1 - c), LD * (2 - c))
                        sp.dma_start(qs[to, p % 2, c, :].bitcast(F32),
                                     qlow[rows, p % 2, :].bitcast(F32)).then_inc(s_qdma[p % 2][c], 16)

                def low_words_and_tokens(b):
                    for p in range(1, NPAIR):
                        low_words(b, p)
                        if p == 4:
                            load_tokens(b)

                load_x(0)
                low_words(0, 0)
                with sp.Fori(0, B - 1) as b:
                    low_words_and_tokens(b)
                    load_x(b + 1)
                    low_words(b + 1, 0)
                low_words_and_tokens(B - 1)

            @blk.tensor
            def _(pe):
                def project(b, p):
                    need(pe, s_qlo, b * (2 * NPAIR) + 2 * p)
                    for k in range(KT):
                        last = pe.matmul(ps_q[:], wqk[:, k, P * p:P * (p + 1)], xT[:, k, :],
                                         start=k == 0, stop=k == KT - 1)
                    last.then_inc(s_q, 1)

                def product(b, h, out, i, keys):
                    p = h // 2
                    if i == 0:
                        need(pe, s_qhi, b * (2 * NPAIR) + h + 1)
                        need(pe, s_qdma[p % 2][h % 2], b * (8 * NPAIR) + 16 * (p // 2 + 1))
                        if h == 0:
                            need(pe, s_kl, b + 1)
                    q = qs[:, p % 2, h % 2, P * i:P * (i + 1)]
                    pe.matmul(out, q, kh[:, 0:keys], start=True, stop=False)
                    return pe.matmul(out, q, kl[:, 0:keys], start=False, stop=True)

                def attend(b, p):
                    sm.need_probT(pe, b * H + 2 * p + 1)
                    need(pe, s_yc, b * NPAIR + p)
                    if p == 0:
                        need(pe, s_latv, b + 1)
                    for k in range(TT):
                        for c in range(2):
                            n = TCOL[k]
                            last = pe.matmul(ps_y[LD * c:LD * (c + 1), P * k:L], latv[:, k, :],
                                             sm.probT[:, (2 * p + c) % 4, n:n + L - P * k],
                                             start=k == 0, stop=k == TT - 1)
                    last.then_inc(s_y, 1)

                def values(b):
                    need(pe, s_yc, b * NPAIR)
                    for t in range(TT):
                        for k in range(KT):
                            last = pe.matmul(ps_y[:, LD * t:LD * (t + 1)], xT[:, k, P * t:P * (t + 1)],
                                             wdn2[:, k, 0, :], start=k == 0, stop=k == KT - 1)
                    last.then_inc(s_v, 1)

                def start(b):
                    need(pe, s_xT, b * 16 + 16)
                    need(pe, ln.s_sum, (b - 1) * TT)
                    for k in range(KT):
                        last = pe.matmul(ps_kv[:], wdn2[:, k, :, :], xT[:, k, :],
                                         start=k == 0, stop=k == KT - 1)
                    last.then_inc(s_lat, 1)
                    project(b, 0)

                def out(b, t):
                    if t == 0:
                        need(pe, s_yc, b * NPAIR + NPAIR)
                        if not (isinstance(b, int) and b == B - 1):
                            need(pe, s_kl, b + 2)
                    else:
                        need(pe, ln.s_sum, b * TT + t)
                    for p in range(NPAIR):
                        last = pe.matmul(ps_kv[:, 0:D], yT[:, p, P * t:P * (t + 1)],
                                         wvo[:, p, :], start=p == 0, stop=p == NPAIR - 1)
                    last.then_inc(s_out, 1)

                def slot(b, h):
                    def between():
                        if h % 2 == 0 and h + 2 < H:
                            project(b, h // 2 + 1)
                        if 5 <= h < H + 5 and h % 2:
                            attend(b, (h - 5) // 2)
                        if h == VALUES:
                            values(b)
                        if h == NEXT and not (isinstance(b, int) and b == B - 1):
                            start(b + 1)

                    sm.tensor_slot(pe, b, h, lambda *to: product(b, h, *to), between)
                    for t in OUT.get(h, ()):
                        out(b, t)

                start(0)
                start_at_one(pe, s_out)
                over_batches(slot, pe, LAG)

            @blk.scalar
            def _(act):
                def q_high(b, p):
                    need(act, s_q, b * NPAIR + p + 1)
                    act.activation(qs[0:LD, p % 2, 0, :], ps_q[0:LD, :], ACT.Copy).then_inc(s_qhi, 1)
                    act.activation(qs[LD:P, p % 2, 1, :], ps_q[LD:P, :], ACT.Copy).then_inc(s_qhi, 1)

                def values(b):
                    need(act, s_v, b + 1)
                    act.activation(latv[:], ps_y[:, 0:TT * LD].rearrange("p (t c) -> p t c", t=TT),
                                   ACT.Copy).then_inc(s_latv, 1)

                def keys(b):
                    need(act, s_lat, b + 1)
                    need(act, sm.s_score, b * (3 * H))
                    act.activation(kh[:], ps_kv[:], ACT.Copy).then_inc(s_kh, 1)

                def slot(b, h):
                    more = not (isinstance(b, int) and b == B - 1)
                    sm.scalar_slot(act, b, h)
                    if h % 2 == 0 and h + 2 < H:
                        q_high(b, h // 2 + 1)
                    if h == NEXT and more:
                        q_high(b + 1, 0)
                    if h == H - 1 and more:
                        keys(b + 1)
                    if 5 <= h < H + 5 and h % 2:
                        outputs(b, (h - 5) // 2)
                    if h == VALUES:
                        values(b)

                def outputs(b, p):
                    if p == 0:
                        need(act, s_out, b * TT)
                    need(act, s_y, b * NPAIR + p + 1)
                    act.activation(yT[:, p, :], ps_y[:], ACT.Copy).then_inc(s_yc, 1)

                keys(0)
                q_high(0, 0)
                start_at_one(act, sm.s_pt_act, s_yc)
                over_batches(slot, act, LAG)

            @blk.vector
            def _(dve):
                def q_low(b, p):
                    for c in range(2):
                        rows = slice(LD * c, LD * (c + 1))
                        need(dve, s_qhi, b * (2 * NPAIR) + 2 * p + c + 1)
                        dve.tensor_tensor(qlow[rows, p % 2, :], ps_q[rows, :],
                                          qs[rows, p % 2, c, :].bitcast(F32),
                                          ALU.subtract).then_inc(s_qlo, 1)

                def keys(b):
                    need(dve, s_kh, b + 1)
                    dve.tensor_tensor(kl[:], ps_kv[:], kh[:].bitcast(F32), ALU.subtract
                                      ).then_inc(s_kl, 1)

                def slot(b, h):
                    more = not (isinstance(b, int) and b == B - 1)
                    sm.vector_slot(dve, b, h)
                    if h % 2 == 0 and h + 2 < H:
                        q_low(b, h // 2 + 1)
                    if h == NEXT and more:
                        q_low(b + 1, 0)
                    if h == H - 1 and more:
                        keys(b + 1)
                    for t in OUT.get(h, ()):
                        if t == 0:
                            need(dve, s_xtok, b * 16 + 16)
                        need(dve, s_out, b * TT + t + 1)
                        ln.add(dve, b, t, ps_kv[:, 0:D], xtok[:, t, :])
                    if h == H + 6:
                        ln.write(dve, b)

                keys(0)
                q_low(0, 0)
                start_at_one(dve, ln.s_sum, ln.s_x, sm.s_pt_dve)
                over_batches(slot, dve, LAG)

            @blk.gpsimd
            def _(pool):
                for b in range(B):
                    meanwhile(pool, b)
                    ln.root(pool, b)


class LayerNorm:

    def __init__(self, S, C, X, n):
        self.C, self.X, self.n = C, X, n
        self.res = S.sb("res", [P, n, D])
        self.stats, self.mv, self.rstd = S.sb("stats", [P, n, 6]), S.sb("mv", [P, n, 2]), S.sb("rstd", [P, n])
        self.s_sum, self.s_x = S.sem("ln_sum", True), S.sem("ln_x", True)
        self.s_stat, self.s_mv, self.s_var, self.s_rstd, self.passed = (
            S.sem("ln_" + k) for k in ("stat", "mv", "var", "rstd", "pass"))
        self.passed_pool = S.sem("ln_pass_pool")

    def add(self, dve, b, t, u, v):
        if t == 0:
            need(dve, self.s_x, b * self.n)
        dve.tensor_tensor(self.res[:, t, :], u, v, ALU.add).then_inc(self.s_sum, 1)
        need(dve, self.s_sum, b * self.n + t + 1)
        self.statistics(dve, b, t)

    def statistics(self, dve, b, t):
        dve.bn_stats(self.stats[:, t, :], self.res[:, t, :]).then_inc(self.s_stat, 1)
        hold(dve, self.s_stat, b * self.n + t + 1, self.passed)
        dve.bn_aggr(self.mv[:, t, :], self.stats[:, t, :]).then_inc(self.s_mv, 1)

    def root(self, pool, b, at=0, n=None):
        n = n or self.n
        hold(pool, self.s_mv, b * n + n, self.passed_pool)
        rstd = self.rstd[:, at:at + n]
        pool.tensor_scalar(rstd, self.mv[:, at:at + n, 1], LN_EPS, None, ALU.add).then_inc(self.s_var, 1)
        hold(pool, self.s_var, b + 1, self.passed_pool)
        pool.tensor_tensor(rstd, rstd, self.C.minus_half[:, 0:n], ALU.pow).then_inc(self.s_rstd, 1)

    def write(self, dve, b):
        need(dve, self.s_rstd, b + 1)
        for t in range(self.n):
            dve.tensor_scalar(self.X[:, bass.ds(b * self.n + t, 1), :].rearrange("p o d -> p (o d)"),
                              self.res[:, t, :], self.mv[:, t, 0:1], self.rstd[:, t:t + 1],
                              ALU.subtract, ALU.mult).then_inc(self.s_x, 1)


NS = 80
SLOTS = NS * P
GT = 4
GL = GT * P
NG = NT // GT
NZ = 16


class Features:

    def __init__(self, S, C, X):
        self.C, self.X = C, X
        self.tok = [S.sb(f"tok{j}", [P, GT, D]) for j in range(2)]
        self.xs = [S.sb(f"xs{j}", [P, KT, GL]) for j in range(2)]
        self.ps = [S.ps(f"ps_turn{k}") for k in range(KT)]
        self.s_tok, self.s_turn, self.s_xs = S.sem("tok"), S.sem("turn"), S.sem("xs")
        self.passed = S.sem("tok_pass")

    def fetch(self, pool, g, j):
        if not isinstance(g, int) or g >= 2:
            hold(pool, self.s_turn, g * KT - KT, self.passed)
        pool.tensor_copy(self.tok[j][:], self.X[:, bass.ds(g * GT, GT), :]).then_inc(self.s_tok, 1)

    def turn(self, pe, g, j):
        need(pe, self.s_tok, g + 1)
        for k in range(KT):
            need(pe, self.s_xs, g * KT - KT + k + 1)
            for t in range(GT):
                last = pe.transpose(self.ps[k][:, P * t:P * (t + 1)],
                                    self.tok[j][:, t, P * k:P * (k + 1)], self.C.ident[:])
            last.then_inc(self.s_turn, 1)

    def keep(self, act, g, j):
        for k in range(KT):
            need(act, self.s_turn, g * KT + k + 1)
            act.activation(self.xs[j][:, k, :], self.ps[k][:], ACT.Copy).then_inc(self.s_xs, 1)


def in_twos(eng, n, step):
    step(0, 0)
    step(1, 1)
    with eng.Fori(1, n // 2) as r:
        for j in range(2):
            step(r * 2 + j, j)


class ExpertStore:

    def __init__(self, nc, ctx):
        S = Held(nc, ctx, "es")
        self.wgu = S.sb("wgu", [P, E, KT * 2 * I])
        self.wd = S.sb("wd", [I, E, D])
        self.shared_gu, self.shared_d = S.sb("shared_gu", [P, KT, 2, I]), S.sb("shared_d", [I, D])
        self.gate, self.bias = S.sb("gate", [P, KT, E]), S.sb("bias", [P, E])
        self.iota, self.tiota = S.sb("iota", [P, E]), S.sb("tiota", [P, NS])
        self.before = S.sb("before", [P, P])
        self.thr = S.sb("thr", [P, 32])
        self.lower = S.sb("lower", [P, E, E])
        self.zero = S.sb("zero", [P, D])
        self.s_w, self.s_small, self.s_z, self.s_zero = (S.sem(n) for n in ("w", "small", "z", "zero"))
        self.Z = nc.dram_tensor("slot_in", (SLOTS, D), F32).ap()
        self.Y = nc.dram_tensor("slot_out", (SLOTS, D), F32).ap()

    def part(self, pool, A, b):
        if b == 0:
            pool.memset(self.zero[:], 0.0).then_inc(self.s_zero, 1)
            small = [(self.gate[:], A["gate_w"].rearrange("(k p) e -> p k e", p=P)),
                     (self.shared_gu[:, :, 0, :], A["swg"].rearrange("(k p) i -> p k i", p=P)),
                     (self.shared_gu[:, :, 1, :], A["swu"].rearrange("(k p) i -> p k i", p=P)),
                     (self.shared_d[:], A["swd"]), (self.bias[:], A["gate_b"]),
                     (self.iota[:], A["iota"]), (self.tiota[:], A["tiota"]),
                     (self.before[:], A["before"]), (self.thr[:], A["thr"]),
                     (self.lower[:], A["lower"])]
            for dst, src in small:
                pool.dma_start(dst, src).then_inc(self.s_small, 16)
            self.small = 16 * len(small)
            need(pool, self.s_zero, 1)
        wgu = self.wgu[:].rearrange("p e (k c i) -> p e k c i", k=KT, c=2)
        for e in range(b * E // B, (b + 1) * E // B):
            for c, src in enumerate(("ewg", "ewu")):
                pool.dma_start(wgu[:, e, :, c, :], A[src][e].rearrange("(k p) i -> p k i", p=P)
                               ).then_inc(self.s_w, 16)
            pool.dma_start(self.wd[:, e, :], A["ewd"][e]).then_inc(self.s_w, 16)
        for n in range(b * NZ // B, (b + 1) * NZ // B):
            rows = self.Z[bass.ts(n, SLOTS // NZ), :].rearrange("(a p) d -> p a d", p=P)
            pool.dma_start(rows, self.zero[:].unsqueeze(1).to_broadcast([P, NS // NZ, D])
                           ).then_inc(self.s_z, 16)

    def ready(self, eng):
        need(eng, self.s_w, 16 * 3 * E)
        need(eng, self.s_z, 16 * NZ)


def logits_of(nc, X, xs_all, logits, C, ES):
    with ExitStack() as ctx:
        S = Held(nc, ctx, "m1")
        F = Features(S, C, X)
        ps_gate = S.ps("ps_gate")
        s_gate, s_log, s_all = S.sem("gate"), S.sem("log"), S.sem("all")
        with nc.Block() as blk:
            @blk.tensor
            def _(pe):
                need(pe, ES.s_small, ES.small)

                def logits_of_group(g, j):
                    need(pe, F.s_xs, g * KT + KT)
                    need(pe, s_log, g)
                    for t in range(GT):
                        for k in range(KT):
                            last = pe.matmul(ps_gate[:, E * t:E * (t + 1)],
                                             F.xs[j][:, k, P * t:P * (t + 1)], ES.gate[:, k, :],
                                             start=k == 0, stop=k == KT - 1)
                    last.then_inc(s_gate, 1)

                F.turn(pe, 0, 0)
                F.turn(pe, 1, 1)
                logits_of_group(0, 0)
                with pe.Fori(1, NG // 2) as r:
                    for j in range(2):
                        F.turn(pe, r * 2 + j, j)
                        logits_of_group(r * 2 + j - 1, 1 - j)
                logits_of_group(NG - 1, 1)

            @blk.scalar
            def _(act):
                def step(g, j):
                    if not isinstance(g, int) or g >= 2:
                        need(act, s_gate, g - 1)
                        need(act, s_all, g - 1)
                    F.keep(act, g, j)

                def keep_logits(g):
                    need(act, s_gate, g + 1)
                    act.activation(logits[:, bass.ds(g * GT, GT), :],
                                   ps_gate[:, 0:GT * E].rearrange("p (t e) -> p t e", e=E),
                                   ACT.Copy).then_inc(s_log, 1)

                step(0, 0)
                step(1, 1)
                keep_logits(0)
                with act.Fori(1, NG // 2) as r:
                    for j in range(2):
                        step(r * 2 + j, j)
                        keep_logits(r * 2 + j - 1)
                keep_logits(NG - 1)

            @blk.vector
            def _(dve):
                F.fetch(dve, 0, 0)

                def step(g, j):
                    if not isinstance(g, int) or g < NG - 1:
                        F.fetch(dve, g + 1, 1 - j)
                    need(dve, F.s_xs, g * KT + KT)
                    dve.tensor_copy(xs_all[:, :, bass.ds(g * GL, GL)], F.xs[j][:]).then_inc(s_all, 1)

                step(0, 0)
                step(1, 1)
                with dve.Fori(1, NG // 2 - 1) as r:
                    for j in range(2):
                        step(r * 2 + j, j)
                step(NG - 2, 0)
                step(NG - 1, 1)


def shared_expert(nc, X, xs_all, base, slot, ES):
    with ExitStack() as ctx:
        S = Held(nc, ctx, "m2")
        wgu, wd = ES.shared_gu, ES.shared_d
        act_g = [S.sb(f"act{j}", [I, GL]) for j in range(2)]
        hid = [S.sb(f"hid{j}", [I, GL]) for j in range(2)]
        ps_g, ps_u = ([S.ps(f"{n}{j}") for j in range(2)] for n in ("ps_g", "ps_u"))
        ps_d = [S.ps("ps_d0"), S.ps("ps_d1")]
        s_scatter, s_gu, s_down = S.sem("scatter"), S.sem("gu"), S.sem("down")
        s_silu, s_hid, s_base = S.sem("silu"), S.sem("hid"), S.sem("base")
        with nc.Block() as blk:
            @blk.gpsimd
            def _(pool):
                ES.ready(pool)
                for t in range(NT):
                    for c in range(2):
                        pool.indirect_dma_start(
                            ES.Z, bass.IndirectOffsetOnAxis(slot[:, t, c:c + 1], 0), X[:, t, :], None
                        ).then_inc(s_scatter, 16)
                need(pool, s_scatter, 16 * 2 * NT)

            @blk.tensor
            def _(pe):
                need(pe, ES.s_small, ES.small)

                def up(g, j):
                    if not isinstance(g, int) or g >= 2:
                        need(pe, s_hid, g - 1)
                    for c, ps in enumerate((ps_g[j], ps_u[j])):
                        for k in range(KT):
                            last = pe.matmul(ps[:], wgu[:, k, c, :], xs_all[:, k, bass.ds(g * GL, GL)],
                                             start=k == 0, stop=k == KT - 1)
                        last.then_inc(s_gu, 1)

                def down(g, j):
                    need(pe, s_hid, g + 1)
                    for t in range(GT):
                        if t % 2 == 0:
                            need(pe, s_base, g * 2 + t // 2 - 1)
                        last = pe.matmul(ps_d[t // 2][:, D * (t % 2):D * (t % 2 + 1)],
                                         hid[j][:, P * t:P * (t + 1)], wd[:], start=True, stop=True)
                        if t % 2:
                            last.then_inc(s_down, 1)

                up(0, 0)
                up(1, 1)
                down(0, 0)
                with pe.Fori(1, NG // 2) as r:
                    for j in range(2):
                        up(r * 2 + j, j)
                        down(r * 2 + j - 1, 1 - j)
                down(NG - 1, 1)

            @blk.scalar
            def _(act):
                def step(g, j):
                    need(act, s_gu, g * 2 + 1)
                    if not isinstance(g, int) or g >= 2:
                        need(act, s_hid, g - 1)
                    act.activation(act_g[j][:], ps_g[j][:], ACT.Silu).then_inc(s_silu, 1)

                in_twos(act, NG, step)

            @blk.vector
            def _(dve):
                def hidden(g, j):
                    need(dve, s_silu, g + 1)
                    need(dve, s_gu, g * 2 + 2)
                    if not isinstance(g, int) or g >= 2:
                        need(dve, s_down, g * 2 - 2)
                    dve.tensor_tensor(hid[j][:], act_g[j][:], ps_u[j][:], ALU.mult).then_inc(s_hid, 1)

                def add(g):
                    for c in range(2):
                        need(dve, s_down, g * 2 + c + 1)
                        tiles = bass.ds(g * GT + 2 * c, 2)
                        dve.scalar_tensor_tensor(
                            base[:, tiles, :], X[:, tiles, :], 2.0,
                            ps_d[c][:].rearrange("p (t d) -> p t d", d=D), ALU.mult, ALU.add
                        ).then_inc(s_base, 1)

                hidden(0, 0)
                hidden(1, 1)
                add(0)
                with dve.Fori(1, NG // 2) as r:
                    for j in range(2):
                        hidden(r * 2 + j, j)
                        add(r * 2 + j - 1)
                add(NG - 1)


def route(nc, logits, slot, weight, tile_expert, ES):
    with ExitStack() as ctx:
        S = Held(nc, ctx, "mr")
        bias, iota, tiota, before, thr, lower = (
            ES.bias, ES.iota, ES.tiota, ES.before, ES.thr, ES.lower)
        ones = S.sb("ones", [P, P])
        sig = S.sb("sig", [P, NT, E])
        top = S.sb("top", [P, NT, 8])
        tidx = S.sb("tidx", [P, NT, 8], U32)
        idx = S.sb("idx", [P, NT, 2])
        total = S.sb("total", [P, NT])
        hot = [S.sb(f"hot{c}", [P, NT, E]) for c in range(2)]
        count = S.sb("count", [P, NT, E])
        scan = [S.sb("scan0", [P, NT, E]), S.sb("scan1", [P, NT, E])]
        pos = S.sb("pos", [P, NT, E])
        big = S.sb("big", [P, E, 32])
        prod = S.sb("prod", [P, E, E])
        tiles, first, after = S.sb("tiles", [P, E]), S.sb("first", [P, E]), S.sb("after", [P, E])
        cmp = S.sb("cmp", [P, NS, E])
        te = S.sb("te", [P, NS])
        slotf = S.sb("slotf", [P, NT, 2])
        ps_rank, ps_tot = S.ps("ps_rank"), S.ps("ps_tot")
        s_sig, s_ps, s_v, s_bias, s_c = (S.sem(n) for n in ("sig", "ps", "v", "bias", "c"))
        with nc.Block() as blk:
            @blk.scalar
            def _(act):
                need(act, s_bias, 1)
                act.activation(sig[:], sig[:], ACT.Sigmoid).then_inc(s_sig, 1)

            @blk.tensor
            def _(pe):
                need(pe, ES.s_small, ES.small)
                need(pe, s_c, 1)
                c = count[:].rearrange("p t e -> p (t e)")
                pe.matmul(ps_rank[:], before[:], c, start=True, stop=True)
                pe.matmul(ps_tot[:], ones[:], c, start=True, stop=True).then_inc(s_ps, 1)

            @blk.vector
            def _(dve):
                done = [0]

                def do(ins):
                    done[0] += 1
                    ins.then_inc(s_v, 1)
                    need(dve, s_v, done[0])

                def over_e(ap):
                    return ap.unsqueeze(2).to_broadcast([P, NT, E])

                need(dve, ES.s_small, ES.small)
                do(dve.memset(ones[:], 1.0))
                dve.tensor_tensor(sig[:], logits[:], bias[:].unsqueeze(1).to_broadcast([P, NT, E]),
                                  ALU.add).then_inc(s_bias, 1)
                need(dve, s_sig, 1)
                for t in range(NT):
                    dve.max(top[:, t, :], sig[:, t, :]).then_inc(s_v, 1)
                done[0] += NT
                need(dve, s_v, done[0])
                for t in range(NT):
                    dve.max_index(tidx[:, t, :], top[:, t, :], sig[:, t, :]).then_inc(s_v, 1)
                done[0] += NT
                need(dve, s_v, done[0])
                do(dve.tensor_tensor(total[:], top[:, :, 0], top[:, :, 1], ALU.add))
                do(dve.reciprocal(total[:], total[:]))
                do(dve.tensor_tensor(weight[:], top[:, :, 0:2],
                                     total[:].unsqueeze(2).to_broadcast([P, NT, 2]), ALU.mult))
                do(dve.tensor_copy(idx[:], tidx[:, :, 0:2]))
                for c in range(2):
                    do(dve.tensor_tensor(hot[c][:], iota[:].unsqueeze(1).to_broadcast([P, NT, E]),
                                         over_e(idx[:, :, c]), ALU.is_equal))
                dve.tensor_tensor(count[:], hot[0][:], hot[1][:], ALU.add).then_inc(s_c, 1)
                need(dve, s_ps, 1)
                tot = ps_tot[:].rearrange("p (t e) -> p t e", e=E)
                do(dve.tensor_copy(scan[0][:], tot))
                n, d = 0, 1
                while d < NT:
                    do(dve.tensor_copy(scan[1 - n][:, 0:d, :], scan[n][:, 0:d, :]))
                    do(dve.tensor_tensor(scan[1 - n][:, d:NT, :], scan[n][:, d:NT, :],
                                         scan[n][:, 0:NT - d, :], ALU.add))
                    n, d = 1 - n, 2 * d
                run = scan[n]
                do(dve.tensor_tensor(big[:], run[:, NT - 1, :].unsqueeze(2).to_broadcast([P, E, 32]),
                                     thr[:].unsqueeze(1).to_broadcast([P, E, 32]), ALU.is_gt))
                do(dve.tensor_reduce(tiles[:], big[:], AX.X, ALU.add))
                do(dve.tensor_tensor(prod[:], tiles[:].unsqueeze(1).to_broadcast([P, E, E]), lower[:],
                                     ALU.mult))
                do(dve.tensor_reduce(first[:], prod[:], AX.X, ALU.add))
                do(dve.tensor_tensor(after[:], first[:], tiles[:], ALU.add))
                do(dve.tensor_tensor(cmp[:], tiota[:].unsqueeze(2).to_broadcast([P, NS, E]),
                                     after[:].unsqueeze(1).to_broadcast([P, NS, E]), ALU.is_ge))
                do(dve.tensor_reduce(te[:], cmp[:], AX.X, ALU.add))
                do(dve.tensor_scalar(te[:], te[:], float(E - 1), None, ALU.min))
                do(dve.tensor_copy(tile_expert[:], te[0:1, :]))
                do(dve.tensor_tensor(pos[:], run[:], tot, ALU.subtract))
                do(dve.tensor_tensor(pos[:], pos[:], ps_rank[:].rearrange("p (t e) -> p t e", e=E),
                                     ALU.add))
                do(dve.tensor_scalar(first[:], first[:], float(P), None, ALU.mult))
                do(dve.tensor_tensor(pos[:], pos[:], first[:].unsqueeze(1).to_broadcast([P, NT, E]),
                                     ALU.add))
                for c in range(2):
                    do(dve.tensor_tensor(hot[c][:], hot[c][:], pos[:], ALU.mult))
                    do(dve.tensor_reduce(slotf[:, :, c], hot[c][:], AX.X, ALU.add))
                do(dve.tensor_copy(slot[:], slotf[:]))


def experts(nc, tile_expert, C, ES):
    Z, Y, wgu, wd = ES.Z, ES.Y, ES.wgu, ES.wd
    with ExitStack() as ctx:
        S = Held(nc, ctx, "m3")
        R, AHEAD = 8, 4
        z = [S.sb(f"z{r}", [P, D]) for r in range(R)]
        y = [S.sb(f"y{r}", [P, D]) for r in range(R)]
        zT = [S.sb(f"zT{r}", [P, KT, P]) for r in range(2)]
        gact = [S.sb(f"gact{r}", [P, I]) for r in range(2)]
        hid = [S.sb(f"hid{r}", [P, I]) for r in range(2)]
        hidT = [S.sb(f"hidT{r}", [I, P]) for r in range(2)]
        ps_zT, ps_gu, ps_hT, ps_y = ([S.ps(f"{n}{r}") for r in range(2)]
                                     for n in ("ps_zT", "ps_gu", "ps_hT", "ps_y"))
        s_z, s_out = [S.sem(f"z{r}") for r in range(R)], [S.sem(f"out{r}") for r in range(R)]
        s_zT, s_zTc, s_gu, s_silu, s_hid, s_hT, s_hTc, s_y, s_yc, s_pass = (
            S.sem(n) for n in ("zT", "zTc", "gu", "silu", "hid", "hT", "hTc", "y", "yc", "pass"))

        def walk(eng, slot, first=0, last=NS + 3):
            for n in range(first, R):
                slot(n, n // R, n % R)
            with eng.Fori(1, NS // R - 1) as q:
                for r in range(R):
                    slot(q * R + r, q, r)
            for n in range(NS - R, last):
                slot(n, n // R, n % R)

        def within(n, back=0):
            return not isinstance(n, int) or back <= n < NS + back

        with nc.Block() as blk:
            @blk.sync
            def _(sp):
                def load(n, q, r):
                    need(sp, s_zT, n - R + 1)
                    if not isinstance(n, int) or n >= R:
                        sp.sem_inc(s_pass, 1)
                    sp.dma_start(z[r][:], Z[bass.ds(n * P, P), :]).then_inc(s_z[r], 16)

                def slot(n, q, r):
                    if not isinstance(n, int) or n + AHEAD < NS:
                        load(n + AHEAD, q + (r + AHEAD) // R, (r + AHEAD) % R)
                    if within(n, AHEAD):
                        m = n - AHEAD
                        hold(sp, s_yc, m + 1, s_pass)
                        sp.dma_start(Y[bass.ds(m * P, P), :], y[(r - AHEAD) % R][:]
                                     ).then_inc(s_out[(r - AHEAD) % R], 16)

                for n in range(AHEAD):
                    load(n, 0, n)
                walk(sp, slot, last=NS + AHEAD)
                for r in range(R):
                    need(sp, s_out[r], NS // R * 16)

            @blk.tensor
            def _(pe):
                def expert_of(m):
                    return pe.value_load(tile_expert[0:1, bass.ds(m, 1)], min_val=0, max_val=E - 1)

                def slot(n, q, r):
                    e_down = None
                    if within(n, 3):
                        e_down = kept[r - 2] if r >= 2 else expert_of(n - 3)
                    e_up = kept[r] = expert_of(n - 1) if within(n, 1) else None
                    if within(n):
                        j = r % 2
                        need(pe, s_z[r], q * 16 + 16)
                        need(pe, s_zTc, n - 1)
                        for k in range(KT):
                            last = pe.transpose(ps_zT[j][:, P * k:P * (k + 1)],
                                                z[r][:, P * k:P * (k + 1)], C.ident[:])
                        last.then_inc(s_zT, 1)
                    if within(n, 1):
                        m, j = n - 1, (r - 1) % 2
                        need(pe, s_zTc, m + 1)
                        need(pe, s_hid, m - 1)
                        for k in range(KT):
                            last = pe.matmul(ps_gu[j][:, 0:2 * I], zT[j][:, k, :],
                                             wgu[:, bass.ds(e_up, 1), 2 * I * k:2 * I * (k + 1)],
                                             start=k == 0, stop=k == KT - 1)
                        last.then_inc(s_gu, 1)
                    if within(n, 2):
                        m, j = n - 2, r % 2
                        need(pe, s_hid, m + 1)
                        need(pe, s_hTc, m - 1)
                        pe.transpose(ps_hT[j][:, 0:P], hid[j][:], C.ident[:]).then_inc(s_hT, 1)
                    if within(n, 3):
                        m, j = n - 3, (r - 3) % 2
                        need(pe, s_hTc, m + 1)
                        need(pe, s_yc, m - 1)
                        pe.matmul(ps_y[j][:, 0:D], hidT[j][:], wd[:, bass.ds(e_down, 1), :],
                                  start=True, stop=True).then_inc(s_y, 1)

                kept = {}
                ES.ready(pe)
                walk(pe, slot)

            @blk.scalar
            def _(act):
                def slot(n, q, r):
                    if within(n):
                        j = r % 2
                        need(act, s_zT, n + 1)
                        need(act, s_gu, n - 1)
                        act.activation(zT[j][:], ps_zT[j][:, 0:D].rearrange("p (k t) -> p k t", k=KT),
                                       ACT.Copy).then_inc(s_zTc, 1)
                    if within(n, 1):
                        m, j = n - 1, (r - 1) % 2
                        need(act, s_gu, m + 1)
                        need(act, s_hid, m - 1)
                        act.activation(gact[j][:], ps_gu[j][:, 0:I], ACT.Silu).then_inc(s_silu, 1)

                walk(act, slot)

            @blk.vector
            def _(dve):
                def slot(n, q, r):
                    if within(n, 1):
                        m, j = n - 1, (r - 1) % 2
                        need(dve, s_silu, m + 1)
                        need(dve, s_hT, m - 1)
                        dve.tensor_tensor(hid[j][:], gact[j][:], ps_gu[j][:, I:2 * I], ALU.mult
                                          ).then_inc(s_hid, 1)
                    if within(n, 2):
                        m, j = n - 2, r % 2
                        need(dve, s_hT, m + 1)
                        need(dve, s_y, m - 1)
                        dve.tensor_copy(hidT[j][:], ps_hT[j][:, 0:P]).then_inc(s_hTc, 1)
                    if within(n, 3):
                        m, j = n - 3, (r - 3) % 2
                        rm = (r - 3) % R
                        need(dve, s_y, m + 1)
                        if not isinstance(m, int):
                            need(dve, s_out[rm], q * 16 - 16 if r < 3 else q * 16)
                        elif m >= R:
                            need(dve, s_out[rm], m // R * 16)
                        dve.tensor_copy(y[rm][:], ps_y[j][:, 0:D]).then_inc(s_yc, 1)

                walk(dve, slot)


def combine(nc, X, base, slot, weight, C, Y):
    with ExitStack() as ctx:
        S = Held(nc, ctx, "m4")
        R = 3
        CT = 2 * GT
        g = [S.sb(f"g{r}", [P, 2, GT, D]) for r in range(R)]
        ln = LayerNorm(S, C, X, NT)
        s_g = [S.sem(f"g{r}") for r in range(R)]
        s_mix = S.sem("mix")
        with nc.Block() as blk:
            @blk.gpsimd
            def _(pool):
                for q in range(NG):
                    if q >= R:
                        need(pool, s_mix, 2 * GT * (q - R + 1))
                    for t in range(GT):
                        for c in range(2):
                            pool.indirect_dma_start(
                                g[q % R][:, c, t, :], None, Y,
                                bass.IndirectOffsetOnAxis(slot[:, q * GT + t, c:c + 1], 0)
                            ).then_inc(s_g[q % R], 16)
                    if q >= 3 and q % 2:
                        ln.root(pool, (q - 3) // 2, (q - 3) // 2 * CT, CT)
                ln.root(pool, NT // CT - 1, NT - CT, CT)

            @blk.vector
            def _(dve):
                def normed(k):
                    need(dve, ln.s_rstd, k + 1)
                    for n in range(k * CT, k * CT + CT):
                        dve.tensor_scalar(X[:, n, :], base[:, n, :], ln.mv[:, n, 0:1],
                                          ln.rstd[:, n:n + 1], ALU.subtract, ALU.mult).then_inc(ln.s_x, 1)

                start_at_one(dve, ln.s_x)
                for q in range(NG):
                    need(dve, s_g[q % R], 16 * 2 * GT * (q // R + 1))
                    for t in range(GT):
                        n = q * GT + t
                        for c in range(2):
                            dve.scalar_tensor_tensor(base[:, n, :], g[q % R][:, c, t, :],
                                                     weight[:, n, c:c + 1], base[:, n, :], ALU.mult,
                                                     ALU.add).then_inc(s_mix, 1)
                            need(dve, s_mix, 2 * n + c + 1)
                        dve.bn_stats(ln.stats[:, n, :], base[:, n, :]).then_inc(ln.s_stat, 1)
                        need(dve, ln.s_stat, n + 1)
                        dve.bn_aggr(ln.mv[:, n, :], ln.stats[:, n, :]).then_inc(ln.s_mv, 1)
                    if q >= 4 and q % 2 == 0:
                        normed(q // 2 - 2)
                normed(NT // CT - 2)
                normed(NT // CT - 1)
                need(dve, ln.s_x, NT)


def layer0_experts(nc, X, ES, C):
    with ExitStack() as ctx:
        S = Held(nc, ctx, "m")
        base = S.sb("base", [P, NT, D])
        logits = S.sb("logits", [P, NT, E])
        slot = S.sb("slot", [P, NT, 2], U32)
        weight = S.sb("weight", [P, NT, 2])
        tile_expert = S.sb("tile_expert", [1, NS], U32)
        with ExitStack() as xctx:
            xs_all = Held(nc, xctx, "mx").sb("xs", [P, KT, NT * P])
            logits_of(nc, X, xs_all, logits, C, ES)
            route(nc, logits, slot, weight, tile_expert, ES)
            shared_expert(nc, X, xs_all, base, slot, ES)
        experts(nc, tile_expert, C, ES)
        combine(nc, X, base, slot, weight, C, ES.Y)


HH = 8
SQ, SK, SV, SG = range(4)
HV = 32
QUAD = 4


def fold_layer1(nc, C, A):
    w = C.sb("w", [P, 4, P])
    qk_norm = C.sb("qk_norm", [P, 2])
    mean8 = C.sb("mean8", [P, HH])
    with ExitStack() as ctx:
        W = Held(nc, ctx, "a1w")
        wdq, wuqT = W.sb("wdq", [P, P]), W.sb("wuqT", [P, P])
        wdkv, wukT, wuvT = W.sb("wdkv", [P, 2, P]), W.sb("wukT", [P, 2, P]), W.sb("wuvT", [P, 2, HD])
        wkr, wqr = W.sb("wkr", [64, P]), W.sb("wqr", [64, P])
        woT, vc, block = W.sb("woT", [HD, P]), W.sb("vc", [HD, P]), W.sb("block", [P, P])
        ps = [W.ps(f"ps{i}") for i in range(5)]
        s_w, s_p, s_c, s_v = W.sem("w"), W.sem("p"), W.sem("c"), W.sem("v")
        with nc.Block() as blk:
            @blk.sync
            def _(sp):
                loads = [(wdq[:], A["wdq"]), (wuqT[:], A["wuqT"]),
                         (wdkv[:], A["wdkv"].rearrange("(c p) d -> p c d", p=P)),
                         (wukT[:], A["wukT"].rearrange("(c p) d -> p c d", p=P)),
                         (wuvT[:], A["wuvT"].rearrange("(c p) d -> p c d", p=P)),
                         (wkr[:], A["wkr"]), (wqr[:], A["wqr"]), (woT[:], A["woT"]),
                         (block[:], A["block"]), (qk_norm[:], A["qk_norm"]), (mean8[:], A["mean8"])]
                for dst, src in loads:
                    sp.dma_start(dst, src).then_inc(s_w, 16)
                need(sp, s_w, 16 * len(loads))

            @blk.tensor
            def _(pe):
                need(pe, s_w, 16 * 11)
                pe.matmul(ps[0][:, 0:P], wdq[:], wuqT[:], start=True, stop=True).then_inc(s_p, 1)
                for c in range(2):
                    last = pe.matmul(ps[1][:, 0:P], wdkv[:, c, :], wukT[:, c, :], start=c == 0, stop=c == 1)
                last.then_inc(s_p, 1)
                pe.matmul(ps[2][:, 0:P], wkr[:], wqr[:], start=True, stop=True).then_inc(s_p, 1)
                for c in range(2):
                    last = pe.matmul(ps[3][0:HD, 0:P], wuvT[:, c, :], wdkv[:, c, :], start=c == 0, stop=c == 1)
                last.then_inc(s_p, 1)
                need(pe, s_v, 1)
                pe.matmul(ps[4][:, 0:P], vc[:], woT[:], start=True, stop=True).then_inc(s_p, 1)

            @blk.vector
            def _(dve):
                need(dve, s_w, 16 * 11)
                dve.tensor_scalar(qk_norm[:, 0:1], qk_norm[:, 0:1], HD ** -0.5, None, ALU.mult
                                  ).then_inc(s_c, 1)
                for n, (bank, to) in enumerate(((0, SQ), (1, SK), (2, SG))):
                    need(dve, s_p, n + 1)
                    dve.tensor_tensor(w[:, to, :], ps[bank][:, 0:P], block[:], ALU.mult).then_inc(s_c, 1)
                need(dve, s_p, 4)
                dve.tensor_copy(vc[:], ps[3][0:HD, 0:P]).then_inc(s_v, 1)
                need(dve, s_p, 5)
                dve.tensor_tensor(w[:, SV, :], ps[4][:, 0:P], block[:], ALU.mult).then_inc(s_c, 1)
    return w, qk_norm, mean8


def layer1_attention(nc, X, folded, C, A):
    bounce = nc.dram_tensor("bounce", (2, 4, P, L), F32).ap()
    with ExitStack() as ctx:
        S = Held(nc, ctx, "a1")
        w, qk_norm, mean8 = folded
        sm = Softmax(S, C, 2 * QUAD, False)
        tok = S.sb("tok", [P, TT, D])
        xs = [S.sb(f"xs{k}", [P, L]) for k in range(KT)]
        raw = S.sb("raw", [P, 2, L])
        sq = S.sb("sq", [P, 2, L])
        ms = S.sb("ms", [P, 2, TT, HH])
        roots = S.sb("roots", [P, 2, TT, P])
        fin = sq
        words = [S.sb(f"words{m}", [P, L], R32) for m in range(4)]
        QS = [S.sb(f"qs{k}", [P, HH, L], R32) for k in range(KT)]
        KS = [S.sb(f"ks{k}", [P, HH, L], R32) for k in range(KT)]
        V = [S.sb(f"v{k}", [P, TT, HH, HV]) for k in range(KT)]
        yq = S.sb("yq", [P, L])
        part = S.sb("part", [P, TT, QUAD, HD])
        LAG = 7
        ln = LayerNorm(S, C, X, TT)
        ps_a, ps_b, ps_y = S.ps("ps_a"), S.ps("ps_b"), S.ps("ps_y")
        s_tok, s_turn, s_xs = S.sem("tok"), S.sem("turn"), S.sem("xs")
        s_zero, s_vzero = S.sem("zero"), S.sem("vzero")
        s_v, s_vc, s_raw, s_sq, s_rawc = S.sem("v"), S.sem("vc"), S.sem("raw"), S.sem("sq"), S.sem("rawc")
        s_ms, s_msc, s_root, s_g, s_bc, s_fin = (S.sem(n) for n in ("ms", "msc", "root", "g", "bc", "fin"))
        s_wide, s_kn, s_hi, s_lo, s_wr, s_rd = (S.sem(n) for n in ("wide", "kn", "hi", "lo", "wr", "rd"))
        s_wrs = [S.sem("wr0"), S.sem("wr1")]
        s_rds = [S.sem("rd0"), S.sem("rd1")]
        s_y, s_yc, s_yt, s_part = S.sem("y", True), S.sem("yc"), S.sem("yt"), S.sem("part")
        s_pass_sp, s_pass_pool = S.sem("pass_sp"), S.sem("pass_pool")

        def walk(slot, eng):
            for step in range(8):
                slot(0, -16, (0, 0, step), (0, 0) if step == 2 else None)
            for step in range(4):
                slot(0, -16, (0, 1, step), None)

            def both(b, h):
                front, values = None, None
                more = not (isinstance(b, int) and b == B - 1)
                if h < 4:
                    front = (b, 1, h + 4)
                elif h < 12 and more:
                    front = (b + 1, 0, h - 4)
                elif h < H and more:
                    front = (b + 1, 1, h - 12)
                if h == 5:
                    values = (b, 1)
                elif h == 13 and more:
                    values = (b + 1, 0)
                slot(b, h, front, values)

            over_batches(both, eng, LAG, 2)

        with nc.Block() as blk:
            @blk.sync
            def _(sp):
                def front(b, k, step):
                    if step != 7:
                        return
                    f = b * 2 + k
                    for m, when in ((0, s_hi), (1, s_lo), (2, s_hi), (3, s_lo)):
                        hold(sp, when, f * 2 + m // 2 + 1, s_pass_sp)
                        sp.dma_start(bounce[k, m], words[m][:].bitcast(F32)).then_inc(s_wrs[k], 16)
                    hold(sp, s_wrs[k], b * 64 + 64, s_pass_sp)
                    for c in range(4):
                        rows = slice(HD * c, HD * (c + 1))
                        for buf, m in ((QS[k], c % 2), (KS[k], 2 + c // 2)):
                            sp.dma_start(buf[rows, :, :].bitcast(F32),
                                         bounce[k, m].rearrange("(h d) t -> d h t", d=HD)
                                         ).then_inc(s_rds[k], 16)

                walk(lambda b, h, f, v: f and front(*f), sp)

            @blk.gpsimd
            def _(pool):
                def fetch(b):
                    pool.tensor_copy(tok[:], X[:, bass.ds(b * TT, TT), :]).then_inc(s_tok, 1)

                def front(b, k, step):
                    f = b * 2 + k
                    if step in (2, 3):
                        a, n = step - 2, f * 2 + step - 2
                        hold(pool, s_msc, n + 1, s_pass_pool)
                        at = ms[:, a, :, :].rearrange("p t h -> p (t h)")
                        pool.tensor_tensor(at, at, C.minus_half[:, 0:TT * HH], ALU.pow
                                           ).then_inc(s_root, 1)
                        hold(pool, s_root, n + 1, s_pass_pool)
                        if a or not (isinstance(b, int) and b == 0 and k == 0):
                            hold(pool, s_bc, n - 1, s_pass_pool)
                        pool.tensor_copy(roots[:, a, :, :].rearrange("p t (h d) -> p t h d", d=HD),
                                         ms[:, a, :, :].unsqueeze(3).to_broadcast([P, TT, HH, HD])
                                         ).then_inc(s_wide, 1)

                    if step in (6, 7):
                        n = f * 2 + step - 6
                        hold(pool, s_hi, n + 1, s_pass_pool)
                        m = 2 * (step - 6)
                        pool.tensor_tensor(words[m + 1][:], fin[:, step - 6, :],
                                           words[m][:].bitcast(F32), ALU.subtract).then_inc(s_lo, 1)

                def slot(b, h, f, v):
                    if h == 0 and not (isinstance(b, int) and b == B - 1):
                        hold(pool, s_turn, b * 2 + 2, s_pass_pool)
                        fetch(b + 1)
                    if f:
                        front(*f)
                    if h == H + 5:
                        ln.root(pool, b)

                fetch(0)
                for k in range(KT):
                    pool.memset(V[k][:], 0.0).then_inc(s_vzero, 1)
                    need(pool, s_vzero, k + 1)
                walk(slot, pool)

            @blk.tensor
            def _(pe):
                def front(b, k, step):
                    f = b * 2 + k
                    if step == 0:
                        need(pe, s_tok, b + 1)
                        need(pe, s_fin, f * 2)
                        for t in range(TT):
                            last = pe.transpose(ps_a[:, P * t:P * (t + 1)], tok[:, t, P * k:P * (k + 1)],
                                                C.ident[:])
                        last.then_inc(s_turn, 1)
                    elif step == 1:
                        need(pe, s_xs, f + 1)
                        need(pe, s_kn, f * 2)
                        pe.matmul(ps_b[:], w[:, SQ, :], xs[k][:], start=True, stop=True).then_inc(s_raw, 1)
                    elif step in (2, 3):
                        a = step - 2
                        need(pe, s_rawc, f * 2 + a + 1)
                        pe.matmul(ps_b[:], w[:, SG if a else SK, :], xs[k][:], start=True, stop=True
                                  ).then_inc(s_g if a else s_raw, 1)
                        need(pe, s_vc, 1 if isinstance(b, int) and f == 0 else f)
                        need(pe, s_msc, f * 2 + a)
                        need(pe, s_sq, f * 2 + a + 1)
                        for t in range(TT):
                            last = pe.matmul(ps_a[:, t * HH:(t + 1) * HH], sq[:, a, P * t:P * (t + 1)],
                                             mean8[:], start=True, stop=True)
                        last.then_inc(s_ms, 1)
                    elif step in (6, 7):
                        a = step - 6
                        need(pe, s_wide, f * 2 + a + 1)
                        need(pe, s_msc, f * 2 + 2)
                        if a:
                            need(pe, s_fin, f * 2 + 1)
                        for t in range(TT):
                            last = pe.transpose(ps_a[:, P * t:P * (t + 1)], roots[:, a, t, :],
                                                C.ident[:])
                        last.then_inc(s_bc, 1)

                def values(b, k):
                    f = b * 2 + k
                    if isinstance(b, int) and f in (0, 2 * B - 1):
                        need(pe, s_xs if f == 0 else s_fin, 1 if f == 0 else f * 2 + 2)
                    else:
                        need(pe, s_xs, f + 2)
                    for t in range(TT):
                        last = pe.matmul(ps_a[:, P * t:P * (t + 1)], xs[k][:, P * t:P * (t + 1)],
                                         w[:, SV, :], start=True, stop=True)
                    last.then_inc(s_v, 1)

                def product(b, h, out, i, keys):
                    k, j = h // HH, h % HH
                    if i == 0 and j == 0:
                        need(pe, s_rds[k], b * 128 + 128)
                        if isinstance(b, int) and b == 0:
                            need(pe, s_zero, 2 * KT)
                    return pe.matmul(out, QS[k][:, j, P * i:P * (i + 1)], KS[k][:, j, 0:keys],
                                     start=True, stop=True)

                def attend(b, u, tiles):
                    if tiles[0] == 0:
                        sm.need_probT(pe, b * H + QUAD * (u + 1) - 1)
                        need(pe, s_part, b * TT + u)
                        need(pe, s_vc, b * 2 + u // 2 + 1)
                    k = u // 2
                    for t in tiles:
                        for j in range(QUAD):
                            h = QUAD * u + j
                            n = TCOL[t]
                            last = pe.matmul(ps_y[HV * j:HV * (j + 1), P * t:L], V[k][:, t, h % HH, :],
                                             sm.probT[:, h % (2 * QUAD), n:n + L - P * t],
                                             start=t == 0, stop=t == TT - 1)
                    if t == TT - 1:
                        last.then_inc(s_y, 1)

                def turn_back(b, u):
                    need(pe, s_yc, b * (H // QUAD) + u + 1)
                    for t in range(TT):
                        last = pe.transpose(ps_y[:, P * t:P * (t + 1)], yq[:, P * t:P * (t + 1)],
                                            C.ident[:])
                    last.then_inc(s_yt, 1)

                def slot(b, h, f, v):
                    def between():
                        if v:
                            values(*v)
                        if f:
                            front(*f)
                        u = (h - 6) // QUAD
                        if u >= 0 and h < H + 6:
                            if h % QUAD == 2:
                                attend(b, u, (0,))
                            elif h % QUAD == 3:
                                attend(b, u, (1,))
                            elif h % QUAD == 0:
                                attend(b, u, (2, 3))

                    if h < 0 or h > H + 1:
                        between()
                    else:
                        sm.tensor_slot(pe, b, h, lambda *to: product(b, h, *to), between)
                    if h >= 9 and h % QUAD == 1:
                        turn_back(b, (h - 9) // QUAD)

                start_at_one(pe, s_y)
                walk(slot, pe)

            @blk.scalar
            def _(act):
                def front(b, k, step):
                    f = b * 2 + k
                    if step == 0:
                        need(act, s_turn, f + 1)
                        need(act, s_g, f - 1)
                        need(act, s_v, f - 1)
                        act.activation(xs[k][:], ps_a[:], ACT.Copy).then_inc(s_xs, 1)
                    elif step in (1, 2):
                        a = step - 1
                        need(act, s_rawc, f * 2 + a + 1)
                        need(act, s_lo, f * 2)
                        act.activation(sq[:, a, :], raw[:, a, :], ACT.Square).then_inc(s_sq, 1)
                    elif step in (6, 7):
                        a = step - 6
                        need(act, s_fin, f * 2 + 1 if a == 0 else f * 2 + 2)
                        if a:
                            need(act, s_kn, f * 2 + 2)
                        if not (isinstance(b, int) and b == 0 and k == 0):
                            need(act, s_wrs[1 - k], b * 64 if k == 0 else b * 64 + 64)
                        act.activation(words[2 * a][:], fin[:, a, :], ACT.Copy).then_inc(s_hi, 1)

                def values(b, k):
                    need(act, s_v, b * 2 + k + 1)
                    need(act, s_y, b * (H // QUAD) - 4 + 2 * k + 2)
                    if isinstance(b, int):
                        need(act, s_vzero, KT)
                    act.activation(V[k][:, :, :, 0:HD],
                                   ps_a[:].rearrange("p (t h d) -> p t h d", t=TT, h=HH),
                                   ACT.Copy).then_inc(s_vc, 1)

                def slot(b, h, f, v):
                    if 0 <= h <= H + 2:
                        sm.scalar_slot(act, b, h)
                    if v:
                        values(*v)
                    if f:
                        front(*f)
                    if h >= 8 and h % QUAD == 0:
                        need(act, s_y, b * (H // QUAD) + (h - 8) // QUAD + 1)
                        act.activation(yq[:], ps_y[:], ACT.Copy).then_inc(s_yc, 1)

                start_at_one(act, sm.s_pt_act)
                walk(slot, act)

            @blk.vector
            def _(dve):
                def front(b, k, step):
                    f = b * 2 + k
                    if step in (1, 2):
                        need(dve, s_raw, f * 2 + step)
                        dve.tensor_copy(raw[:, step - 1, :], ps_b[:]).then_inc(s_rawc, 1)
                    if step in (2, 3):
                        a = step - 2
                        need(dve, s_ms, f * 2 + a + 1)
                        dve.tensor_scalar(ms[:, a, :, :].rearrange("p t h -> p (t h)"),
                                          ps_a[:, 0:TT * HH], RMS_EPS, None, ALU.add
                                          ).then_inc(s_msc, 1)
                    elif step in (6, 7):
                        a = step - 6
                        need(dve, s_bc, f * 2 + a + 1)
                        dve.scalar_tensor_tensor(fin[:, a, :], raw[:, a, :], qk_norm[:, a:a + 1],
                                                 ps_a[:], ALU.mult, ALU.mult).then_inc(s_fin, 1)
                        if a:
                            need(dve, s_fin, f * 2 + 2)
                            need(dve, s_g, f + 1)
                            dve.tensor_tensor(fin[:, 1, :], fin[:, 1, :], ps_b[:], ALU.add
                                              ).then_inc(s_kn, 2)

                def reciprocals(b, u):
                    j = slice(QUAD * (u % 2), QUAD * (u % 2) + QUAD)
                    need(dve, sm.s_exp, (b * H + QUAD * (u + 1)) * TT)
                    dve.reciprocal(sm.recip[:, j, :], sm.rowsum[:, j, :]).then_inc(sm.s_recip, 1)

                def outputs(b, u):
                    j = QUAD * (u % 2)
                    recip = sm.recip[:, j:j + QUAD, :]
                    n = b * (H // QUAD) + u + 1
                    need(dve, sm.s_recip, n)
                    need(dve, s_yt, n)
                    dve.tensor_tensor(
                        part[:], ps_y[:].rearrange("p (t j d) -> p t j d", t=TT, j=QUAD)[:, :, :, 0:HD],
                        recip.rearrange("p j t -> p t j").unsqueeze(3).to_broadcast([P, TT, QUAD, HD]),
                        ALU.mult).then_inc(s_part, 1)
                    need(dve, s_part, n)
                    if u == 0:
                        need(dve, ln.s_x, b * TT)
                    cols = slice(QUAD * HD * u, QUAD * HD * (u + 1))
                    dve.tensor_tensor(
                        ln.res[:, :, cols].rearrange("p t (j d) -> p t j d", d=HD),
                        X[:, bass.ds(b * TT, TT), cols].rearrange("p t (j d) -> p t j d", d=HD),
                        part[:], ALU.add).then_inc(ln.s_sum, 1)

                cleared = [buf[4 * HD:P, :, :].bitcast(F32) for buf in QS + KS]

                def slot(b, h, f, v):
                    if h < 0 and f[1] == 0 and f[2] in (0, 3, 4, 5):
                        dve.memset(cleared.pop(), 0.0).then_inc(s_zero, 1)
                    if h >= 7 and h % QUAD == 3:
                        reciprocals(b, (h - 7) // QUAD)
                    if 0 <= h <= H + 1:
                        sm.vector_slot(dve, b, h)
                    if f:
                        front(*f)
                    if h >= 9 and h % QUAD == 1:
                        outputs(b, (h - 9) // QUAD)
                    if h == H + 5:
                        need(dve, ln.s_sum, b * TT + TT)
                        for t in range(TT):
                            ln.statistics(dve, b, t)
                    if h == H + 6:
                        ln.write(dve, b)

                start_at_one(dve, ln.s_sum, ln.s_x, sm.s_pt_dve)
                walk(slot, dve)


def layer1_ffn(nc, X, C, A):
    STEPS, BETA, THRESHOLD = 5, 0.9, 1.0
    with ExitStack() as ctx:
        S = Held(nc, ctx, "f1")
        F = Features(S, C, X)
        wfc = S.sb("wfc", [P, KT, FF])
        wpj = S.sb("wpj", [P, NF, D])
        hid = [S.sb(f"hid{j}", [P, NF, GL]) for j in range(2)]
        pos = [S.sb(f"pos{j}", [P, GL]) for j in range(2)]
        cur = S.sb("cur", [P, GL])
        acc = S.sb("acc", [P, GL])
        mem, nxt = S.sb("mem", [P, GL]), S.sb("nxt", [P, GL])
        ln = LayerNorm(S, C, X, GT)
        ps_h = [S.ps(f"ps_h{j}") for j in range(2)]
        ps_y = [S.ps(f"ps_y{c}") for c in range(2)]
        s_wfc0, s_wfc, s_wpj, s_h, s_pos, s_hid, s_y, s_cur = (
            S.sem(n) for n in ("wfc0", "wfc", "wpj", "h", "pos", "hid", "y", "cur"))
        s_v, s_store = S.sem("v"), S.sem("store")
        V_STEPS = 3 * (STEPS - 1) + 1
        with nc.Block() as blk:
            @blk.sync
            def _(sp):
                wfcT = A["wfcT"].rearrange("(k p) f -> p k f", p=P)
                for cols, sem in ((slice(0, 2 * P), s_wfc0), (slice(2 * P, FF), s_wfc)):
                    sp.dma_start(wfc[:, :, cols], wfcT[:, :, cols]).then_inc(sem, 16)
                sp.dma_start(wpj[:], A["wpjT"].rearrange("(k p) d -> p k d", p=P)).then_inc(s_wpj, 16)
                out = A["out"].rearrange("b (t p) d -> p (b t) d", p=P)
                with sp.Fori(0, NG) as g:
                    hold(sp, ln.s_x, g * GT + GT, F.passed)
                    sp.dma_start(out[:, bass.ds(g * GT, GT), :], X[:, bass.ds(g * GT, GT), :]
                                 ).then_inc(s_store, 16)
                need(sp, s_store, 16 * NG)

            @blk.gpsimd
            def _(pool):
                F.fetch(pool, 0, 0)
                F.fetch(pool, 1, 1)
                with pool.Fori(1, NG // 2) as r:
                    for j in range(2):
                        F.fetch(pool, r * 2 + j, j)
                        ln.root(pool, r * 2 + j - 2)
                for g in range(NG - 2, NG):
                    ln.root(pool, g)

            @blk.tensor
            def _(pe):
                def up(g, j):
                    F.turn(pe, g, j)
                    need(pe, F.s_xs, g * KT + KT)
                    for f in range(NF):
                        if f in (0, 2):
                            need(pe, s_wfc if f else s_wfc0, 16)
                        need(pe, s_pos, g * NF + f - 1)
                        for k in range(KT):
                            last = pe.matmul(ps_h[f % 2][:], wfc[:, k, P * f:P * (f + 1)], F.xs[j][:, k, :],
                                             start=k == 0, stop=k == KT - 1)
                        last.then_inc(s_h, 1)

                def down(g, j):
                    need(pe, s_wpj, 16)
                    need(pe, s_hid, g * NF + NF)
                    for t in range(GT):
                        if t % 2 == 0:
                            need(pe, s_cur, g * 2 + t // 2 - 1)
                        for f in range(NF):
                            last = pe.matmul(ps_y[t // 2][:, D * (t % 2):D * (t % 2 + 1)],
                                             hid[j][:, f, P * t:P * (t + 1)], wpj[:, f, :],
                                             start=f == 0, stop=f == NF - 1)
                        if t % 2:
                            last.then_inc(s_y, 1)

                up(0, 0)
                up(1, 1)
                down(0, 0)
                with pe.Fori(1, NG // 2) as r:
                    for j in range(2):
                        up(r * 2 + j, j)
                        down(r * 2 + j - 1, 1 - j)
                down(NG - 1, 1)

            @blk.scalar
            def _(act):
                def step(g, j):
                    if not isinstance(g, int) or g >= 2:
                        need(act, s_y, g * 2 - 2)
                    F.keep(act, g, j)
                    for f in range(NF):
                        need(act, s_h, g * NF + f + 1)
                        need(act, s_hid, g * NF + f - 1)
                        act.activation(pos[f % 2][:], ps_h[f % 2][:], ACT.Relu).then_inc(s_pos, 1)
                        need(act, s_pos, g * NF + f + 1)
                        act.activation(hid[j][:, f, :], pos[f % 2][:], ACT.Square).then_inc(s_hid, 1)

                step(0, 0)
                step(1, 1)
                with act.Fori(1, NG // 2) as r:
                    for j in range(2):
                        step(r * 2 + j, j)

            @blk.vector
            def _(dve):
                start_at_one(dve, ln.s_sum, ln.s_x)
                with dve.Fori(0, NG) as g:
                    for c in range(2):
                        n = g * 2 + c
                        need(dve, s_y, n + 1)
                        dve.tensor_copy(cur[:], ps_y[c][:]).then_inc(s_cur, 1)
                        need(dve, s_cur, n + 1)
                        base = n * V_STEPS
                        m = cur
                        dve.tensor_scalar(acc[:], cur[:], THRESHOLD, None, ALU.is_gt).then_inc(s_v, 1)
                        for i in range(STEPS - 1):
                            at = base + 3 * i + 1
                            dve.scalar_tensor_tensor(nxt[:], m[:], BETA, cur[:], ALU.mult, ALU.add
                                                     ).then_inc(s_v, 1)
                            need(dve, s_v, at + 1)
                            dve.scalar_tensor_tensor(mem[:], m[:], THRESHOLD, nxt[:], ALU.is_gt,
                                                     ALU.subtract, reverse1=True).then_inc(s_v, 1)
                            need(dve, s_v, at + 2)
                            dve.scalar_tensor_tensor(acc[:], mem[:], THRESHOLD, acc[:], ALU.is_gt,
                                                     ALU.add).then_inc(s_v, 1)
                            need(dve, s_v, at + 3)
                            m = mem
                        tiles = bass.ds(g * GT + 2 * c, 2)
                        if c == 0:
                            need(dve, ln.s_x, g * GT)
                        dve.scalar_tensor_tensor(ln.res[:, 2 * c:2 * c + 2, :].rearrange("p t d -> p (t d)"),
                                                 acc[:], 1.0 / STEPS,
                                                 X[:, tiles, :].rearrange("p t d -> p (t d)"), ALU.mult,
                                                 ALU.add).then_inc(ln.s_sum, 1)
                        need(dve, ln.s_sum, n + 1)
                        for t in range(2):
                            ln.statistics(dve, g, 2 * c + t)
                    ln.write(dve, g)


def build(nc, A):
    with ExitStack() as ctx:
        C = Held(nc, ctx, "c")
        X = C.sb("X", [P, NT, D])
        C.ident, C.mask = C.sb("ident", [P, P]), C.sb("mask", [P, L])
        C.minus_half = C.sb("minus_half", [P, 2 * TT * HH])
        s_const = C.sem("const")
        with nc.Block() as blk:
            @blk.sync
            def _(sp):
                sp.dma_start(C.ident[:], A["ident"]).then_inc(s_const, 16)
                sp.dma_start(C.mask[:], A["mask"]).then_inc(s_const, 16)
                sp.wait_ge(s_const, 32)

            @blk.gpsimd
            def _(pool):
                pool.memset(C.minus_half[:], -0.5)
        folded = fold_layer1(nc, C, A)
        with ExitStack() as ectx:
            ES = ExpertStore(nc, ectx)
            layer0_attention(nc, X, C, A, lambda pool, b: ES.part(pool, A, b))
            layer0_experts(nc, X, ES, C)
        layer1_attention(nc, X, folded, C, A)
        layer1_ffn(nc, X, C, A)


def shape_constants():
    f32 = np.float32
    after = np.arange(P)[None, :] > np.arange(P)[:, None]
    mask = np.zeros((P, L), f32)
    mask[:, L - P:] = np.where(after, f32(MASKED), f32(0))
    heads = np.kron(np.eye(HH), np.ones((HD, HD))).astype(f32)
    rows = lambda a: np.ascontiguousarray(np.broadcast_to(np.asarray(a, f32), (P,) + np.shape(a)))
    return {
        "ident": np.eye(P, dtype=f32), "mask": mask, "before": after.astype(f32),
        "iota": rows(np.arange(E)), "tiota": rows(np.arange(NS)), "thr": rows(P * np.arange(NT)),
        "lower": rows(np.tril(np.ones((E, E)), -1)), "block": heads,
        "mean8": np.ascontiguousarray(heads[:, ::HD] / f32(HD)),
    }


def laid_out(i):
    a0, f0, a1, f1 = "L0_attn_", "L0_ffn_", "L1_attn_", "L1_ffn_"
    eight = lambda a: np.tile(a, (1, HH))
    out = {
        "x": i[a0 + "x_bld"], "xT": i[a0 + "x_bld"].transpose(0, 2, 1),
        "wqT": i[a0 + "Wq"].transpose(2, 1, 0), "wkT": i[a0 + "Wk_up"].transpose(2, 1, 0),
        "wvT": i[a0 + "Wv_up"].transpose(2, 1, 0), "wo": i[a0 + "Wout"].transpose(1, 0, 2),
        "wdn": i[a0 + "Wkv_down"],
        "gate_w": i[f0 + "gate_w"], "gate_b": np.broadcast_to(i[f0 + "gate_b"], (P, E)),
        "swg": i[f0 + "shared_wg"], "swu": i[f0 + "shared_wu"], "swd": i[f0 + "shared_wd"],
        "ewg": i[f0 + "experts_wg"], "ewu": i[f0 + "experts_wu"], "ewd": i[f0 + "experts_wd"],
        "wdq": eight(i[a1 + "W_DQ"]), "wuqT": eight(i[a1 + "W_UQ"].T),
        "wdkv": eight(i[a1 + "W_DKV"]), "wukT": eight(i[a1 + "W_UKV"][:HD].T),
        "wuvT": i[a1 + "W_UKV"][HD:].T, "wkr": eight(i[a1 + "W_KR"]), "wqr": eight(i[a1 + "W_QR"]),
        "woT": eight(i[a1 + "W_O"].T),
        "qk_norm": np.stack([np.tile(i[a1 + "q_norm_w"], HH), np.tile(i[a1 + "k_norm_w"], HH)], 1),
        "wfcT": i[f1 + "W_fc"].T, "wpjT": i[f1 + "W_proj"].T,
    }
    return {k: np.ascontiguousarray(v) for k, v in out.items()}


def kernel(**inputs):
    from concourse import bacc
    from concourse.bass_utils import run_bass_kernel_spmd

    arrays = {**laid_out({k: np.asarray(v) for k, v in inputs.items()}), **shape_constants()}
    nc = bacc.Bacc("TRN2", target_bir_lowering=False, num_devices=1)
    A = {k: nc.dram_tensor(f"in_{k}", v.shape, mybir.dt.from_np(v.dtype), kind="ExternalInput").ap()
         for k, v in arrays.items()}
    A["out"] = nc.dram_tensor("out", (B, L, D), F32, kind="ExternalOutput").ap()
    build(nc, A)
    r = run_bass_kernel_spmd(nc, [{f"in_{k}": v for k, v in arrays.items()}], core_ids=[0])
    return r.results[0]["out"]
```
